# Optimizing a Trainium2 kernel written in Bass

```python
import numpy as np
import jax
import jax.numpy as jnp

def _softmax(x, axis=-1):
    return jax.nn.softmax(x, axis=axis)

def _gelu(x):
    return jax.nn.gelu(x, approximate=True)

def _silu(x):
    return jax.nn.silu(x)

def _sigmoid(x):
    return jax.nn.sigmoid(x)

def _layernorm(x, axis=-1, eps=1e-05):
    m = jnp.mean(x, axis=axis, keepdims=True)
    v = jnp.var(x, axis=axis, keepdims=True)
    return (x - m) / jnp.sqrt(v + eps)

def _scatter_add(tgt, idx, src, axis=0):
    return tgt.at[idx].add(src)

def _segment_sum(src, seg, n):
    return jax.ops.segment_sum(src, seg, n)
kernel_name = 'mk_seq_postln_d2_jaxref_r8_0e98e3'

def setup_inputs(seed: int=0):
    np.random.seed(seed)
    _w = jnp.asarray

    def _L0_attn_setup():
        import jax, jax.numpy as jnp
        import numpy as np
        B, N, E, H = (1, 512, 256, 16)
        D = E // H
        DEGREE = 4
        LN_EPS = 1e-05
        ROPE_BASE = 10000.0

        def rope_cos_sin(n, d):
            inv_freq = 1.0 / ROPE_BASE ** (jnp.arange(0, d, 2, dtype=jnp.float32) / d)
            t = jnp.arange(n, dtype=jnp.float32)[:, None] * inv_freq[None, :]
            return (jnp.cos(t), jnp.sin(t))

        def apply_rope(x, cos, sin):
            x1, x2 = jnp.split(x, 2, axis=-1)
            c = cos[None, :, None, :]
            s = sin[None, :, None, :]
            return jnp.concatenate([x1 * c - x2 * s, x1 * s + x2 * c], axis=-1)

        def layernorm(x, scale, bias, eps=LN_EPS):
            m = jnp.mean(x, axis=-1, keepdims=True)
            v = jnp.var(x, axis=-1, keepdims=True)
            return (x - m) * jax.lax.rsqrt(v + eps) * scale + bias

        def polynomial_attention(q, k, v, degree, is_causal):
            a = jnp.einsum('bhnd,bhmd->bhnm', q, k) ** degree
            if is_causal:
                a = jnp.tril(a)
            denom = jnp.sum(a, axis=-1, keepdims=True)
            return jnp.einsum('bhnm,bhmd->bhnd', a / denom, v)
        key = jax.random.key(seed)
        k0, k1, k2 = jax.random.split(key, 3)
        x = jax.random.normal(k0, (B, N, E), dtype=jnp.float32)
        w_qkv = jax.random.normal(k1, (E, 3 * E), dtype=jnp.float32) * (1.0 / np.sqrt(E))
        w_out = jax.random.normal(k2, (E, E), dtype=jnp.float32) * (1.0 / np.sqrt(E))
        ln_scale = jnp.ones((D,), dtype=jnp.float32)
        ln_bias = jnp.zeros((D,), dtype=jnp.float32)
        return {'x': x, 'w_qkv': w_qkv, 'w_out': w_out, 'ln_scale': ln_scale, 'ln_bias': ln_bias}
    _L0_attn_in = _L0_attn_setup()

    def _L0_ffn_setup():
        import jax, jax.numpy as jnp
        import numpy as np
        DIM_IN = 256
        DIM_HIDDEN = 1024
        key = jax.random.key(seed)
        k_x, k_g, k_u, k_d = jax.random.split(key, 4)
        s_in = 1.0 / np.sqrt(DIM_IN)
        s_hid = 1.0 / np.sqrt(DIM_HIDDEN)
        x = jax.random.normal(k_x, (4, 256, DIM_IN), dtype=jnp.float32)
        w_gate = jax.random.uniform(k_g, (DIM_HIDDEN, DIM_IN), jnp.float32, -s_in, s_in)
        w_up = jax.random.uniform(k_u, (DIM_HIDDEN, DIM_IN), jnp.float32, -s_in, s_in)
        w_down = jax.random.uniform(k_d, (DIM_IN, DIM_HIDDEN), jnp.float32, -s_hid, s_hid)
        return {'x': x, 'w_gate': w_gate, 'w_up': w_up, 'w_down': w_down}
    _L0_ffn_in = _L0_ffn_setup()

    def _L1_attn_setup():
        import jax, jax.numpy as jnp
        import numpy as np
        HIDDEN = 256
        HEADS = 32
        HEAD_DIM = HIDDEN // HEADS
        MAX_POS = 64
        TABLE = 2 * MAX_POS - 1

        def _rel_bias(rel_pos, seq_len):
            pos = jnp.arange(seq_len)
            rel = pos[None, :] - pos[:, None] + (MAX_POS - 1)
            rel = jnp.clip(rel, 0, TABLE - 1)
            return rel_pos[rel].mean(axis=-1)
        key = jax.random.key(seed)
        k = jax.random.split(key, 6)
        B, S = (16, 64)
        return {'hidden_states': jax.random.normal(k[0], (B, S, HIDDEN), dtype=jnp.float32), 'wq': jax.random.normal(k[1], (HIDDEN, HIDDEN), dtype=jnp.float32) * 0.02, 'wk': jax.random.normal(k[2], (HIDDEN, HIDDEN), dtype=jnp.float32) * 0.02, 'wv': jax.random.normal(k[3], (HIDDEN, HIDDEN), dtype=jnp.float32) * 0.02, 'wo': jax.random.normal(k[4], (HIDDEN, HIDDEN), dtype=jnp.float32) * 0.02, 'rel_pos': jax.random.normal(k[5], (TABLE, HEAD_DIM), dtype=jnp.float32)}
    _L1_attn_in = _L1_attn_setup()

    def _L1_ffn_setup():
        import jax, jax.numpy as jnp
        import numpy as np
        E = 8
        TOP_K = 2
        H = 256
        I = 176
        SI = 704
        key = jax.random.key(seed)
        ks = jax.random.split(key, 9)
        s = lambda fan_in: 1.0 / np.sqrt(fan_in)
        return {'hidden_states': jax.random.normal(ks[0], (4, 256, H), dtype=jnp.float32), 'router_w': jax.random.normal(ks[1], (E, H), dtype=jnp.float32) * s(H), 'w_gate': jax.random.normal(ks[2], (E, H, I), dtype=jnp.float32) * s(H), 'w_up': jax.random.normal(ks[3], (E, H, I), dtype=jnp.float32) * s(H), 'w_down': jax.random.normal(ks[4], (E, I, H), dtype=jnp.float32) * s(I), 'sw_gate': jax.random.normal(ks[5], (H, SI), dtype=jnp.float32) * s(H), 'sw_up': jax.random.normal(ks[6], (H, SI), dtype=jnp.float32) * s(H), 'sw_down': jax.random.normal(ks[7], (SI, H), dtype=jnp.float32) * s(SI), 'shared_gate_w': jax.random.normal(ks[8], (H,), dtype=jnp.float32) * s(H)}
    _L1_ffn_in = _L1_ffn_setup()
    _d = {'L0_attn_x': _L0_attn_in['x'], 'L0_attn_w_qkv': _L0_attn_in['w_qkv'], 'L0_attn_w_out': _L0_attn_in['w_out'], 'L0_attn_ln_scale': _L0_attn_in['ln_scale'], 'L0_attn_ln_bias': _L0_attn_in['ln_bias'], 'L0_ffn_w_gate': _L0_ffn_in['w_gate'], 'L0_ffn_w_up': _L0_ffn_in['w_up'], 'L0_ffn_w_down': _L0_ffn_in['w_down'], 'L1_attn_wq': _L1_attn_in['wq'], 'L1_attn_wk': _L1_attn_in['wk'], 'L1_attn_wv': _L1_attn_in['wv'], 'L1_attn_wo': _L1_attn_in['wo'], 'L1_attn_rel_pos': _L1_attn_in['rel_pos'], 'L1_ffn_router_w': _L1_ffn_in['router_w'], 'L1_ffn_w_gate': _L1_ffn_in['w_gate'], 'L1_ffn_w_up': _L1_ffn_in['w_up'], 'L1_ffn_w_down': _L1_ffn_in['w_down'], 'L1_ffn_sw_gate': _L1_ffn_in['sw_gate'], 'L1_ffn_sw_up': _L1_ffn_in['sw_up'], 'L1_ffn_sw_down': _L1_ffn_in['sw_down'], 'L1_ffn_shared_gate_w': _L1_ffn_in['shared_gate_w']}
    _x0 = _d['L0_attn_x']
    _d['L0_attn_x'] = jax.random.normal(jax.random.fold_in(jax.random.key(seed), 1), (8, 256, 256), dtype=_x0.dtype)
    del _x0
    return _d

def reference(L0_attn_x, L0_attn_w_qkv, L0_attn_w_out, L0_attn_ln_scale, L0_attn_ln_bias, L0_ffn_w_gate, L0_ffn_w_up, L0_ffn_w_down, L1_attn_wq, L1_attn_wk, L1_attn_wv, L1_attn_wo, L1_attn_rel_pos, L1_ffn_router_w, L1_ffn_w_gate, L1_ffn_w_up, L1_ffn_w_down, L1_ffn_sw_gate, L1_ffn_sw_up, L1_ffn_sw_down, L1_ffn_shared_gate_w):

    def _L0_attn_ref(x, w_qkv, w_out, ln_scale, ln_bias):
        import jax, jax.numpy as jnp
        import numpy as np
        B, N, E, H = (1, 512, 256, 16)
        D = E // H
        DEGREE = 4
        LN_EPS = 1e-05
        ROPE_BASE = 10000.0

        def rope_cos_sin(n, d):
            inv_freq = 1.0 / ROPE_BASE ** (jnp.arange(0, d, 2, dtype=jnp.float32) / d)
            t = jnp.arange(n, dtype=jnp.float32)[:, None] * inv_freq[None, :]
            return (jnp.cos(t), jnp.sin(t))

        def apply_rope(x, cos, sin):
            x1, x2 = jnp.split(x, 2, axis=-1)
            c = cos[None, :, None, :]
            s = sin[None, :, None, :]
            return jnp.concatenate([x1 * c - x2 * s, x1 * s + x2 * c], axis=-1)

        def layernorm(x, scale, bias, eps=LN_EPS):
            m = jnp.mean(x, axis=-1, keepdims=True)
            v = jnp.var(x, axis=-1, keepdims=True)
            return (x - m) * jax.lax.rsqrt(v + eps) * scale + bias

        def polynomial_attention(q, k, v, degree, is_causal):
            a = jnp.einsum('bhnd,bhmd->bhnm', q, k) ** degree
            if is_causal:
                a = jnp.tril(a)
            denom = jnp.sum(a, axis=-1, keepdims=True)
            return jnp.einsum('bhnm,bhmd->bhnd', a / denom, v)
        b, n, e = x.shape
        proj = x @ w_qkv
        q, k, v = jnp.split(proj, 3, axis=-1)
        q = q.reshape(b, n, H, D)
        k = k.reshape(b, n, H, D)
        v = v.reshape(b, n, H, D)
        cos, sin = rope_cos_sin(n, D)
        q = apply_rope(q, cos, sin)
        k = apply_rope(k, cos, sin)
        q = q.transpose(0, 2, 1, 3)
        k = k.transpose(0, 2, 1, 3)
        v = v.transpose(0, 2, 1, 3)
        q = layernorm(q, ln_scale, ln_bias)
        k = layernorm(k, ln_scale, ln_bias)
        out = polynomial_attention(q, k, v, DEGREE, True)
        out = out.transpose(0, 2, 1, 3).reshape(b, n, e)
        out = out @ w_out
        return out

    def _L0_ffn_ref(x, w_gate, w_up, w_down):
        import jax, jax.numpy as jnp
        import numpy as np
        DIM_IN = 256
        DIM_HIDDEN = 1024
        gate = jnp.einsum('bsd,hd->bsh', x, w_gate)
        up = jnp.einsum('bsd,hd->bsh', x, w_up)
        gated = jax.nn.silu(gate) * up
        return jnp.einsum('bsh,dh->bsd', gated, w_down)

    def _L1_attn_ref(hidden_states, wq, wk, wv, wo, rel_pos):
        import jax, jax.numpy as jnp
        import numpy as np
        HIDDEN = 256
        HEADS = 32
        HEAD_DIM = HIDDEN // HEADS
        MAX_POS = 64
        TABLE = 2 * MAX_POS - 1

        def _rel_bias(rel_pos, seq_len):
            pos = jnp.arange(seq_len)
            rel = pos[None, :] - pos[:, None] + (MAX_POS - 1)
            rel = jnp.clip(rel, 0, TABLE - 1)
            return rel_pos[rel].mean(axis=-1)
        B, S, _ = hidden_states.shape
        scale = jnp.sqrt(jnp.float32(HEAD_DIM))
        q = (hidden_states @ wq.T).reshape(B, S, HEADS, HEAD_DIM).transpose(0, 2, 1, 3)
        k = (hidden_states @ wk.T).reshape(B, S, HEADS, HEAD_DIM).transpose(0, 2, 1, 3)
        v = (hidden_states @ wv.T).reshape(B, S, HEADS, HEAD_DIM).transpose(0, 2, 1, 3)
        scores = jnp.einsum('bhqd,bhkd->bhqk', q, k) / scale
        scores = scores + _rel_bias(rel_pos, S)[None, None]
        attn = jax.nn.softmax(scores, axis=-1)
        ctx = jnp.einsum('bhqk,bhkd->bhqd', attn, v)
        ctx = ctx.transpose(0, 2, 1, 3).reshape(B, S, HIDDEN)
        return ctx @ wo.T

    def _L1_ffn_ref(hidden_states, router_w, w_gate, w_up, w_down, sw_gate, sw_up, sw_down, shared_gate_w):
        import jax, jax.numpy as jnp
        import numpy as np
        E = 8
        TOP_K = 2
        H = 256
        I = 176
        SI = 704
        B, S, Hd = hidden_states.shape
        x = hidden_states.reshape(-1, Hd)
        shared = jnp.einsum('ts,sh->th', jax.nn.silu(x @ sw_gate) * (x @ sw_up), sw_down)
        logits = x @ router_w.T
        probs = jax.nn.softmax(logits.astype(jnp.float32), axis=-1)
        top_w, top_i = jax.lax.top_k(probs, TOP_K)
        top_w = top_w / jnp.sum(top_w, axis=-1, keepdims=True)
        combine = jnp.sum(jax.nn.one_hot(top_i, E, dtype=x.dtype) * top_w[..., None].astype(x.dtype), axis=1)
        h = jax.nn.silu(jnp.einsum('th,ehi->eti', x, w_gate)) * jnp.einsum('th,ehi->eti', x, w_up)
        expert_out = jnp.einsum('eti,eih->eth', h, w_down)
        routed = jnp.einsum('eth,te->th', expert_out, combine)
        shared_out = jax.nn.sigmoid(x @ shared_gate_w)[:, None] * shared
        return (routed + shared_out).reshape(B, S, Hd)
    x = L0_attn_x
    x = _layernorm(x + _L0_attn_ref(x, L0_attn_w_qkv, L0_attn_w_out, L0_attn_ln_scale, L0_attn_ln_bias), axis=-1)
    x = _layernorm(x + _L0_ffn_ref(x, L0_ffn_w_gate, L0_ffn_w_up, L0_ffn_w_down), axis=-1)
    x = _layernorm(x + _L1_attn_ref(x, L1_attn_wq, L1_attn_wk, L1_attn_wv, L1_attn_wo, L1_attn_rel_pos), axis=-1)
    x = _layernorm(x + _L1_ffn_ref(x, L1_ffn_router_w, L1_ffn_w_gate, L1_ffn_w_up, L1_ffn_w_down, L1_ffn_sw_gate, L1_ffn_sw_up, L1_ffn_sw_down, L1_ffn_shared_gate_w), axis=-1)
    return x

_drawn_inputs = setup_inputs


def setup_inputs(seed=0):
    import zlib

    import numpy as np

    out = dict(_drawn_inputs(seed))
    spreads = {'L0_attn_ln_scale': (1.0, 0.2), 'L0_attn_ln_bias': (0.0, 0.1)}
    factors = {'L1_attn_wq': 8.0, 'L1_attn_wk': 8.0, 'L1_attn_rel_pos': 8.0}
    for name, (base, spread) in spreads.items():
        noise = np.random.default_rng([zlib.crc32(name.encode()), seed]).standard_normal(out[name].shape)
        drawn = base * np.exp(spread * noise) if base else spread * noise
        out[name] = jnp.asarray(drawn.astype(out[name].dtype))
    for name, factor in factors.items():
        out[name] = (out[name] * factor).astype(out[name].dtype)
    return out
```

```python
from contextlib import ExitStack

import concourse.bass as bass
from concourse import mybir

ALU = mybir.AluOpType
ACT = mybir.ActivationFunctionType
F32 = mybir.dt.float32
F32R = mybir.dt.float32r
AX_X = mybir.AxisListType.X

P = 128
T = 2048
E = 256
S = 256
KT = E // P
EPS = 1e-5
ROWS = 2 * S
NBANK = 8
FMIN = -3.0e38

H0, D0 = 16, 16
H2, D2 = 32, 8
MAXPOS = 64
TABLE = 2 * MAXPOS - 1
F1 = 1024
NEXP, IE, SI = 8, 176, 704
TILES1 = F1 // P
TILES3 = -(-(NEXP * IE + SI) // P)
UNIT = 2 * KT * P + E
GATES = NEXP + 1
QSCALE = -float(D2) ** -0.5


def program(nc, x, rope, ln, aw0, wu1, aw2, rel, wu3, router, sel, out):
    with ExitStack() as ctx:
        def sem(name):
            return ctx.enter_context(nc.semaphore(name))

        def sb(name, width, dt=F32):
            return ctx.enter_context(nc.sbuf_tensor(name, [P, width], dt))

        def cut(buf, at, shape, parts=P):
            n = 1
            for s in shape:
                n *= s
            v = buf[0:parts, at:at + n]
            if len(shape) == 2:
                return v.rearrange("p (a b) -> p a b", a=shape[0])
            if len(shape) == 3:
                return v.rearrange("p (a b c) -> p a b c", a=shape[0], b=shape[1])
            if len(shape) == 4:
                return v.rearrange("p (a b c d) -> p a b c d", a=shape[0], b=shape[1], c=shape[2])
            return v

        x1 = nc.dram_tensor("x1", [T, E], F32, kind="Internal").ap()
        x2 = nc.dram_tensor("x2", [T, E], F32, kind="Internal").ap()
        x3 = nc.dram_tensor("x3", [T, E], F32, kind="Internal").ap()
        ediag = nc.dram_tensor("ediag", [1, ROWS], F32, kind="Internal").ap()

        WU = ctx.enter_context(nc.sbuf_tensor("WU", [P, TILES3, 2, UNIT], F32R))
        AW = ctx.enter_context(nc.sbuf_tensor("AW", [P, 2, KT, 1024], F32R))
        RT = sb("RT", 9216, F32R)
        G = sb("G", 11264)
        wraw = sb("wraw", UNIT)
        small = sb("small", 704)
        ident = sb("ident", P)
        nb = sb("nb", 2 * S)
        lnt = sb("lnt", 2 * D0)
        ropet = sb("ropet", 2 * 16)
        routh = sb("routh", KT * GATES, F32R)
        routl = sb("routl", KT * GATES, F32R)
        ps = ctx.enter_context(nc.psum_tensor("ps", [P, NBANK, 512], F32))

        xt_in_a = cut(G, 0, [2, E])
        xr_a = cut(G, 512, [2, E])
        xo_a = cut(G, 1024, [2, E])
        ctx_a = cut(G, 1536, [2, E])
        OT = G[:, 2048:4096]
        VP = G[:, 4096:4736]
        WORK = G[:, 4736:11264]
        QT = cut(RT, 0, [8, S])
        KTT = cut(RT, 2048, [8, S])
        QS = RT[:, 4096:6144]
        KS = RT[:, 6144:8192]
        XT_a = [cut(RT, 8192 + 512 * h, [KT, S]) for h in range(2)]
        spare = WU[:, TILES3 - 1].rearrange("p a n -> p (a n)")
        CT_a = [spare[:, 512 * h:512 * (h + 1)].rearrange("p (k t) -> p k t", k=KT) for h in range(2)]
        xt_in_f = cut(G, 0, [4, E])
        xr_f = cut(G, 1024, [4, E])
        xo_f = cut(G, 2048, [4, E])
        sg = cut(G, 3072, [2, 512])
        tt = cut(G, 4096, [3, 512])
        hf = cut(G, 5632, [3, 512])
        lgT = G[0:GATES, 7168:7680]
        sel_raw = G[0:2 * GATES, 7680:7680 + TILES3 * P]
        router_raw = G[:, 9856:9856 + KT * GATES]
        XT_f = [cut(RT, 1024 * h, [KT, 512]) for h in range(2)]
        HT = cut(RT, 2048, [3, 2, 512])

        stats = cut(small, 0, [4, 6])
        mv = cut(small, 32, [4, 2])
        rstd = cut(small, 48, [4])
        minus_half = small[:, 56:120]
        hsum = small[:, 120:184]
        hvar = small[:, 184:248]
        hrs = small[:, 248:312]
        mneg = small[:, 312:316]
        rden = small[:, 640:704]
        lg = cut(small, 352, [4, GATES])
        top = cut(small, 392, [4, 8])
        pick = cut(small, 424, [4, 8])
        ex = cut(small, 460, [4, GATES])
        cw = cut(small, 500, [4, GATES])
        cs2 = cut(small, 540, [4, 2 * GATES])
        den = cut(small, 616, [4])

        iterations = {0: 8, 1: 4, 2: 8, 3: 4}
        x_in = {0: x, 1: x1, 2: x2, 3: x3}
        x_out = {0: x1, 1: x2, 2: x3, 3: out}

        def U(p):
            return WORK[:, 768 * (p % 2):768 * (p % 2 + 1)].rearrange("p (h c) -> p h c", h=2)

        def P4(p):
            return WORK[:, 1536 + 768 * (p % 2):1536 + 768 * (p % 2 + 1)].rearrange("p (h c) -> p h c", h=2)

        def biased(h):
            return WORK[:, 512 * (h % 2):512 * (h % 2 + 1)].rearrange("p (t k) -> p t k", t=2)

        def prob(h):
            return WORK[:, 1024 + 512 * (h % 3):1024 + 512 * (h % 3 + 1)].rearrange("p (t k) -> p t k", t=2)

        def probT(h):
            return WORK[:, 2560 + 512 * (h % 6):2560 + 512 * (h % 6 + 1)].rearrange("p (t k) -> p t k", t=2)

        SELW = AW[0:2 * GATES].rearrange("p a b c -> p (a b c)")[:, 0:TILES3 * P]
        CWT = AW[0:2 * GATES].rearrange("p a b c -> p (a b c)")[:, TILES3 * P:TILES3 * P + 512]
        ROT, SQ, CEN = (WORK[:, 3072 + 1024 * n:4096 + 1024 * n] for n in range(3))
        ROT2 = SQ

        def v_and_one(f):
            return VP.rearrange("p (t c) -> p t c", t=2)

        B_XT, B_QK, B_V, B_CT, B_QT, B_KT = 6, (6, 7), 7, 7, 7, 6
        B_Y = 6
        C_BANKS = {0: (7, 6), 2: (7, 6, 7, 6)}

        per_phase = {}

        def sems(name, phases=range(4)):
            per_phase[name] = {f: sem(f"{name}{f}") for f in phases}
            return per_phase[name]

        xt_loaded = sems("xt_loaded")
        xr_loaded = sems("xr_loaded")
        xt_turned = sems("xt_turned")
        xt_hi = sems("xt_hi")
        xt_ready = sems("xt_ready")
        y_ready = sems("y_ready", (0, 2))
        z_done = sems("z_done", (1, 3))
        var_ready = sems("var_ready")
        eps_added = sems("eps_added")
        rstd_ready = sems("rstd_ready")
        xo_ready = sems("xo_ready")
        stored = sems("stored")
        out_step = sems("out_step")
        qk_ready = sems("qk_ready", (0, 2))
        v_ready = sems("v_ready", (0, 2))
        split_hi = sems("split_hi", (0, 2))
        split_ready = sems("split_ready", (0, 2))
        vp_ready = sems("vp_ready", (0, 2))
        heads_turned = sems("heads_turned", (0, 2))
        heads_q = sems("heads_q", (0, 2))
        heads_k = sems("heads_k", (0, 2))
        score_ready = sems("score_ready", (0, 2))
        o_copied = sems("o_copied", (0, 2))
        c_turned = sems("c_turned", (0, 2))
        ctx_done = sems("ctx_done", (0, 2))
        ct_turned = sems("ct_turned", (0, 2))
        ct_hi = sems("ct_hi", (0, 2))
        ct_ready = sems("ct_ready", (0, 2))
        gate_ready = sems("gate_ready", (1, 3))
        up_ready = sems("up_ready", (1, 3))
        silu_ready = sems("silu_ready", (1, 3))
        prod_ready = sems("prod_ready", (1, 3))
        hid_hi = sems("hid_hi", (1, 3))
        hid_ready = sems("hid_ready", (1, 3))
        down_done = sems("down_done", (1, 3))
        names = ("in_step route_step rope_added cen_squared head_eps head_rstd squared masked quartic mixed0 biased_ready prob_ready probT_turned "
                 "probT_act probT_dve mixed2 wcol_ready prod_u lgT_turned lgT_ready lg_turned lg_ready ex_ready cw_ready "
                 "cwT_turned cwT_ready ident_ready half_ready consts aw0_raw aw0_hi aw0_ready phase_done vp_ones "
                 "rel_loaded rel_mean rel_neg diag_row diag_ready diag_stored skewed flip_zero flip_ready bias_turned "
                 "bias_ready rsel_loaded rsel_hi rsel_ready raw_ready raw_free split_w_hi split_w passed").split()
        (in_step, route_step, rope_added, cen_squared, head_eps, head_rstd, squared, masked, quartic, mixed0, biased_ready, prob_ready, probT_turned,
         probT_act, probT_dve, mixed2, wcol_ready, prod_u, lgT_turned, lgT_ready, lg_turned, lg_ready, ex_ready, cw_ready,
         cwT_turned, cwT_ready, ident_ready, half_ready, consts, aw0_raw, aw0_hi, aw0_ready, phase_done, vp_ones,
         rel_loaded, rel_mean, rel_neg, diag_row, diag_ready, diag_stored, skewed, flip_zero, flip_ready, bias_turned,
         bias_ready, rsel_loaded, rsel_hi, rsel_ready, raw_ready, raw_free, split_w_hi, split_w, passed) = (
            sem(n) for n in names)

        PIECES = 4
        PARTS = {0: 0, 1: PIECES * TILES1, 2: PIECES * TILES1 + iterations[1]}
        LOADS = {0: 0, 1: TILES1, 2: TILES1 + iterations[1]}
        IN_STEPS = 12
        ROUTE_STEPS = 10
        OUT_STEPS = {0: 4, 1: 3, 2: 6, 3: 3}

        def on_act(h):
            return h % 8 in (1, 4, 6)

        def count_act(h):
            return sum(on_act(n) for n in range(h + 1))

        def taken(eng, i, h):
            if on_act(h):
                eng.wait_ge(probT_act, count_act(H2 - 1) * i + count_act(h))
            else:
                eng.wait_ge(probT_dve, (H2 - count_act(H2 - 1)) * i + h + 1 - count_act(h))

        blk = ctx.enter_context(nc.Block())

        def apart(eng):
            eng.sem_inc(passed, 1)

        def passes(eng, n, body):
            body(0, True, False)
            with eng.Fori(1, n - 1) as i:
                body(i, False, False)
            body(n - 1, False, True)

        def leave(eng):
            eng.drain().then_inc(phase_done, 1)

        def product3(pe, o, lh, ll, rh, rl, start, stop):
            pe.matmul(o, lh, rh, start=start, stop=False, skip_group_check=True)
            pe.matmul(o, lh, rl, start=False, stop=False, skip_group_check=True)
            return pe.matmul(o, ll, rh, start=False, stop=stop, skip_group_check=True)

        @blk.sync
        def _(sp):
            def rows(ap, i, nt):
                return ap[bass.ts(i, nt * P), :].rearrange("(t p) e -> p t e", p=P)

            sp.dma_start(WORK[:, 0:2048], aw0.rearrange("p k n -> p (k n)")).then_inc(aw0_raw, 16)
            sp.dma_start(ropet[:], rope.rearrange("p a b -> p (a b)")).then_inc(consts, 16)
            sp.dma_start(lnt[:], ln.rearrange("p a b -> p (a b)")).then_inc(consts, 16)
            sp.sem_inc(raw_free, 1)
            for f in range(4):
                nt = 2 if f in (0, 2) else 4
                n = iterations[f]
                x_turned_in = xt_in_a if nt == 2 else xt_in_f
                x_added = xr_a if nt == 2 else xr_f
                normed = xo_a if nt == 2 else xo_f
                turns = 1 if nt == 2 else KT
                if f:
                    sp.wait_ge(phase_done, 4 * f)
                    sp.wait_ge(stored[f - 1], 16 * iterations[f - 1] + 16)
                if f == 3:
                    sp.dma_start(router_raw, router.rearrange("p k n -> p (k n)")).then_inc(rsel_loaded, 16)
                    sp.dma_start(sel_raw, sel).then_inc(rsel_loaded, 16)
                sp.dma_start(x_turned_in, rows(x_in[f], 0, nt)).then_inc(xt_loaded[f], 16)
                sp.dma_start(x_added, rows(x_in[f], 0, nt)).then_inc(xr_loaded[f], 16)
                sp.sem_inc(stored[f], 16)
                if f == 2:
                    sp.dma_start(small[0:TABLE, 0:D2], rel).then_inc(rel_loaded, 16)
                    sp.wait_ge(diag_ready, 1)
                    sp.dma_start(ediag, WORK[0:1, 0:ROWS]).then_inc(diag_stored, 16)
                    sp.wait_ge(diag_stored, 16)
                    for t in range(2):
                        skew = bass.AP(ediag.tensor, S - P * (t + 1), [[1, P], [1, S]])
                        sp.dma_start(WORK[:, 512 + S * t:512 + S * (t + 1)], skew).then_inc(skewed, 16)
                if nt == 2:
                    sp.wait_ge(xt_turned[f], 1)
                    sp.dma_start(x_turned_in, rows(x_in[f], 1, nt)).then_inc(xt_loaded[f], 16)

                def weights(i):
                    if f == 0:
                        sp.wait_ge(raw_free, i + 1)
                        apart(sp)
                        sp.dma_start(wraw[:], wu1[bass.ts(i, 1), :, :].rearrange("a p n -> p (a n)")).then_inc(raw_ready, 16)
                    if f == 1:
                        sp.wait_ge(raw_free, LOADS[1] + i + 1)
                        apart(sp)
                        sp.dma_start(wraw[:, 0:512], aw2[:, bass.ts(i, 512)]).then_inc(raw_ready, 16)
                    if f == 2:
                        for k in range(2):
                            sp.wait_ge(raw_free, LOADS[2] + 2 * i + k + 1)
                            apart(sp)
                            sp.dma_start(wraw[:], wu3[bass.ts(2 * i + k, 1), :, :].rearrange("a p n -> p (a n)")
                                         ).then_inc(raw_ready, 16)

                def turn_next(i):
                    ahead = i + 2 if nt == 2 else i + 1
                    sp.wait_ge(xt_turned[f], turns * ahead)
                    apart(sp)
                    sp.dma_start(x_turned_in, rows(x_in[f], ahead, nt)).then_inc(xt_loaded[f], 16)

                def store(i):
                    sp.wait_ge(xo_ready[f], i + 1)
                    apart(sp)
                    sp.dma_start(rows(x_out[f], i, nt), normed).then_inc(stored[f], 16)

                def add_next(i):
                    sp.dma_start(x_added, rows(x_in[f], i, nt)).then_inc(xr_loaded[f], 16)

                turn_next(0)
                weights(0)
                with sp.Fori(1, n - 2 if nt == 2 else n - 1) as i:
                    turn_next(i)
                    weights(i)
                    store(i - 1)
                    add_next(i)
                for i in (range(n - 2, n) if nt == 2 else range(n - 1, n)):
                    weights(i)
                    store(i - 1)
                    add_next(i)
                if f == 2:
                    sp.wait_ge(raw_free, LOADS[2] + TILES3)
                    sp.dma_start(wraw[:], wu3[TILES3 - 1]).then_inc(raw_ready, 16)
                store(n - 1)
            sp.wait_ge(stored[3], 16 * iterations[3] + 16)

        @blk.tensor
        def _(pe):
            pe.wait_ge(ident_ready, 2)

            def x_turn(f, b):
                pe.wait_ge(xt_loaded[f], 16 * b + 16)
                for k in range(KT):
                    for t in range(2):
                        m = pe.transpose(ps[:, B_XT, S * k + P * t:S * k + P * (t + 1)],
                                         xt_in_a[:, t, P * k:P * (k + 1)], ident[:])
                m.then_inc(xt_turned[f], 1)

            def qk(f, b, t):
                tok = slice(P * t, P * (t + 1))
                for k in range(KT):
                    m = product3(pe, ps[:, B_QK[t], :], XT_a[0][:, k, tok], XT_a[1][:, k, tok],
                                 AW[:, 0, k, 0:512], AW[:, 1, k, 0:512], k == 0, k == KT - 1)
                m.then_inc(qk_ready[f], 1)

            def v(f, b):
                pe.wait_ge(heads_q[f], 4 * b + 4)
                for t in range(2):
                    tok = slice(P * t, P * (t + 1))
                    for k in range(KT):
                        m = product3(pe, ps[:, B_V, S * t:S * (t + 1)], XT_a[0][:, k, tok], XT_a[1][:, k, tok],
                                     AW[:, 0, k, 512:768], AW[:, 1, k, 512:768], k == 0, k == KT - 1)
                m.then_inc(v_ready[f], 1)

            def heads(f, b, n):
                if n == 0:
                    pe.wait_ge(split_ready[f], 4 * b + 4)
                else:
                    pe.wait_ge(heads_q[f], 4 * b + n)
                    pe.wait_ge(heads_k[f], 4 * b + n)
                for src, bank in ((QS, B_QT), (KS, B_KT)):
                    w = src.bitcast(F32).rearrange("p (t g c) -> p t g c", t=2, g=8)
                    for g in range(2):
                        for t in range(2):
                            m = pe.transpose(ps[:, bank, S * g + P * t:S * g + P * (t + 1)],
                                             w[:, t, 2 * n + g, :], ident[:])
                    m.then_inc(heads_turned[f], 1)

            def c_turn(f, b, n, groups):
                if n == 0:
                    pe.wait_ge(o_copied[f], groups // 2 * (b + 1))
                if n >= 2:
                    pe.wait_ge(ctx_done[f], len(C_BANKS[f]) * b + n - 1)
                ot = OT[:, 0:groups * S].rearrange("p (g q) -> p g q", g=groups)
                t, c = divmod(n, len(C_BANKS[f]) // 2)
                for g in range(4):
                    m = pe.transpose(ps[:, C_BANKS[f][n], P * g:P * (g + 1)], ot[:, 4 * c + g, P * t:P * (t + 1)], ident[:])
                m.then_inc(c_turned[f], 1)

            def ct_turn(f, b):
                pe.wait_ge(ctx_done[f], len(C_BANKS[f]) * (b + 1))
                for k in range(KT):
                    for t in range(2):
                        m = pe.transpose(ps[:, B_CT, S * k + P * t:S * k + P * (t + 1)],
                                         ctx_a[:, t, P * k:P * (k + 1)], ident[:])
                m.then_inc(ct_turned[f], 1)

            def project(f, b):
                pe.wait_ge(ct_ready[f], b + 1)
                for t in range(2):
                    tok = slice(P * t, P * (t + 1))
                    for k in range(KT):
                        m = product3(pe, ps[:, B_Y, E * t:E * (t + 1)], CT_a[0][:, k, tok], CT_a[1][:, k, tok],
                                     AW[:, 0, k, 768:1024], AW[:, 1, k, 768:1024], k == 0, k == KT - 1)
                m.then_inc(y_ready[f], 1)

            vp = v_and_one(0)

            def phase0():
                pe.wait_ge(aw0_ready, 1)
                pe.wait_ge(vp_ones, 1)
                n = iterations[0]

                def scores(i, p):
                    if p % 2 == 0:
                        pe.wait_ge(heads_q[0], 4 * i + p // 2 + 1)
                        pe.wait_ge(heads_k[0], 4 * i + p // 2 + 1)
                    if p >= 2:
                        pe.wait_ge(squared, H0 // 2 * i + p - 1)
                    for h in (2 * p, 2 * p + 1):
                        r = slice(64 * (h % 2), 64 * (h % 2) + 64)
                        b = 2 * (p % 2) + h % 2
                        pe.matmul(ps[:, b, 0:S], KTT[r, h // 2, 0:P], QT[r, h // 2, :], start=True, stop=True)
                        m = pe.matmul(ps[:, b, S:S + P], KTT[r, h // 2, P:S], QT[r, h // 2, P:S], start=True, stop=True)
                    m.then_inc(score_ready[0], 1)

                def mix(i, quad):
                    pe.wait_ge(quartic, H0 // 2 * i + 2 * quad + 2)
                    for kt in range(2):
                        for j in range(4):
                            pv = P4(2 * quad + j // 2)[:, j % 2, :]
                            cols = slice(S * (quad % 2) + P * kt, S * (quad % 2) + S)
                            at = (D0 + 1) * (4 * quad + j)
                            m = pe.matmul(ps[32 * j:32 * j + 32, 4 + quad // 2, cols], vp[:, kt, at:at + 32],
                                          pv[:, 0:S] if kt == 0 else pv[:, S:S + P],
                                          start=kt == 0, stop=kt == 1, skip_group_check=True,
                                          tile_position=(0, 32 * j))
                    m.then_inc(mixed0, 1)

                def one(i, first, last):
                    for p in range(H0 // 2):
                        scores(i, p)
                        if p >= 2 and p % 2 == 0:
                            mix(i, p // 2 - 1)
                        if p == 0:
                            pe.wait_ge(heads_k[0], 4 * i + 4)
                            pe.wait_ge(vp_ready[0], i + 1)
                            if not last:
                                x_turn(0, i + 1)
                            if not first:
                                c_turn(0, i - 1, 0, 4)
                        if p == 1 and not first:
                            if not last:
                                pe.wait_ge(xt_ready[0], i + 2)
                            c_turn(0, i - 1, 1, 4)
                        if p == 2:
                            if not first:
                                ct_turn(0, i - 1)
                            if not last:
                                pe.wait_ge(xt_ready[0], i + 2)
                                qk(0, i + 1, 0)
                        if p == 3:
                            if not first:
                                pe.wait_ge(ct_ready[0], i)
                            if not last:
                                qk(0, i + 1, 1)
                                pe.wait_ge(in_step, IN_STEPS * (i + 1) + 3)
                            if not first:
                                project(0, i - 1)
                    if not last:
                        if not first:
                            pe.wait_ge(out_step[0], OUT_STEPS[0] * (i - 1) + 3)
                        heads(0, i + 1, 0)
                        heads(0, i + 1, 1)
                        heads(0, i + 1, 2)
                    mix(i, H0 // 4 - 1)
                    if not last:
                        heads(0, i + 1, 3)
                        v(0, i + 1)

                x_turn(0, 0)
                pe.wait_ge(xt_ready[0], 1)
                for t in range(2):
                    qk(0, 0, t)
                for q in range(4):
                    heads(0, 0, q)
                v(0, 0)
                passes(pe, n, one)
                for c in range(2):
                    c_turn(0, n - 1, c, 4)
                ct_turn(0, n - 1)
                project(0, n - 1)
                leave(pe)

            def phase2():
                pe.wait_ge(rel_neg, 1)
                pe.matmul(ps[0:1, 0, 0:TABLE], small[0:TABLE, 16:17], ident[0:TABLE, 0:TABLE],
                          start=True, stop=True).then_inc(diag_row, 1)
                pe.wait_ge(skewed, 32)
                pe.wait_ge(flip_ready, 1)
                pe.matmul(ps[:, 1, :], WORK[:, 1024:1024 + P], WORK[:, 512:1024], start=True, stop=True
                          ).then_inc(bias_turned, 1)
                pe.wait_ge(split_w, PARTS[2])
                pe.wait_ge(vp_ones, 2)
                pe.wait_ge(bias_ready, 1)

                n = iterations[2]

                def scores(i, h):
                    j, g = h % 4, h // 4
                    r = slice(32 * j, 32 * j + 32)
                    if h % 8 == 0:
                        pe.wait_ge(heads_q[2], 4 * i + h // 8 + 1)
                        pe.wait_ge(heads_k[2], 4 * i + h // 8 + 1)
                    if h >= 2:
                        pe.wait_ge(biased_ready, H2 * i + h - 1)
                    for t in range(2):
                        m = pe.matmul(ps[:, h % 2, S * t:S * (t + 1)], QT[r, g, P * t:P * (t + 1)], KTT[r, g, :],
                                      start=True, stop=True, tile_position=(32 * j, 0))
                    m.then_inc(score_ready[2], 1)

                def turn(i, h):
                    pe.wait_ge(prob_ready, H2 * i + h + 1)
                    if h >= 2:
                        taken(pe, i, h - 2)
                    for kt in range(2):
                        for t in range(2):
                            m = pe.transpose(ps[:, 2 + h % 2, S * kt + P * t:S * kt + P * (t + 1)],
                                             prob(h)[:, t, P * kt:P * (kt + 1)], ident[:])
                    m.then_inc(probT_turned, 1)

                def mix(i, quad):
                    if quad >= 4 and quad % 2 == 0:
                        pe.wait_ge(o_copied[2], 4 * i + quad // 2 - 1)
                    taken(pe, i, max(h for h in range(4 * quad, 4 * quad + 4) if on_act(h)))
                    taken(pe, i, max(h for h in range(4 * quad, 4 * quad + 4) if not on_act(h)))
                    for kt in range(2):
                        for j in range(4):
                            h = 4 * quad + j
                            at = (D2 + 1) * h
                            m = pe.matmul(ps[32 * j:32 * j + 32, 4 + quad // 2 % 2, S * (quad % 2):S * (quad % 2 + 1)],
                                          vp[:, kt, at:at + 32], probT(h)[:, kt, :], start=kt == 0, stop=kt == 1,
                                          skip_group_check=True, tile_position=(0, 32 * j))
                    m.then_inc(mixed2, 1)

                def one(i, first, last):
                    for h in range(H2 + 4):
                        if h < H2:
                            scores(i, h)
                        if 2 <= h < H2 + 2:
                            turn(i, h - 2)
                        if h >= 7 and h % 4 == 3:
                            mix(i, (h - 7) // 4)
                        if h == 0:
                            pe.wait_ge(heads_k[2], 4 * i + 4)
                            pe.wait_ge(vp_ready[2], i + 1)
                            if not last:
                                x_turn(2, i + 1)
                        if not first:
                            if h == 1:
                                c_turn(2, i - 1, 0, 8)
                            if h == 2:
                                if not last:
                                    pe.wait_ge(xt_ready[2], i + 2)
                                c_turn(2, i - 1, 1, 8)
                            if h in (4, 5):
                                c_turn(2, i - 1, h - 2, 8)
                            if h == 7:
                                ct_turn(2, i - 1)
                        if not last:
                            if h == 8:
                                pe.wait_ge(xt_ready[2], i + 2)
                                qk(2, i + 1, 0)
                            if h == 10:
                                if not first:
                                    pe.wait_ge(ct_ready[2], i)
                                qk(2, i + 1, 1)
                        if h == 12 and not first:
                            if not last:
                                pe.wait_ge(split_ready[2], 4 * (i + 1) + 2)
                            project(2, i - 1)
                        if not last:
                            if h == 18:
                                if not first:
                                    pe.wait_ge(out_step[2], OUT_STEPS[2] * (i - 1) + 5)
                                heads(2, i + 1, 0)
                            if h == 22:
                                heads(2, i + 1, 1)
                            if h == 26:
                                heads(2, i + 1, 2)
                            if h == H2 + 1:
                                heads(2, i + 1, 3)
                    if not last:
                        v(2, i + 1)

                x_turn(2, 0)
                pe.wait_ge(xt_ready[2], 1)
                for t in range(2):
                    qk(2, 0, t)
                for q in range(4):
                    heads(2, 0, q)
                v(2, 0)
                passes(pe, n, one)
                for c in range(4):
                    c_turn(2, n - 1, c, 8)
                ct_turn(2, n - 1)
                project(2, n - 1)
                leave(pe)

            def feed_forward(f, tiles):
                def gate_up(i, j):
                    if j >= 2:
                        pe.wait_ge(prod_ready[f], tiles * i + j - 1)
                    for n, ready in enumerate((gate_ready[f], up_ready[f])):
                        for k in range(KT):
                            c = slice((n * KT + k) * P, (n * KT + k + 1) * P)
                            m = product3(pe, ps[:, 2 + 2 * (j % 2) + n, :], WU[:, j, 0, c], WU[:, j, 1, c],
                                         XT_f[0][:, k, :], XT_f[1][:, k, :], k == 0, k == KT - 1)
                        m.then_inc(ready, 1)
                    if f == 3:
                        if j == 0:
                            logits_turned(i)
                        if j == 1:
                            router_columns(i)
                            spread(j - 1)
                        if j >= 1:
                            spread(j)

                def spread(j):
                    pe.matmul(ps[:, 7 - j % 2, :], SELW[:, P * j:P * (j + 1)], CWT, start=True, stop=True
                              ).then_inc(wcol_ready, 1)

                def down(i, j):
                    pe.wait_ge(hid_ready[f], tiles * i + j + 1)
                    if j == 0:
                        pe.wait_ge(z_done[f], i + 1)
                    hh, hl = HT[:, j % 3, 0, :], HT[:, j % 3, 1, :]
                    wd = [WU[:, j, h, 2 * KT * P:UNIT] for h in range(2)]
                    for t in range(4):
                        tok = slice(P * t, P * (t + 1))
                        m = product3(pe, ps[:, t // 2, E * (t % 2):E * (t % 2 + 1)], hh[:, tok], hl[:, tok],
                                     wd[0], wd[1], j == 0 and t % 2 == 0, j == tiles - 1)
                    m.then_inc(down_done[f], 1)

                def router_logits(i):
                    n = 0
                    for k in range(KT):
                        for a in (routh, routl):
                            for b in XT_f:
                                m = pe.matmul(ps[0:GATES, 6, :], a[:, GATES * k:GATES * (k + 1)], b[:, k, :],
                                              start=n == 0, stop=n == 4 * KT - 1, skip_group_check=True)
                                n += 1
                    m.then_inc(lgT_turned, 1)

                def logits_turned(i):
                    pe.wait_ge(lgT_ready, i + 1)
                    apart(pe)
                    for t in range(4):
                        m = pe.transpose(ps[:, 7, GATES * t:GATES * (t + 1)], lgT[:, P * t:P * (t + 1)],
                                         ident[0:GATES, 0:GATES])
                    m.then_inc(lg_turned, 1)

                def router_columns(i):
                    pe.wait_ge(cw_ready, i + 1)
                    for t in range(4):
                        m = pe.transpose(ps[0:2 * GATES, 6, P * t:P * (t + 1)], cs2[:, t, :], ident[:])
                    m.then_inc(cwT_turned, 1)
                    pe.wait_ge(cwT_ready, i + 1)

                def x_turn(b, k):
                    if k == 0:
                        pe.wait_ge(xt_loaded[f], 16 * b + 16)
                    for t in range(4):
                        m = pe.transpose(ps[:, 6 + k, P * t:P * (t + 1)], xt_in_f[:, t, P * k:P * (k + 1)], ident[:])
                    m.then_inc(xt_turned[f], 1)

                def one(i, last):
                    pe.wait_ge(xt_ready[f], KT * i + KT)
                    if f == 3:
                        router_logits(i)
                    gate_up(i, 0)
                    gate_up(i, 1)
                    for j in range(2, tiles):
                        if j == tiles - 1 and f == 3:
                            pe.wait_ge(split_w, PARTS[2] + TILES3)
                        gate_up(i, j)
                        down(i, j - 2)
                    for k in range(KT):
                        if not last:
                            if f == 3:
                                pe.wait_ge(prod_ready[f], tiles * i + tiles - 1 + k)
                            x_turn(i + 1, k)
                        down(i, tiles - 2 + k)

                x_turn(0, 0)
                x_turn(0, 1)
                with pe.Fori(0, iterations[f] - 1) as i:
                    one(i, False)
                one(iterations[f] - 1, True)
                leave(pe)

            phase0()
            pe.wait_ge(split_w, PARTS[1])
            feed_forward(1, TILES1)
            phase2()
            pe.wait_ge(split_w, PARTS[2] + TILES3 - 1)
            pe.wait_ge(rsel_ready, 1)
            feed_forward(3, TILES3)

        @blk.scalar
        def _(act):
            def halves(bank):
                return ps[:, bank, :].rearrange("p (k t) -> p k t", k=2)

            def x_hi(f, b):
                act.wait_ge(xt_turned[f], b + 1)
                act.copy(XT_a[0], halves(B_XT)).then_inc(xt_hi[f], 1)

            def q_heads(f, b, n):
                act.wait_ge(heads_turned[f], 8 * b + 2 * n + 1)
                act.copy(QT[:, 2 * n:2 * n + 2, :], halves(B_QT)).then_inc(heads_q[f], 1)

            def context_hi(f, b):
                act.wait_ge(ct_turned[f], b + 1)
                act.copy(CT_a[0], halves(B_CT)).then_inc(ct_hi[f], 1)

            def phase0():
                act.wait_ge(aw0_raw, 16)
                act.copy(AW[:, 0], WORK[:, 0:2048].rearrange("p (k n) -> p k n", k=KT)).then_inc(aw0_hi, 1)
                n = iterations[0]

                def centred_squares(b):
                    act.wait_ge(in_step, IN_STEPS * b + 8)
                    act.square(SQ, CEN).then_inc(cen_squared, 1)

                def hi_parts(b):
                    act.wait_ge(in_step, IN_STEPS * b + 12)
                    n5 = SQ.rearrange("p (t w h d) -> p t w h d", t=2, w=2, h=H0)
                    for w, (dst, places) in enumerate(((QS, (0, 2)), (KS, (0, 1)))):
                        d5 = dst.rearrange("p (t h s d) -> p t h s d", t=2, h=H0, s=4)
                        for s in places:
                            act.copy(d5[:, :, :, s, :], n5[:, :, w]).then_inc(split_hi[0], 1)

                def k_heads(b, n):
                    act.wait_ge(heads_turned[0], 8 * b + 2 * n + 2)
                    act.copy(KTT[:, 2 * n:2 * n + 2, :], halves(B_KT)).then_inc(heads_k[0], 1)

                def values(b):
                    act.wait_ge(v_ready[0], b + 1)
                    o = v_and_one(0)[:, :, 0:H0 * (D0 + 1)].rearrange("p t (h c) -> p t h c", h=H0)
                    act.copy(o[:, :, :, 0:D0], ps[:, B_V, :].rearrange("p (t h d) -> p t h d", t=2, h=H0)
                             ).then_inc(vp_ready[0], 1)

                def one(i, first, last):
                    for p in range(H0 // 2):
                        act.wait_ge(score_ready[0], H0 // 2 * i + p + 1)
                        if p >= 2:
                            act.wait_ge(quartic, H0 // 2 * i + p - 1)
                        b = 2 * (p % 2)
                        act.square(U(p), ps[:, b:b + 2, 0:384]).then_inc(squared, 1)
                        if p == 0 and not last:
                            x_hi(0, i + 1)
                        if p == 2 and not first:
                            context_hi(0, i - 1)
                        if p == 5 and not last:
                            centred_squares(i + 1)
                    if not last:
                        hi_parts(i + 1)
                        for n in range(4):
                            q_heads(0, i + 1, n)
                            k_heads(i + 1, n)
                        values(i + 1)

                x_hi(0, 0)
                centred_squares(0)
                hi_parts(0)
                for q in range(4):
                    q_heads(0, 0, q)
                    k_heads(0, q)
                values(0)
                passes(act, n, one)
                context_hi(0, n - 1)
                leave(act)

            def phase2():
                n = iterations[2]

                def hi_parts(b, t):
                    act.wait_ge(qk_ready[2], 2 * b + t + 1)
                    src = ps[:, B_QK[t], :].rearrange("p (w h d) -> p w h d", w=2, h=H2)
                    for w, (dst, places) in enumerate(((QS, (0, 2)), (KS, (0, 1)))):
                        d5 = dst.rearrange("p (t h s d) -> p t h s d", t=2, h=H2, s=4)
                        for s in places:
                            act.mul(d5[:, t, :, s, :], src[:, w], QSCALE if w == 0 else 1.0).then_inc(split_hi[2], 1)

                def one(i, first, last):
                    for h in range(H2 + 2):
                        if h < H2:
                            act.wait_ge(biased_ready, H2 * i + h + 1)
                            if h >= 3:
                                taken(act, i, h - 3)
                            for t in range(2):
                                k = 2 * (h % 2) + t
                                m = act.activation(prob(h)[:, t, :], biased(h)[:, t, :], ACT.Exp, scale=-1.0,
                                                   bias=mneg[:, k:k + 1])
                            m.then_inc(prob_ready, 1)
                        if h >= 2 and on_act(h - 2):
                            act.wait_ge(probT_turned, H2 * i + h - 1)
                            if h >= 8:
                                act.wait_ge(mixed2, H2 // 4 * i + (h - 8) // 4 + 1)
                            act.copy(probT(h - 2), halves(2 + (h - 2) % 2)).then_inc(probT_act, 1)
                        if h == 1 and not last:
                            x_hi(2, i + 1)
                        if h == 8 and not first:
                            context_hi(2, i - 1)
                        if not last:
                            if h in (9, 11):
                                hi_parts(i + 1, (h - 9) // 2)
                            if h in (19, 23, 27):
                                q_heads(2, i + 1, (h - 19) // 4)
                    if not last:
                        q_heads(2, i + 1, 3)

                x_hi(2, 0)
                for t in range(2):
                    hi_parts(0, t)
                for q in range(4):
                    q_heads(2, 0, q)
                passes(act, n, one)
                context_hi(2, n - 1)
                leave(act)

            def feed_forward(f, tiles):
                if f == 3:
                    act.wait_ge(rsel_loaded, 32)
                    act.copy(SELW, sel_raw)
                    act.copy(routh[:], router_raw).then_inc(rsel_hi, 1)

                def x_hi(b, k):
                    act.wait_ge(xt_turned[f], KT * b + k + 1)
                    act.copy(XT_f[0][:, k, :], ps[:, 6 + k, :]).then_inc(xt_hi[f], 1)

                def one(i, last):
                    if f == 3:
                        act.wait_ge(lgT_turned, i + 1)
                        act.copy(lgT, ps[0:GATES, 6, :]).then_inc(lgT_ready, 1)
                        act.wait_ge(lg_ready, i + 1)
                        act.activation(ex, lg, ACT.Exp).then_inc(ex_ready, 1)

                    def silu(j):
                        act.wait_ge(gate_ready[f], tiles * i + j + 1)
                        act.activation(sg[:, j % 2, :], ps[:, 2 + 2 * (j % 2), :], ACT.Silu).then_inc(silu_ready[f], 1)

                    def hidden_hi(j):
                        act.wait_ge(prod_ready[f], tiles * i + j + 1)
                        if j >= 3:
                            act.wait_ge(down_done[f], tiles * i + j - 2)
                        act.copy(HT[:, j % 3, 0, :], hf[:, j % 3, :]).then_inc(hid_hi[f], 1)

                    silu(0)
                    if f == 3:
                        act.wait_ge(cwT_turned, i + 1)
                        act.copy(CWT, ps[0:2 * GATES, 6, :]).then_inc(cwT_ready, 1)
                    for j in range(1, tiles):
                        silu(j)
                        hidden_hi(j - 1)
                    hidden_hi(tiles - 1)
                    if not last:
                        x_hi(i + 1, 0)
                        x_hi(i + 1, 1)

                x_hi(0, 0)
                x_hi(0, 1)
                with act.Fori(0, iterations[f] - 1) as i:
                    one(i, False)
                one(iterations[f] - 1, True)
                leave(act)

            phase0()
            feed_forward(1, TILES1)
            phase2()
            feed_forward(3, TILES3)

        @blk.vector
        def _(dve):
            def halves(bank):
                return ps[:, bank, :].rearrange("p (k t) -> p k t", k=2)

            def step(count, value, m, alone=False):
                m.then_inc(count, 1)
                dve.wait_ge(count, value)
                if alone:
                    apart(dve)

            def add(f, b, nt, xr, banks):
                n = OUT_STEPS[f] * b + OUT_STEPS[f] - 1 - len(banks)
                dve.wait_ge(xr_loaded[f], 16 * b + 16)
                for k, bank in enumerate(banks):
                    m = dve.tensor_tensor(xr[:, 2 * k:2 * k + 2, :], halves(bank), xr[:, 2 * k:2 * k + 2, :], ALU.add)
                    step(out_step[f], n + k + 1, m)
                if f in (1, 3):
                    dve.sem_inc(z_done[f], 1)
                for t in range(nt):
                    m = dve.bn_stats(stats[:, t, :], xr[:, t, :])
                step(out_step[f], n + len(banks) + 1, m, alone=True)
                for t in range(nt):
                    m = dve.bn_aggr(mv[:, t, :], stats[:, t, :])
                m.then_inc(var_ready[f], 1)

            def norm(f, b, nt, xr, xo):
                dve.wait_ge(rstd_ready[f], b + 1)
                dve.wait_ge(stored[f], 16 * b + 16)
                for t in range(nt):
                    m = dve.tensor_scalar(xo[:, t, :], xr[:, t, :], mv[:, t, 0:1], rstd[:, t:t + 1], ALU.subtract, ALU.mult)
                m.then_inc(xo_ready[f], 1)

            def x_lo(f, b):
                dve.wait_ge(xt_hi[f], b + 1)
                dve.tensor_tensor(XT_a[1], halves(B_XT), XT_a[0].bitcast(F32), ALU.subtract).then_inc(xt_ready[f], 1)

            def outputs(f, b, n, groups):
                if f == 0:
                    dve.wait_ge(mixed0, H0 // 4 * b + 2 * n + 2)
                else:
                    dve.wait_ge(mixed2, H2 // 4 * b + 2 * n + 2)
                dve.tensor_copy(OT[:, 512 * n:512 * (n + 1)], ps[:, 4 + n % 2, :]).then_inc(o_copied[f], 1)

            def context(f, b, n, d):
                nb = len(C_BANKS[f])
                dve.wait_ge(c_turned[f], nb * b + n + 1)
                v = ps[:, C_BANKS[f][n], :].rearrange("p (h c) -> p h c", c=32)
                r = rden[:, 16 * n:16 * (n + 1)].unsqueeze(2)
                step(out_step[f], OUT_STEPS[f] * b + n + 1, dve.reciprocal(r, v[:, :, d:d + 1]))
                t, part = divmod(n, nb // 2)
                o = ctx_a[:, t, 16 * d * part:16 * d * (part + 1)].rearrange("p (h c) -> p h c", h=16)
                dve.tensor_tensor(o, v[:, :, 0:d], r.to_broadcast([P, 16, d]), ALU.mult).then_inc(ctx_done[f], 1)

            def context_lo(f, b):
                dve.wait_ge(ct_hi[f], b + 1)
                dve.tensor_tensor(CT_a[1], halves(B_CT), CT_a[0].bitcast(F32), ALU.subtract).then_inc(ct_ready[f], 1)

            def phase0():
                dve.wait_ge(aw0_hi, 1)
                raw = WORK[:, 0:2048].rearrange("p (k n) -> p k n", k=KT)
                dve.tensor_tensor(AW[:, 1], raw, AW[:, 0].bitcast(F32), ALU.subtract).then_inc(aw0_ready, 1)
                dve.wait_ge(aw0_ready, 1)
                dve.wait_ge(consts, 32)
                n = iterations[0]
                rh = ROT.rearrange("p (n d) -> p n d", d=D0)
                ch = CEN.rearrange("p (n d) -> p n d", d=D0)
                sh = SQ.rearrange("p (n d) -> p n d", d=D0)
                full = [P, 4 * H0, D0]

                def rope_half(b, t):
                    r4 = ROT.rearrange("p (t h s e) -> p t h s e", t=2, s=2, e=8)
                    r24 = ROT2.rearrange("p (t h s e) -> p t h s e", t=2, s=2, e=8)
                    dve.wait_ge(qk_ready[0], 2 * b + t + 1)
                    src = ps[:, B_QK[t], :].rearrange("p (h s e) -> p h s e", s=2, e=8)
                    cos = ropet[:, 16 * t:16 * t + 8].unsqueeze(1).unsqueeze(1).to_broadcast([P, 2 * H0, 2, 8])
                    sin = ropet[:, 16 * t + 8:16 * t + 16].unsqueeze(1).to_broadcast([P, 2 * H0, 8])
                    dve.tensor_tensor(r4[:, t], src, cos, ALU.mult)
                    dve.scalar_tensor_tensor(out=r24[:, t, :, 0, :], in0=src[:, :, 1, :], scalar=-1.0, in1=sin,
                                             op0=ALU.mult, op1=ALU.mult)
                    dve.tensor_tensor(r24[:, t, :, 1, :], src[:, :, 0, :], sin, ALU.mult).then_inc(in_step, 3)

                def centre(b):
                    dve.wait_ge(rope_added, b + 1)
                    step(in_step, IN_STEPS * b + 7, dve.tensor_reduce(hsum, rh, AX_X, ALU.add))
                    step(in_step, IN_STEPS * b + 8,
                         dve.scalar_tensor_tensor(out=ch, in0=hsum.unsqueeze(2).to_broadcast(full), scalar=-1.0 / D0,
                                                  in1=rh, op0=ALU.mult, op1=ALU.add))

                def variance(b):
                    dve.wait_ge(cen_squared, b + 1)
                    dve.tensor_reduce(hvar, sh, AX_X, ALU.add).then_inc(in_step, 1)

                def scaled(b):
                    dve.wait_ge(head_rstd, b + 1)
                    step(in_step, IN_STEPS * b + 10, dve.tensor_tensor(ch, ch, hrs.unsqueeze(2).to_broadcast(full), ALU.mult))
                    step(in_step, IN_STEPS * b + 11,
                         dve.tensor_tensor(ch, ch, lnt[:, 0:D0].unsqueeze(1).to_broadcast(full), ALU.mult))
                    step(in_step, IN_STEPS * b + 12,
                         dve.tensor_tensor(sh, ch, lnt[:, D0:2 * D0].unsqueeze(1).to_broadcast(full), ALU.add))

                def lo_parts(b):
                    n5 = SQ.rearrange("p (t w h d) -> p t w h d", t=2, w=2, h=H0)
                    for w, (dst, places) in enumerate(((QS, (1, 3)), (KS, (2, 3)))):
                        d5 = dst.rearrange("p (t h s d) -> p t h s d", t=2, h=H0, s=4)
                        dve.wait_ge(split_hi[0], 4 * b + 2 * w + 2)
                        for s in places:
                            dve.tensor_tensor(d5[:, :, :, s, :], n5[:, :, w], d5[:, :, :, 0, :].bitcast(F32), ALU.subtract
                                              ).then_inc(split_ready[0], 1)

                def one(i, first, last):
                    for p in range(H0 // 2):
                        if p == 0:
                            if not first:
                                outputs(0, i - 1, 1, 4)
                            if not last:
                                x_lo(0, i + 1)
                        if p == 2 and not first:
                            context(0, i - 1, 1, D0)
                        dve.wait_ge(masked, H0 // 2 * i + p + 1)
                        if p >= 2:
                            dve.wait_ge(mixed0, H0 // 4 * i + p // 2)
                        dve.tensor_tensor(P4(p), U(p), U(p), ALU.mult).then_inc(quartic, 1)
                        if p == 0 and not first:
                            context(0, i - 1, 0, D0)
                        if p == 2 and not first:
                            context_lo(0, i - 1)
                        if p in (2, 3) and not last:
                            rope_half(i + 1, p - 2)
                        if p == 4:
                            if not first:
                                dve.wait_ge(y_ready[0], i)
                                add(0, i - 1, 2, xr_a, (B_Y,))
                            if not last:
                                centre(i + 1)
                        if p == 5:
                            if not first:
                                norm(0, i - 1, 2, xr_a, xo_a)
                            if not last:
                                variance(i + 1)
                        if p == 6:
                            outputs(0, i, 0, 4)
                            if not last:
                                scaled(i + 1)
                    if not last:
                        lo_parts(i + 1)

                x_lo(0, 0)
                for t in range(2):
                    rope_half(0, t)
                centre(0)
                variance(0)
                scaled(0)
                lo_parts(0)
                passes(dve, n, one)
                outputs(0, n - 1, 1, 4)
                for c in range(2):
                    context(0, n - 1, c, D0)
                context_lo(0, n - 1)
                dve.wait_ge(y_ready[0], n)
                add(0, n - 1, 2, xr_a, (B_Y,))
                norm(0, n - 1, 2, xr_a, xo_a)
                leave(dve)

            def phase2():
                dve.wait_ge(rel_loaded, 16)
                dve.tensor_reduce(small[0:TABLE, 15:16], small[0:TABLE, 0:D2], AX_X, ALU.add).then_inc(rel_mean, 1)
                dve.wait_ge(rel_mean, 1)
                dve.tensor_scalar(small[0:TABLE, 16:17], small[0:TABLE, 15:16], -1.0 / D2, None, ALU.mult
                                  ).then_inc(rel_neg, 1)
                dve.wait_ge(diag_row, 1)
                lo = S - MAXPOS
                dve.tensor_copy(WORK[0:1, lo:lo + TABLE], ps[0:1, 0, 0:TABLE])
                dve.tensor_copy(WORK[0:1, 0:lo], ps[0:1, 0, 0:1].to_broadcast([1, lo]))
                dve.tensor_copy(WORK[0:1, lo + TABLE:ROWS], ps[0:1, 0, TABLE - 1:TABLE].to_broadcast([1, ROWS - lo - TABLE])
                                ).then_inc(diag_ready, 1)
                dve.wait_ge(bias_turned, 1)
                dve.tensor_copy(nb[:], ps[:, 1, :]).then_inc(bias_ready, 1)
                dve.wait_ge(bias_ready, 1)
                nbv = nb[:].rearrange("p (t k) -> p t k", t=2)
                n = iterations[2]

                def lo_parts(b, t):
                    src = ps[:, B_QK[t], :].rearrange("p (w h d) -> p w h d", w=2, h=H2)
                    dve.wait_ge(split_hi[2], 8 * b + 4 * t + 4)
                    for w, (dst, places) in enumerate(((QS, (1, 3)), (KS, (2, 3)))):
                        d5 = dst.rearrange("p (t h s d) -> p t h s d", t=2, h=H2, s=4)
                        for s in places:
                            m = dve.scalar_tensor_tensor(out=d5[:, t, :, s, :], in0=src[:, w],
                                                         scalar=QSCALE if w == 0 else 1.0,
                                                         in1=d5[:, t, :, 0, :].bitcast(F32), op0=ALU.mult, op1=ALU.subtract)
                    m.then_inc(split_ready[2], 2)

                def k_heads(b, n):
                    dve.wait_ge(heads_turned[2], 8 * b + 2 * n + 2)
                    dve.tensor_copy(KTT[:, 2 * n:2 * n + 2, :], halves(B_KT)).then_inc(heads_k[2], 1)

                def values(b):
                    dve.wait_ge(v_ready[2], b + 1)
                    o = v_and_one(2)[:, :, 0:H2 * (D2 + 1)].rearrange("p t (h c) -> p t h c", h=H2)
                    dve.tensor_copy(o[:, :, :, 0:D2], ps[:, B_V, :].rearrange("p (t h d) -> p t h d", t=2, h=H2)
                                    ).then_inc(vp_ready[2], 1)

                def one(i, first, last):
                    for h in range(H2 + 3):
                        if h < H2:
                            dve.wait_ge(score_ready[2], H2 * i + h + 1)
                            if h >= 2:
                                dve.wait_ge(prob_ready, H2 * i + h - 1)
                            apart(dve)
                            for t in range(2):
                                k = 2 * (h % 2) + t
                                m = dve.tensor_tensor_reduce(biased(h)[:, t, :], ps[:, h % 2, S * t:S * (t + 1)],
                                                             nbv[:, t, :], 1.0, -FMIN, ALU.add, ALU.min,
                                                             mneg[:, k:k + 1])
                            m.then_inc(biased_ready, 1)
                        if 3 <= h and not on_act(h - 3):
                            dve.wait_ge(probT_turned, H2 * i + h - 2)
                            if h >= 9:
                                dve.wait_ge(mixed2, H2 // 4 * i + (h - 9) // 4 + 1)
                            dve.tensor_copy(probT(h - 3), halves(2 + (h - 3) % 2)).then_inc(probT_dve, 1)
                        if h >= 13 and (h - 13) % 8 == 0:
                            outputs(2, i, (h - 13) // 8, 8)
                        if h == 0 and not first:
                            outputs(2, i - 1, 3, 8)
                        if h == 1 and not last:
                            x_lo(2, i + 1)
                        if not first:
                            if h in (2, 4, 5, 6):
                                context(2, i - 1, (2, 4, 5, 6).index(h), D2)
                            if h == 9:
                                context_lo(2, i - 1)
                            if h == 14:
                                dve.wait_ge(y_ready[2], i)
                                add(2, i - 1, 2, xr_a, (B_Y,))
                            if h == 17:
                                norm(2, i - 1, 2, xr_a, xo_a)
                        if not last:
                            if h in (10, 12):
                                lo_parts(i + 1, (h - 10) // 2)
                            if h in (20, 24, 28):
                                k_heads(i + 1, (h - 20) // 4)
                    if not last:
                        k_heads(i + 1, 3)
                        values(i + 1)

                x_lo(2, 0)
                for t in range(2):
                    lo_parts(0, t)
                for q in range(4):
                    k_heads(0, q)
                values(0)
                passes(dve, n, one)
                outputs(2, n - 1, 3, 8)
                for c in range(4):
                    context(2, n - 1, c, D2)
                context_lo(2, n - 1)
                dve.wait_ge(y_ready[2], n)
                add(2, n - 1, 2, xr_a, (B_Y,))
                norm(2, n - 1, 2, xr_a, xo_a)
                leave(dve)

            def feed_forward(f, tiles):
                if f == 3:
                    dve.wait_ge(rsel_hi, 1)
                    dve.tensor_tensor(routl[:], router_raw, routh[:].bitcast(F32), ALU.subtract).then_inc(rsel_ready, 1)
                dve.sem_inc(z_done[f], 1)

                def x_lo(b, k):
                    dve.wait_ge(xt_hi[f], KT * b + k + 1)
                    dve.tensor_tensor(XT_f[1][:, k, :], ps[:, 6 + k, :], XT_f[0][:, k, :].bitcast(F32), ALU.subtract
                                      ).then_inc(xt_ready[f], 1)

                def one(i, first, last):
                    if f == 3:
                        route(i)

                    def product(j):
                        dve.wait_ge(silu_ready[f], tiles * i + j + 1)
                        dve.wait_ge(up_ready[f], tiles * i + j + 1)
                        up, s, h = ps[:, 3 + 2 * (j % 2), :], sg[:, j % 2, :], hf[:, j % 3, :]
                        if f == 1:
                            dve.tensor_tensor(h, up, s, ALU.mult).then_inc(prod_ready[f], 1)
                        else:
                            dve.tensor_tensor(tt[:, j % 3, :], up, s, ALU.mult).then_inc(prod_u, 1)
                            dve.wait_ge(prod_u, tiles * i + j + 1)
                            dve.wait_ge(wcol_ready, tiles * i + j + 1)
                            dve.tensor_tensor(h, ps[:, 7 - j % 2, :], tt[:, j % 3, :], ALU.mult).then_inc(prod_ready[f], 1)

                    def hidden_lo(j):
                        dve.wait_ge(hid_hi[f], tiles * i + j + 1)
                        dve.tensor_tensor(HT[:, j % 3, 1, :], hf[:, j % 3, :], HT[:, j % 3, 0, :].bitcast(F32),
                                          ALU.subtract).then_inc(hid_ready[f], 1)

                    product(0)
                    if not first:
                        norm(f, i - 1, 4, xr_f, xo_f)
                    for j in range(1, tiles):
                        product(j)
                        hidden_lo(j - 1)
                    hidden_lo(tiles - 1)
                    if not last:
                        x_lo(i + 1, 0)
                        x_lo(i + 1, 1)
                    dve.wait_ge(down_done[f], tiles * i + tiles)
                    add(f, i, 4, xr_f, (0, 1))

                x_lo(0, 0)
                x_lo(0, 1)
                passes(dve, iterations[f], one)
                norm(f, iterations[f] - 1, 4, xr_f, xo_f)
                leave(dve)

            def route(i):
                dve.wait_ge(lg_turned, i + 1)
                raw = ps[:, 7, 0:4 * GATES].rearrange("p (t g) -> p t g", t=4)
                step(route_step, ROUTE_STEPS * i + 1, dve.tensor_reduce(den, raw[:, :, 0:NEXP], AX_X, ALU.max))
                dve.tensor_tensor(lg[:, :, 0:NEXP], raw[:, :, 0:NEXP], den.unsqueeze(2).to_broadcast([P, 4, NEXP]), ALU.subtract)
                dve.tensor_scalar(lg[:, :, NEXP:GATES], raw[:, :, NEXP:GATES], -1.0, None, ALU.mult).then_inc(lg_ready, 1)
                dve.wait_ge(ex_ready, i + 1)
                apart(dve)
                for t in range(4):
                    m = dve.max(top[:, t, :], ex[:, t, 0:NEXP])
                step(route_step, ROUTE_STEPS * i + 2, m)
                step(route_step, ROUTE_STEPS * i + 3, dve.memset(top[:, :, 2:8], -5.0), alone=True)
                for t in range(4):
                    m = dve.match_replace(pick[:, t, :], top[:, t, :], ex[:, t, 0:NEXP], -1.0)
                step(route_step, ROUTE_STEPS * i + 4, m)
                step(route_step, ROUTE_STEPS * i + 5, dve.tensor_reduce(den, top[:, :, 0:2], AX_X, ALU.add))
                step(route_step, ROUTE_STEPS * i + 6, dve.tensor_scalar(pick, pick, 0.0, None, ALU.is_lt))
                dve.tensor_scalar(cw[:, :, NEXP:GATES], ex[:, :, NEXP:GATES], 1.0, None, ALU.add)
                dve.tensor_tensor(cw[:, :, 0:NEXP], pick, ex[:, :, 0:NEXP], ALU.mult)
                step(route_step, ROUTE_STEPS * i + 7, dve.reciprocal(den, den))
                step(route_step, ROUTE_STEPS * i + 8, dve.reciprocal(cw[:, :, NEXP:GATES], cw[:, :, NEXP:GATES]))
                step(route_step, ROUTE_STEPS * i + 9, dve.tensor_tensor(cw[:, :, 0:NEXP], cw[:, :, 0:NEXP],
                                                den.unsqueeze(2).to_broadcast([P, 4, NEXP]), ALU.mult))
                step(route_step, ROUTE_STEPS * i + 10, dve.tensor_copy(cs2[:, :, 0:GATES].bitcast(F32R), cw))
                dve.tensor_tensor(cs2[:, :, GATES:2 * GATES], cw, cs2[:, :, 0:GATES], ALU.subtract).then_inc(cw_ready, 1)

            phase0()
            feed_forward(1, TILES1)
            phase2()
            feed_forward(3, TILES3)

        @blk.gpsimd
        def _(pool):
            pool.memset(ident[:], 0.0).then_inc(ident_ready, 1)
            pool.memset(minus_half, -0.5).then_inc(half_ready, 1)
            pool.wait_ge(ident_ready, 1)
            pool.affine_select(out=ident[:], in_=ident[:], compare_op=ALU.not_equal, fill=1.0, base=0,
                               pattern=[[-1, P]], channel_multiplier=1).then_inc(ident_ready, 1)

            def ones():
                pool.memset(VP, 1.0).then_inc(vp_ones, 1)

            def split_hi_part(part, hi, raw):
                pool.tensor_copy(hi, raw).then_inc(split_w_hi, 1)

            def split_lo_part(part, lo, hi, raw):
                pool.wait_ge(split_w_hi, part + 1)
                pool.tensor_tensor(lo, raw, hi.bitcast(F32), ALU.subtract).then_inc(split_w, 1)

            def free_raw(parts):
                pool.wait_ge(split_w, parts)
                pool.sem_inc(raw_free, 1)

            def split(load, part, hi, lo, raw):
                pool.wait_ge(raw_ready, 16 * load + 16)
                split_hi_part(part, hi, raw)
                split_lo_part(part, lo, hi, raw)
                free_raw(part + 1)

            def unit(load, part, tile):
                wu = WU[:, bass.ts(tile, 1), :, :]
                split(load, part, wu[:, :, 0, :], wu[:, :, 1, :], wraw[:].unsqueeze(1))

            def layernorm_rstd(f, i, nt):
                pool.wait_ge(var_ready[f], i + 1)
                apart(pool)
                pool.tensor_scalar(rstd[:, 0:nt], mv[:, 0:nt, 1:2].rearrange("p t o -> p (t o)"), EPS, None, ALU.add
                                   ).then_inc(eps_added[f], 1)
                pool.wait_ge(eps_added[f], i + 1)
                pool.tensor_tensor(rstd[:, 0:nt], rstd[:, 0:nt], minus_half[:, 0:nt], ALU.pow).then_inc(rstd_ready[f], 1)

            pool.wait_ge(half_ready, 1)
            ones()
            cols = UNIT // PIECES

            def head_layernorm(b):
                pool.wait_ge(in_step, IN_STEPS * b + 6)
                pool.tensor_tensor(ROT, ROT, ROT2, ALU.add).then_inc(rope_added, 1)

            def head_rsqrt(b):
                pool.wait_ge(in_step, IN_STEPS * b + 9)
                apart(pool)
                pool.tensor_scalar(hrs, hvar, 1.0 / D0, EPS, ALU.mult, ALU.add).then_inc(head_eps, 1)
                pool.wait_ge(head_eps, b + 1)
                pool.tensor_tensor(hrs, hrs, minus_half, ALU.pow).then_inc(head_rstd, 1)

            def one(i, first, last):
                wu = WU[:, bass.ts(i, 1), :, :]
                for p in range(H0 // 2):
                    pool.wait_ge(squared, H0 // 2 * i + p + 1)
                    apart(pool)
                    for block in (0, 2):
                        u = U(p)[:, :, P * block:P * (block + 1)]
                        m = pool.affine_select(out=u, in_=u, compare_op=ALU.is_ge, fill=0.0, base=0,
                                               pattern=[[0, 2], [1, P]], channel_multiplier=-1)
                    m.then_inc(masked, 1)
                    if p == 3 and not last:
                        head_layernorm(i + 1)
                    if p == 4 and not first:
                        layernorm_rstd(0, i - 1, 2)
                    if p == 5 and not last:
                        head_rsqrt(i + 1)
                    piece = slice(cols * (p // 2), cols * (p // 2 + 1))
                    raw, hi, lo = wraw[:, piece].unsqueeze(1), wu[:, :, 0, piece], wu[:, :, 1, piece]
                    if p == 0:
                        pool.wait_ge(raw_ready, 16 * i + 16)
                    if p % 2 == 0:
                        split_hi_part(PIECES * i + p // 2, hi, raw)
                    else:
                        split_lo_part(PIECES * i + p // 2, lo, hi, raw)
                free_raw(PIECES * (i + 1))

            head_layernorm(0)
            head_rsqrt(0)
            passes(pool, iterations[0], one)
            layernorm_rstd(0, iterations[0] - 1, 2)
            leave(pool)
            pool.wait_ge(phase_done, 4)
            aw = AW[:].rearrange("p a b c -> p a (b c)")
            with pool.Fori(0, iterations[1]) as i:
                part = bass.ts(i, 512)
                split(LOADS[1] + i, PARTS[1] + i, aw[:, 0, part], aw[:, 1, part], wraw[:, 0:512])
                layernorm_rstd(1, i, 4)
            leave(pool)
            pool.wait_ge(phase_done, 8)
            ones()
            flip = WORK[:, 1024:1024 + P]
            pool.memset(flip, 0.0).then_inc(flip_zero, 1)
            pool.wait_ge(flip_zero, 1)
            pool.affine_select(out=flip, in_=flip, compare_op=ALU.not_equal, fill=1.0, base=1 - P,
                               pattern=[[1, P]], channel_multiplier=1).then_inc(flip_ready, 1)
            with pool.Fori(0, iterations[2]) as i:
                for k in range(2):
                    unit(LOADS[2] + 2 * i + k, PARTS[2] + 2 * i + k, 2 * i + k)
                layernorm_rstd(2, i, 2)
            leave(pool)
            pool.wait_ge(phase_done, 12)
            unit(LOADS[2] + TILES3 - 1, PARTS[2] + TILES3 - 1, TILES3 - 1)
            with pool.Fori(0, iterations[3]) as i:
                layernorm_rstd(3, i, 4)
            leave(pool)


def kernel(**inputs):
    import numpy as np
    import concourse.bacc as bacc
    from concourse.bass_utils import run_bass_kernel_spmd

    a = {k: np.asarray(v) for k, v in inputs.items()}

    def by_partition(w):
        return np.ascontiguousarray(w.reshape(KT, P, -1).transpose(1, 0, 2))

    def units(gate, up, down, tiles):
        out = np.zeros((tiles, P, UNIT), np.float32)
        for m, w in enumerate((gate, up)):
            full = np.zeros((E, tiles * P), np.float32)
            full[:, :w.shape[1]] = w
            out[:, :, m * KT * P:(m + 1) * KT * P] = (
                full.reshape(KT, P, tiles, P).transpose(2, 1, 0, 3).reshape(tiles, P, KT * P))
        rows = np.zeros((tiles * P, E), np.float32)
        rows[:down.shape[0]] = down
        out[:, :, 2 * KT * P:] = rows.reshape(tiles, P, E)
        return out

    inv = (1.0 / np.float32(10000.0) ** (np.arange(0, D0, 2, dtype=np.float32) / np.float32(D0))).astype(np.float32)
    angle = np.arange(S, dtype=np.float32)[:, None] * inv[None, :]
    rope = np.concatenate([np.cos(angle), np.sin(angle)], axis=1).astype(np.float32)
    sel = np.zeros((2 * GATES, TILES3 * P), np.float32)
    for row in range(NEXP * IE + SI):
        g = min(row // IE, NEXP)
        sel[[g, g + GATES], row] = 1.0

    arrays = {
        "x": a["L0_attn_x"].reshape(T, E),
        "rope": np.ascontiguousarray(rope.reshape(2, P, 16).transpose(1, 0, 2)),
        "ln": np.ascontiguousarray(np.broadcast_to(np.stack([a["L0_attn_ln_scale"], a["L0_attn_ln_bias"]]), (P, 2, D0))),
        "aw0": by_partition(np.concatenate([a["L0_attn_w_qkv"], a["L0_attn_w_out"]], axis=1)),
        "wu1": units(a["L0_ffn_w_gate"].T, a["L0_ffn_w_up"].T, a["L0_ffn_w_down"].T, TILES1),
        "aw2": by_partition(np.concatenate([a["L1_attn_wq"].T, a["L1_attn_wk"].T, a["L1_attn_wv"].T,
                                            a["L1_attn_wo"].T], axis=1)).reshape(P, KT * 1024),
        "rel": a["L1_attn_rel_pos"],
        "wu3": units(np.concatenate([a["L1_ffn_w_gate"].transpose(1, 0, 2).reshape(E, -1), a["L1_ffn_sw_gate"]], axis=1),
                     np.concatenate([a["L1_ffn_w_up"].transpose(1, 0, 2).reshape(E, -1), a["L1_ffn_sw_up"]], axis=1),
                     np.concatenate([a["L1_ffn_w_down"].reshape(-1, E), a["L1_ffn_sw_down"]], axis=0), TILES3),
        "router": by_partition(np.concatenate([a["L1_ffn_router_w"].T, a["L1_ffn_shared_gate_w"][:, None]], axis=1)),
        "sel": sel,
    }
    nc = bacc.Bacc("TRN2", target_bir_lowering=False, num_devices=1)
    in_map, args = {}, []
    for name, v in arrays.items():
        v = np.ascontiguousarray(v)
        in_map[f"in_{name}"] = v
        args.append(nc.dram_tensor(f"in_{name}", v.shape, mybir.dt.from_np(v.dtype), kind="ExternalInput").ap())
    out = nc.dram_tensor("out_x", (T, E), F32, kind="ExternalOutput").ap()
    program(nc, *args, out)
    r = run_bass_kernel_spmd(nc, [in_map], core_ids=[0])
    return r.results[0]["out_x"].reshape(a["L0_attn_x"].shape)
```

```python
from contextlib import ExitStack

import concourse.bass as bass
from concourse import mybir

ALU = mybir.AluOpType
ACT = mybir.ActivationFunctionType
F32 = mybir.dt.float32
F32R = mybir.dt.float32r
AX_X = mybir.AxisListType.X

P = 128
T = 2048
E = 256
S = 256
KT = E // P
EPS = 1e-5
ROWS = 2 * S
NBANK = 8
FMIN = -3.0e38

H0, D0 = 16, 16
H2, D2 = 32, 8
MAXPOS = 64
TABLE = 2 * MAXPOS - 1
F1 = 1024
NEXP, IE, SI = 8, 176, 704
TILES1 = F1 // P
TILES3 = -(-(NEXP * IE + SI) // P)
UNIT = 2 * KT * P + E
GATES = NEXP + 1
QSCALE = -float(D2) ** -0.5


def program(nc, x, rope, ln, aw0, wu1, aw2, rel, wu3, router, sel, out):
    with ExitStack() as ctx:
        def sem(name):
            return ctx.enter_context(nc.semaphore(name))

        def sb(name, width, dt=F32):
            return ctx.enter_context(nc.sbuf_tensor(name, [P, width], dt))

        def cut(buf, at, shape, parts=P):
            n = 1
            for s in shape:
                n *= s
            v = buf[0:parts, at:at + n]
            if len(shape) == 2:
                return v.rearrange("p (a b) -> p a b", a=shape[0])
            if len(shape) == 3:
                return v.rearrange("p (a b c) -> p a b c", a=shape[0], b=shape[1])
            if len(shape) == 4:
                return v.rearrange("p (a b c d) -> p a b c d", a=shape[0], b=shape[1], c=shape[2])
            return v

        x1 = nc.dram_tensor("x1", [T, E], F32, kind="Internal").ap()
        x2 = nc.dram_tensor("x2", [T, E], F32, kind="Internal").ap()
        x3 = nc.dram_tensor("x3", [T, E], F32, kind="Internal").ap()
        ediag = nc.dram_tensor("ediag", [1, ROWS], F32, kind="Internal").ap()

        WU = ctx.enter_context(nc.sbuf_tensor("WU", [P, TILES3, 2, UNIT], F32R))
        AW = ctx.enter_context(nc.sbuf_tensor("AW", [P, 2, KT, 1024], F32R))
        RT = sb("RT", 9216, F32R)
        G = sb("G", 11392)
        wraw = sb("wraw", UNIT)
        small = sb("small", 704)
        ident = sb("ident", P)
        nb = sb("nb", 2 * S)
        lnt = sb("lnt", 2 * D0)
        ropet = sb("ropet", 2 * 16)
        routh = sb("routh", KT * GATES, F32R)
        routl = sb("routl", KT * GATES, F32R)
        ps = ctx.enter_context(nc.psum_tensor("ps", [P, NBANK, 512], F32))

        xt_in_a = cut(G, 0, [2, E])
        xr_a = cut(G, 512, [2, E])
        xo_a = cut(G, 1024, [2, E])
        ctx_a = cut(G, 1536, [2, E])
        OT = G[:, 2048:4096]
        VP = G[:, 4096:4736]
        WORK = G[:, 4736:11392]
        QT = cut(RT, 0, [8, S])
        KTT = cut(RT, 2048, [8, S])
        QS = RT[:, 4096:6144]
        KS = RT[:, 6144:8192]
        XT_a = [cut(RT, 8192 + 512 * h, [KT, S]) for h in range(2)]
        spare = WU[:, TILES3 - 1].rearrange("p a n -> p (a n)")
        CT_a = [spare[:, 512 * h:512 * (h + 1)].rearrange("p (k t) -> p k t", k=KT) for h in range(2)]
        xt_in_f = cut(G, 0, [4, E])
        xr_f = cut(G, 1024, [4, E])
        xo_f = cut(G, 2048, [4, E])
        sg = cut(G, 3072, [2, 512])
        tt = cut(G, 4096, [3, 512])
        hf = cut(G, 5632, [3, 512])
        lgT = G[0:GATES, 7168:7680]
        sel_raw = G[0:2 * GATES, 7680:7680 + TILES3 * P]
        router_raw = G[:, 9856:9856 + KT * GATES]
        XT_f = [cut(RT, 1024 * h, [KT, 512]) for h in range(2)]
        HT = cut(RT, 2048, [3, 2, 512])

        stats = cut(small, 0, [4, 6])
        mv = cut(small, 32, [4, 2])
        rstd = cut(small, 48, [4])
        minus_half = small[:, 56:120]
        hsum = small[:, 120:184]
        hvar = small[:, 184:248]
        hrs = small[:, 248:312]
        mneg = small[:, 312:316]
        eps_col = small[:, 316:317]
        rden = small[:, 640:704]
        lg = cut(small, 352, [4, GATES])
        top = cut(small, 392, [4, 8])
        pick = cut(small, 424, [4, 8])
        ex = cut(small, 460, [4, GATES])
        cw = cut(small, 500, [4, GATES])
        cs2 = cut(small, 540, [4, 2 * GATES])
        den = cut(small, 616, [4])

        iterations = {0: 8, 1: 4, 2: 8, 3: 4}
        x_in = {0: x, 1: x1, 2: x2, 3: x3}
        x_out = {0: x1, 1: x2, 2: x3, 3: out}

        def U(p):
            return WORK[:, 768 * (p % 2):768 * (p % 2 + 1)].rearrange("p (h c) -> p h c", h=2)

        def P4(p):
            return WORK[:, 1536 + 768 * (p % 2):1536 + 768 * (p % 2 + 1)].rearrange("p (h c) -> p h c", h=2)

        def biased(h):
            return WORK[:, 512 * (h % 2):512 * (h % 2 + 1)].rearrange("p (t k) -> p t k", t=2)

        def prob(h):
            return WORK[:, 1024 + 512 * (h % 2):1024 + 512 * (h % 2 + 1)].rearrange("p (t k) -> p t k", t=2)

        def probT(h):
            return WORK[:, 2048 + 512 * (h % 8):2048 + 512 * (h % 8 + 1)].rearrange("p (t k) -> p t k", t=2)

        SELW = AW[0:2 * GATES].rearrange("p a b c -> p (a b c)")[:, 0:TILES3 * P]
        CWT = AW[0:2 * GATES].rearrange("p a b c -> p (a b c)")[:, TILES3 * P:TILES3 * P + 512]
        ROT, SQ, CEN = (WORK[:, 3072 + 1024 * n:4096 + 1024 * n] for n in range(3))
        ROT2 = SQ
        VS = {0: nb[:], 2: WORK[:, 6144:6656]}

        def v_and_one(f):
            return VP.rearrange("p (t c) -> p t c", t=2)

        B_XT, B_QK, B_V, B_CT, B_QT, B_KT = 6, (6, 7), 7, 7, 7, 6
        B_Y = 6
        C_BANKS = {0: (7, 6), 2: (7, 6, 7, 6)}

        per_phase = {}

        def sems(name, phases=range(4)):
            per_phase[name] = {f: sem(f"{name}{f}") for f in phases}
            return per_phase[name]

        xt_loaded = sems("xt_loaded")
        xr_loaded = sems("xr_loaded")
        xt_turned = sems("xt_turned")
        xt_hi = sems("xt_hi")
        xt_ready = sems("xt_ready")
        y_ready = sems("y_ready", (0, 2))
        z_done = sems("z_done", (1, 3))
        var_ready = sems("var_ready")
        eps_added = sems("eps_added")
        rstd_ready = sems("rstd_ready")
        xo_ready = sems("xo_ready")
        stored = sems("stored")
        out_step = sems("out_step")
        qk_ready = sems("qk_ready", (0, 2))
        v_ready = sems("v_ready", (0, 2))
        split_hi = sems("split_hi", (0, 2))
        split_ready = sems("split_ready", (0, 2))
        v_staged = sems("v_staged", (0, 2))
        vp_ready = sems("vp_ready", (0, 2))
        heads_turned = sems("heads_turned", (0, 2))
        heads_q = sems("heads_q", (0, 2))
        heads_k = sems("heads_k", (0, 2))
        score_ready = sems("score_ready", (0, 2))
        o_copied = sems("o_copied", (0, 2))
        c_turned = sems("c_turned", (0, 2))
        ctx_done = sems("ctx_done", (0, 2))
        ct_turned = sems("ct_turned", (0, 2))
        ct_hi = sems("ct_hi", (0, 2))
        ct_ready = sems("ct_ready", (0, 2))
        gate_ready = sems("gate_ready", (1, 3))
        up_ready = sems("up_ready", (1, 3))
        silu_ready = sems("silu_ready", (1, 3))
        prod_ready = sems("prod_ready", (1, 3))
        hid_hi = sems("hid_hi", (1, 3))
        hid_ready = sems("hid_ready", (1, 3))
        down_done = sems("down_done", (1, 3))
        names = ("in_step route_step rope_added cen_squared head_std squared masked quartic_even quartic_odd mixed0 biased_ready prob_ready probT_turned "
                 "probT_odd probT_even mixed2 wcol_ready prod_u lgT_turned lgT_ready lg_turned lg_ready ex_ready cw_ready "
                 "cwT_turned cwT_ready ident_ready half_ready consts aw0_raw aw0_hi aw0_ready phase_done vp_ones "
                 "rel_loaded rel_mean rel_neg diag_row diag_ready diag_stored skewed flip_zero flip_ready bias_turned "
                 "bias_ready rsel_loaded rsel_hi rsel_ready raw_ready raw_free split_w_hi split_w passed").split()
        (in_step, route_step, rope_added, cen_squared, head_std, squared, masked, quartic_even, quartic_odd, mixed0, biased_ready, prob_ready, probT_turned,
         probT_odd, probT_even, mixed2, wcol_ready, prod_u, lgT_turned, lgT_ready, lg_turned, lg_ready, ex_ready, cw_ready,
         cwT_turned, cwT_ready, ident_ready, half_ready, consts, aw0_raw, aw0_hi, aw0_ready, phase_done, vp_ones,
         rel_loaded, rel_mean, rel_neg, diag_row, diag_ready, diag_stored, skewed, flip_zero, flip_ready, bias_turned,
         bias_ready, rsel_loaded, rsel_hi, rsel_ready, raw_ready, raw_free, split_w_hi, split_w, passed) = (
            sem(n) for n in names)

        PIECES = 4
        PARTS = {0: 0, 1: PIECES * TILES1, 2: PIECES * TILES1 + iterations[1]}
        LOADS = {0: 0, 1: TILES1, 2: TILES1 + iterations[1]}
        IN_STEPS = 13
        ROUTE_STEPS = 10
        OUT_STEPS = {0: 4, 1: 3, 2: 6, 3: 3}

        def taken(eng, i, h):
            if h % 2:
                eng.wait_ge(probT_odd, H2 // 2 * i + (h + 1) // 2)
            else:
                eng.wait_ge(probT_even, H2 // 2 * i + h // 2 + 1)

        blk = ctx.enter_context(nc.Block())

        def apart(eng):
            eng.sem_inc(passed, 1)

        def passes(eng, n, body):
            body(0, True, 2)
            with eng.Fori(1, n - 2) as i:
                body(i, False, 2)
            body(n - 2, False, 1)
            body(n - 1, False, 0)

        def leave(eng):
            eng.drain().then_inc(phase_done, 1)

        def product3(pe, o, lh, ll, rh, rl, start, stop):
            pe.matmul(o, lh, rh, start=start, stop=False, skip_group_check=True)
            pe.matmul(o, lh, rl, start=False, stop=False, skip_group_check=True)
            return pe.matmul(o, ll, rh, start=False, stop=stop, skip_group_check=True)

        @blk.sync
        def _(sp):
            def rows(ap, i, nt):
                return ap[bass.ts(i, nt * P), :].rearrange("(t p) e -> p t e", p=P)

            sp.dma_start(WORK[:, 0:2048], aw0.rearrange("p k n -> p (k n)")).then_inc(aw0_raw, 16)
            sp.dma_start(ropet[:], rope.rearrange("p a b -> p (a b)")).then_inc(consts, 16)
            sp.dma_start(lnt[:], ln.rearrange("p a b -> p (a b)")).then_inc(consts, 16)
            sp.sem_inc(raw_free, 1)
            for f in range(4):
                nt = 2 if f in (0, 2) else 4
                n = iterations[f]
                x_turned_in = xt_in_a if nt == 2 else xt_in_f
                x_added = xr_a if nt == 2 else xr_f
                normed = xo_a if nt == 2 else xo_f
                turns = 1 if nt == 2 else KT
                if f:
                    sp.wait_ge(phase_done, 4 * f)
                    sp.wait_ge(stored[f - 1], 16 * iterations[f - 1] + 16)
                if f == 3:
                    sp.dma_start(router_raw, router.rearrange("p k n -> p (k n)")).then_inc(rsel_loaded, 16)
                    sp.dma_start(sel_raw, sel).then_inc(rsel_loaded, 16)
                sp.dma_start(x_turned_in, rows(x_in[f], 0, nt)).then_inc(xt_loaded[f], 16)
                sp.dma_start(x_added, rows(x_in[f], 0, nt)).then_inc(xr_loaded[f], 16)
                sp.sem_inc(stored[f], 16)
                if f == 2:
                    sp.dma_start(small[0:TABLE, 0:D2], rel).then_inc(rel_loaded, 16)
                    sp.wait_ge(diag_ready, 1)
                    sp.dma_start(ediag, WORK[0:1, 0:ROWS]).then_inc(diag_stored, 16)
                    sp.wait_ge(diag_stored, 16)
                    for t in range(2):
                        skew = bass.AP(ediag.tensor, S - P * (t + 1), [[1, P], [1, S]])
                        sp.dma_start(WORK[:, 512 + S * t:512 + S * (t + 1)], skew).then_inc(skewed, 16)
                if nt == 2:
                    sp.wait_ge(xt_turned[f], 1)
                    sp.dma_start(x_turned_in, rows(x_in[f], 1, nt)).then_inc(xt_loaded[f], 16)

                def weights(i):
                    if f == 0:
                        sp.wait_ge(raw_free, i + 1)
                        apart(sp)
                        sp.dma_start(wraw[:], wu1[bass.ts(i, 1), :, :].rearrange("a p n -> p (a n)")).then_inc(raw_ready, 16)
                    if f == 1:
                        sp.wait_ge(raw_free, LOADS[1] + i + 1)
                        apart(sp)
                        sp.dma_start(wraw[:, 0:512], aw2[:, bass.ts(i, 512)]).then_inc(raw_ready, 16)
                    if f == 2:
                        for k in range(2):
                            sp.wait_ge(raw_free, LOADS[2] + 2 * i + k + 1)
                            apart(sp)
                            sp.dma_start(wraw[:], wu3[bass.ts(2 * i + k, 1), :, :].rearrange("a p n -> p (a n)")
                                         ).then_inc(raw_ready, 16)

                def turn_next(i):
                    ahead = i + 2 if nt == 2 else i + 1
                    sp.wait_ge(xt_turned[f], turns * ahead)
                    apart(sp)
                    sp.dma_start(x_turned_in, rows(x_in[f], ahead, nt)).then_inc(xt_loaded[f], 16)

                def store(i):
                    sp.wait_ge(xo_ready[f], i + 1)
                    apart(sp)
                    sp.dma_start(rows(x_out[f], i, nt), normed).then_inc(stored[f], 16)

                def add_next(i):
                    sp.dma_start(x_added, rows(x_in[f], i, nt)).then_inc(xr_loaded[f], 16)

                turn_next(0)
                weights(0)
                with sp.Fori(1, n - 2 if nt == 2 else n - 1) as i:
                    turn_next(i)
                    weights(i)
                    store(i - 1)
                    add_next(i)
                for i in (range(n - 2, n) if nt == 2 else range(n - 1, n)):
                    weights(i)
                    store(i - 1)
                    add_next(i)
                if f == 2:
                    sp.wait_ge(raw_free, LOADS[2] + TILES3)
                    sp.dma_start(wraw[:], wu3[TILES3 - 1]).then_inc(raw_ready, 16)
                store(n - 1)
            sp.wait_ge(stored[3], 16 * iterations[3] + 16)

        @blk.tensor
        def _(pe):
            pe.wait_ge(ident_ready, 2)

            def x_turn(f, b):
                pe.wait_ge(xt_loaded[f], 16 * b + 16)
                for k in range(KT):
                    for t in range(2):
                        m = pe.transpose(ps[:, B_XT, S * k + P * t:S * k + P * (t + 1)],
                                         xt_in_a[:, t, P * k:P * (k + 1)], ident[:])
                m.then_inc(xt_turned[f], 1)

            def qk(f, b, t):
                tok = slice(P * t, P * (t + 1))
                for k in range(KT):
                    m = product3(pe, ps[:, B_QK[t], :], XT_a[0][:, k, tok], XT_a[1][:, k, tok],
                                 AW[:, 0, k, 0:512], AW[:, 1, k, 0:512], k == 0, k == KT - 1)
                m.then_inc(qk_ready[f], 1)

            def v(f, b):
                for t in range(2):
                    tok = slice(P * t, P * (t + 1))
                    for k in range(KT):
                        m = product3(pe, ps[:, B_V, S * t:S * (t + 1)], XT_a[0][:, k, tok], XT_a[1][:, k, tok],
                                     AW[:, 0, k, 512:768], AW[:, 1, k, 512:768], k == 0, k == KT - 1)
                m.then_inc(v_ready[f], 1)

            def heads_out(f, b, n):
                pe.wait_ge(heads_q[f], 4 * b + n)
                pe.wait_ge(heads_k[f], 4 * b + n)

            def heads(f, b, n):
                for src, bank in ((QS, B_QT), (KS, B_KT)):
                    w = src.bitcast(F32).rearrange("p (t g c) -> p t g c", t=2, g=8)
                    for g in range(2):
                        for t in range(2):
                            m = pe.transpose(ps[:, bank, S * g + P * t:S * g + P * (t + 1)],
                                             w[:, t, 2 * n + g, :], ident[:])
                    m.then_inc(heads_turned[f], 1)

            def c_turn(f, b, n, groups):
                if n == 0:
                    pe.wait_ge(o_copied[f], groups // 2 * (b + 1))
                if n >= 2:
                    pe.wait_ge(ctx_done[f], len(C_BANKS[f]) * b + n - 1)
                ot = OT[:, 0:groups * S].rearrange("p (g q) -> p g q", g=groups)
                t, c = divmod(n, len(C_BANKS[f]) // 2)
                for g in range(4):
                    m = pe.transpose(ps[:, C_BANKS[f][n], P * g:P * (g + 1)], ot[:, 4 * c + g, P * t:P * (t + 1)], ident[:])
                m.then_inc(c_turned[f], 1)

            def ct_turn(f, b):
                pe.wait_ge(ctx_done[f], len(C_BANKS[f]) * (b + 1))
                for k in range(KT):
                    for t in range(2):
                        m = pe.transpose(ps[:, B_CT, S * k + P * t:S * k + P * (t + 1)],
                                         ctx_a[:, t, P * k:P * (k + 1)], ident[:])
                m.then_inc(ct_turned[f], 1)

            def project(f, b):
                pe.wait_ge(ct_ready[f], b + 1)
                for t in range(2):
                    tok = slice(P * t, P * (t + 1))
                    for k in range(KT):
                        m = product3(pe, ps[:, B_Y, E * t:E * (t + 1)], CT_a[0][:, k, tok], CT_a[1][:, k, tok],
                                     AW[:, 0, k, 768:1024], AW[:, 1, k, 768:1024], k == 0, k == KT - 1)
                m.then_inc(y_ready[f], 1)

            vp = v_and_one(0)

            def phase0():
                pe.wait_ge(aw0_ready, 1)
                pe.wait_ge(vp_ones, 1)
                n = iterations[0]

                def scores(i, p, first):
                    if p % 2 == 0:
                        heads_out(0, i, p // 2 + 1)
                    if p >= 2 or not first:
                        pe.wait_ge(squared, H0 // 2 * i + p - 1)
                    for h in (2 * p, 2 * p + 1):
                        r = slice(64 * (h % 2), 64 * (h % 2) + 64)
                        b = 2 * (p % 2) + h % 2
                        pe.matmul(ps[:, b, 0:S], KTT[r, h // 2, 0:P], QT[r, h // 2, :], start=True, stop=True)
                        m = pe.matmul(ps[:, b, S:S + P], KTT[r, h // 2, P:S], QT[r, h // 2, P:S], start=True, stop=True)
                    m.then_inc(score_ready[0], 1)

                def mix(i, quad):
                    if quad == 0:
                        pe.wait_ge(vp_ready[0], i + 1)
                    pe.wait_ge(quartic_even, H0 // 4 * i + quad + 1)
                    pe.wait_ge(quartic_odd, H0 // 4 * i + quad + 1)
                    for kt in range(2):
                        for j in range(4):
                            pv = P4(2 * quad + j // 2)[:, j % 2, :]
                            cols = slice(S * (quad % 2) + P * kt, S * (quad % 2) + S)
                            at = (D0 + 1) * (4 * quad + j)
                            m = pe.matmul(ps[32 * j:32 * j + 32, 4 + quad // 2, cols], vp[:, kt, at:at + 32],
                                          pv[:, 0:S] if kt == 0 else pv[:, S:S + P],
                                          start=kt == 0, stop=kt == 1, skip_group_check=True,
                                          tile_position=(0, 32 * j))
                    m.then_inc(mixed0, 1)

                def one(i, first, left):
                    for p in range(H0 // 2):
                        scores(i, p, first)
                        if p % 2 and (p > 1 or not first):
                            mix(i if p > 1 else i - 1, (p // 2 - 1) % 4)
                        if p == 1:
                            if left:
                                pe.wait_ge(in_step, IN_STEPS * (i + 1) + 6)
                            else:
                                heads_out(0, i, 3)
                            heads(0, i, 3)
                        if p == 2 and not first:
                            heads_out(0, i, 4)
                            for c in range(2):
                                c_turn(0, i - 1, c, 4)
                        if p == 3 and not first:
                            ct_turn(0, i - 1)
                        if p == 4:
                            if first:
                                heads_out(0, i, 4)
                            else:
                                project(0, i - 1)
                            if left:
                                v(0, i + 1)
                        if p == 5 and left:
                            pe.wait_ge(v_staged[0], i + 2)
                            if not first:
                                pe.wait_ge(out_step[0], OUT_STEPS[0] * (i - 1) + 3)
                            pe.wait_ge(split_ready[0], 4 * (i + 1) + 4)
                            heads(0, i + 1, 0)
                            if left > 1:
                                pe.wait_ge(heads_k[0], 4 * (i + 1) + 1)
                                x_turn(0, i + 2)
                        if p == 6 and left:
                            heads_out(0, i + 1, 1)
                            if left > 1:
                                pe.wait_ge(xt_ready[0], i + 3)
                            heads(0, i + 1, 1)
                        if p == 7 and left:
                            heads_out(0, i + 1, 2)
                            heads(0, i + 1, 2)
                            if left > 1:
                                heads_out(0, i + 1, 3)
                                for t in range(2):
                                    qk(0, i + 2, t)

                x_turn(0, 0)
                pe.wait_ge(xt_ready[0], 1)
                for t in range(2):
                    qk(0, 0, t)
                pe.wait_ge(in_step, 6)
                v(0, 0)
                pe.wait_ge(v_staged[0], 1)
                x_turn(0, 1)
                pe.wait_ge(xt_ready[0], 2)
                pe.wait_ge(split_ready[0], 4)
                for q in range(3):
                    if q:
                        heads_out(0, 0, q)
                    heads(0, 0, q)
                heads_out(0, 0, 3)
                for t in range(2):
                    qk(0, 1, t)
                passes(pe, n, one)
                mix(n - 1, H0 // 4 - 1)
                for c in range(2):
                    c_turn(0, n - 1, c, 4)
                ct_turn(0, n - 1)
                project(0, n - 1)
                leave(pe)

            def phase2():
                pe.wait_ge(rel_neg, 1)
                pe.matmul(ps[0:1, 0, 0:TABLE], small[0:TABLE, 16:17], ident[0:TABLE, 0:TABLE],
                          start=True, stop=True).then_inc(diag_row, 1)
                pe.wait_ge(skewed, 32)
                pe.wait_ge(flip_ready, 1)
                pe.matmul(ps[:, 1, :], WORK[:, 1024:1024 + P], WORK[:, 512:1024], start=True, stop=True
                          ).then_inc(bias_turned, 1)
                pe.wait_ge(split_w, PARTS[2])
                pe.wait_ge(vp_ones, 2)
                pe.wait_ge(bias_ready, 1)

                n = iterations[2]

                def scores(i, h, first):
                    j, g = h % 4, h // 4
                    r = slice(32 * j, 32 * j + 32)
                    if h % 8 == 0:
                        heads_out(2, i, h // 8 + 1)
                    if h >= 2 or not first:
                        pe.wait_ge(biased_ready, H2 * i + h - 1)
                    for t in range(2):
                        m = pe.matmul(ps[:, h % 2, S * t:S * (t + 1)], QT[r, g, P * t:P * (t + 1)], KTT[r, g, :],
                                      start=True, stop=True, tile_position=(32 * j, 0))
                    m.then_inc(score_ready[2], 1)

                def turn(i, h, first):
                    pe.wait_ge(prob_ready, H2 * i + h + 1)
                    if h >= 2 or not first:
                        taken(pe, i, h - 2)
                    for kt in range(2):
                        for t in range(2):
                            m = pe.transpose(ps[:, 2 + h % 2, S * kt + P * t:S * kt + P * (t + 1)],
                                             prob(h)[:, t, P * kt:P * (kt + 1)], ident[:])
                    m.then_inc(probT_turned, 1)

                def mix(i, quad, first):
                    if quad == 0:
                        pe.wait_ge(vp_ready[2], i + 1)
                    if quad % 2 == 0 and (quad >= 4 or not first):
                        pe.wait_ge(o_copied[2], 4 * i + quad // 2 - 1)
                    taken(pe, i, 4 * quad + 2)
                    taken(pe, i, 4 * quad + 3)
                    for kt in range(2):
                        for j in range(4):
                            h = 4 * quad + j
                            at = (D2 + 1) * h
                            m = pe.matmul(ps[32 * j:32 * j + 32, 4 + quad // 2 % 2, S * (quad % 2):S * (quad % 2 + 1)],
                                          vp[:, kt, at:at + 32], probT(h)[:, kt, :], start=kt == 0, stop=kt == 1,
                                          skip_group_check=True, tile_position=(0, 32 * j))
                    m.then_inc(mixed2, 1)

                def one(i, first, left):
                    for h in range(H2):
                        scores(i, h, first)
                        if h >= 2 or not first:
                            turn(i, h - 2, first)
                        if h % 4 == 3 and (h > 3 or not first):
                            mix(i if h > 3 else i - 1, (h - 7) // 4 % 8, first)
                        if h == 1:
                            pe.wait_ge(v_staged[2], i + 1)
                            heads_out(2, i, 3)
                            heads(2, i, 3)
                        if h == 5:
                            heads_out(2, i, 4)
                            if left:
                                x_turn(2, i + 1)
                        if not first:
                            if h == 8:
                                c_turn(2, i - 1, 0, 8)
                            if h == 10:
                                if left:
                                    pe.wait_ge(xt_ready[2], i + 2)
                                c_turn(2, i - 1, 1, 8)
                            if h in (12, 13):
                                c_turn(2, i - 1, h - 10, 8)
                            if h == 16:
                                ct_turn(2, i - 1)
                        if h == 17 and left:
                            pe.wait_ge(xt_ready[2], i + 2)
                            qk(2, i + 1, 0)
                        if h == 20 and not first:
                            if left:
                                pe.wait_ge(split_ready[2], 4 * (i + 1) + 2)
                            project(2, i - 1)
                        if left:
                            if h == 21:
                                qk(2, i + 1, 1)
                            if h == 25:
                                pe.wait_ge(split_ready[2], 4 * (i + 1) + 4)
                                v(2, i + 1)
                            if h == 27:
                                pe.wait_ge(v_staged[2], i + 2)
                                if not first:
                                    pe.wait_ge(out_step[2], OUT_STEPS[2] * (i - 1) + 5)
                                heads(2, i + 1, 0)
                            if h in (29, 31):
                                heads_out(2, i + 1, (h - 27) // 2)
                                heads(2, i + 1, (h - 27) // 2)

                x_turn(2, 0)
                pe.wait_ge(xt_ready[2], 1)
                for t in range(2):
                    qk(2, 0, t)
                pe.wait_ge(split_ready[2], 4)
                v(2, 0)
                pe.wait_ge(v_staged[2], 1)
                for q in range(3):
                    if q:
                        heads_out(2, 0, q)
                    heads(2, 0, q)
                passes(pe, n, one)
                for h in (H2 - 2, H2 - 1):
                    turn(n - 1, h, False)
                mix(n - 1, H2 // 4 - 1, False)
                for c in range(4):
                    c_turn(2, n - 1, c, 8)
                ct_turn(2, n - 1)
                project(2, n - 1)
                leave(pe)

            def feed_forward(f, tiles):
                def gate_up(i, j):
                    if j >= 2:
                        pe.wait_ge(prod_ready[f], tiles * i + j - 1)
                    for n, ready in enumerate((gate_ready[f], up_ready[f])):
                        for k in range(KT):
                            c = slice((n * KT + k) * P, (n * KT + k + 1) * P)
                            m = product3(pe, ps[:, 2 + 2 * (j % 2) + n, :], WU[:, j, 0, c], WU[:, j, 1, c],
                                         XT_f[0][:, k, :], XT_f[1][:, k, :], k == 0, k == KT - 1)
                        m.then_inc(ready, 1)
                    if f == 3:
                        if j == 0:
                            logits_turned(i)
                        if j == 1:
                            router_columns(i)
                            spread(j - 1)
                        if j >= 1:
                            spread(j)

                def spread(j):
                    pe.matmul(ps[:, 7 - j % 2, :], SELW[:, P * j:P * (j + 1)], CWT, start=True, stop=True
                              ).then_inc(wcol_ready, 1)

                def down(i, j):
                    pe.wait_ge(hid_ready[f], tiles * i + j + 1)
                    if j == 0:
                        pe.wait_ge(z_done[f], i + 1)
                    hh, hl = HT[:, j % 3, 0, :], HT[:, j % 3, 1, :]
                    wd = [WU[:, j, h, 2 * KT * P:UNIT] for h in range(2)]
                    for t in range(4):
                        tok = slice(P * t, P * (t + 1))
                        m = product3(pe, ps[:, t // 2, E * (t % 2):E * (t % 2 + 1)], hh[:, tok], hl[:, tok],
                                     wd[0], wd[1], j == 0 and t % 2 == 0, j == tiles - 1)
                    m.then_inc(down_done[f], 1)

                def router_logits(i):
                    n = 0
                    for k in range(KT):
                        for a in (routh, routl):
                            for b in XT_f:
                                m = pe.matmul(ps[0:GATES, 6, :], a[:, GATES * k:GATES * (k + 1)], b[:, k, :],
                                              start=n == 0, stop=n == 4 * KT - 1, skip_group_check=True)
                                n += 1
                    m.then_inc(lgT_turned, 1)

                def logits_turned(i):
                    pe.wait_ge(lgT_ready, i + 1)
                    apart(pe)
                    for t in range(4):
                        m = pe.transpose(ps[:, 7, GATES * t:GATES * (t + 1)], lgT[:, P * t:P * (t + 1)],
                                         ident[0:GATES, 0:GATES])
                    m.then_inc(lg_turned, 1)

                def router_columns(i):
                    pe.wait_ge(cw_ready, i + 1)
                    for t in range(4):
                        m = pe.transpose(ps[0:2 * GATES, 6, P * t:P * (t + 1)], cs2[:, t, :], ident[:])
                    m.then_inc(cwT_turned, 1)
                    pe.wait_ge(cwT_ready, i + 1)

                def x_turn(b, k):
                    if k == 0:
                        pe.wait_ge(xt_loaded[f], 16 * b + 16)
                    for t in range(4):
                        m = pe.transpose(ps[:, 6 + k, P * t:P * (t + 1)], xt_in_f[:, t, P * k:P * (k + 1)], ident[:])
                    m.then_inc(xt_turned[f], 1)

                def one(i, last):
                    pe.wait_ge(xt_ready[f], KT * i + KT)
                    if f == 3:
                        router_logits(i)
                    gate_up(i, 0)
                    gate_up(i, 1)
                    for j in range(2, tiles):
                        if j == tiles - 1 and f == 3:
                            pe.wait_ge(split_w, PARTS[2] + TILES3)
                        gate_up(i, j)
                        down(i, j - 2)
                    for k in range(KT):
                        if not last:
                            if f == 3:
                                pe.wait_ge(prod_ready[f], tiles * i + tiles - 1 + k)
                            x_turn(i + 1, k)
                        down(i, tiles - 2 + k)

                x_turn(0, 0)
                x_turn(0, 1)
                with pe.Fori(0, iterations[f] - 1) as i:
                    one(i, False)
                one(iterations[f] - 1, True)
                leave(pe)

            phase0()
            pe.wait_ge(split_w, PARTS[1])
            feed_forward(1, TILES1)
            phase2()
            pe.wait_ge(split_w, PARTS[2] + TILES3 - 1)
            pe.wait_ge(rsel_ready, 1)
            feed_forward(3, TILES3)

        @blk.scalar
        def _(act):
            def halves(bank):
                return ps[:, bank, :].rearrange("p (k t) -> p k t", k=2)

            def x_hi(f, b):
                act.wait_ge(xt_turned[f], b + 1)
                act.copy(XT_a[0], halves(B_XT)).then_inc(xt_hi[f], 1)

            def q_heads(f, b, n):
                act.wait_ge(heads_turned[f], 8 * b + 2 * n + 1)
                act.copy(QT[:, 2 * n:2 * n + 2, :], halves(B_QT)).then_inc(heads_q[f], 1)

            def stage_v(f, b):
                act.wait_ge(v_ready[f], b + 1)
                act.copy(VS[f], ps[:, B_V, :]).then_inc(v_staged[f], 1)

            def place_v(f, b, first, h, d):
                act.wait_ge(v_staged[f], b + 1)
                if not first:
                    act.wait_ge(mixed0 if f == 0 else mixed2, h // 4 * b)
                o = v_and_one(f)[:, :, 0:h * (d + 1)].rearrange("p t (h c) -> p t h c", h=h)
                act.copy(o[:, :, :, 0:d], VS[f].rearrange("p (t h d) -> p t h d", t=2, h=h)).then_inc(vp_ready[f], 1)

            def context_hi(f, b):
                act.wait_ge(ct_turned[f], b + 1)
                act.copy(CT_a[0], halves(B_CT)).then_inc(ct_hi[f], 1)

            def phase0():
                act.wait_ge(half_ready, 2)
                act.wait_ge(aw0_raw, 16)
                act.copy(AW[:, 0], WORK[:, 0:2048].rearrange("p (k n) -> p k n", k=KT)).then_inc(aw0_hi, 1)
                n = iterations[0]

                def centred_squares(b):
                    act.wait_ge(in_step, IN_STEPS * b + 8)
                    act.square(SQ, CEN).then_inc(cen_squared, 1)

                def deviation(b):
                    act.wait_ge(in_step, IN_STEPS * b + 9)
                    act.activation(hrs, hvar, ACT.Sqrt, scale=1.0 / D0, bias=eps_col).then_inc(head_std, 1)

                def hi_parts(b):
                    act.wait_ge(in_step, IN_STEPS * b + 13)
                    n5 = SQ.rearrange("p (t w h d) -> p t w h d", t=2, w=2, h=H0)
                    for w, (dst, places) in enumerate(((QS, (0, 2)), (KS, (0, 1)))):
                        d5 = dst.rearrange("p (t h s d) -> p t h s d", t=2, h=H0, s=4)
                        for s in places:
                            act.copy(d5[:, :, :, s, :], n5[:, :, w]).then_inc(split_hi[0], 1)

                def turned_heads(b, n):
                    q_heads(0, b, n)
                    act.wait_ge(heads_turned[0], 8 * b + 2 * n + 2)
                    act.copy(KTT[:, 2 * n:2 * n + 2, :], halves(B_KT)).then_inc(heads_k[0], 1)

                def quartic(i, p, first):
                    act.wait_ge(masked, H0 // 2 * i + p + 1)
                    if p >= 2 or not first:
                        act.wait_ge(mixed0, H0 // 4 * i + p // 2)
                    act.square(P4(p), U(p)).then_inc(quartic_odd, 1)

                def outputs(b, n):
                    act.wait_ge(mixed0, H0 // 4 * b + 2 * n + 2)
                    act.copy(OT[:, 512 * n:512 * (n + 1)], ps[:, 4 + n, :]).then_inc(o_copied[0], 1)

                def one(i, first, left):
                    for p in range(H0 // 2):
                        act.wait_ge(score_ready[0], H0 // 2 * i + p + 1)
                        if p >= 2 or not first:
                            if p % 2:
                                act.wait_ge(quartic_odd, H0 // 4 * i + p // 2)
                            else:
                                act.wait_ge(quartic_even, H0 // 4 * i + p // 2)
                        b = 2 * (p % 2)
                        act.square(U(p), ps[:, b:b + 2, 0:384]).then_inc(squared, 1)
                        if p % 2 == 0 and (p or not first):
                            quartic(i, p - 1, first)
                        if p == 1 and not first:
                            outputs(i - 1, 1)
                        if p == 2:
                            turned_heads(i, 3)
                            place_v(0, i, first, H0, D0)
                            if left:
                                centred_squares(i + 1)
                        if p == 3:
                            if left:
                                deviation(i + 1)
                            if not first:
                                context_hi(0, i - 1)
                        if p == 4 and left:
                            hi_parts(i + 1)
                        if p == 5 and left:
                            stage_v(0, i + 1)
                            turned_heads(i + 1, 0)
                            if left > 1:
                                x_hi(0, i + 2)
                        if p == 6:
                            outputs(i, 0)
                            if left:
                                turned_heads(i + 1, 1)
                        if p == 7 and left:
                            turned_heads(i + 1, 2)

                x_hi(0, 0)
                stage_v(0, 0)
                x_hi(0, 1)
                centred_squares(0)
                deviation(0)
                hi_parts(0)
                for q in range(3):
                    turned_heads(0, q)
                passes(act, n, one)
                quartic(n - 1, H0 // 2 - 1, False)
                outputs(n - 1, 1)
                context_hi(0, n - 1)
                leave(act)

            def phase2():
                n = iterations[2]

                def exponential(i, h, first):
                    act.wait_ge(biased_ready, H2 * i + h + 1)
                    if h >= 2 or not first:
                        act.wait_ge(probT_turned, H2 * i + h - 1)
                    for t in range(2):
                        k = 2 * (h % 2) + t
                        m = act.activation(prob(h)[:, t, :], biased(h)[:, t, :], ACT.Exp, scale=-1.0,
                                           bias=mneg[:, k:k + 1])
                    m.then_inc(prob_ready, 1)

                def take(i, h, first):
                    act.wait_ge(probT_turned, H2 * i + h + 1)
                    if h >= 8 or not first:
                        act.wait_ge(mixed2, H2 // 4 * i + (h - 8) // 4 + 1)
                    act.copy(probT(h), halves(2 + h % 2)).then_inc(probT_odd, 1)

                def hi_parts(b, t):
                    act.wait_ge(qk_ready[2], 2 * b + t + 1)
                    src = ps[:, B_QK[t], :].rearrange("p (w h d) -> p w h d", w=2, h=H2)
                    for w, (dst, places) in enumerate(((QS, (0, 2)), (KS, (0, 1)))):
                        d5 = dst.rearrange("p (t h s d) -> p t h s d", t=2, h=H2, s=4)
                        for s in places:
                            act.mul(d5[:, t, :, s, :], src[:, w], QSCALE if w == 0 else 1.0).then_inc(split_hi[2], 1)

                def one(i, first, left):
                    for h in range(H2):
                        exponential(i, h, first)
                        if h % 2 and (h > 2 or not first):
                            take(i, h - 2, first)
                        if h == 2:
                            q_heads(2, i, 3)
                        if h == 5:
                            place_v(2, i, first, H2, D2)
                        if h == 6 and left:
                            x_hi(2, i + 1)
                        if h == 17 and not first:
                            context_hi(2, i - 1)
                        if left:
                            if h in (18, 22):
                                hi_parts(i + 1, (h - 18) // 4)
                            if h == 26:
                                stage_v(2, i + 1)
                            if h in (28, 30, 31):
                                q_heads(2, i + 1, (h - 27) // 2 if h < 31 else 2)

                x_hi(2, 0)
                for t in range(2):
                    hi_parts(0, t)
                stage_v(2, 0)
                for q in range(3):
                    q_heads(2, 0, q)
                passes(act, n, one)
                take(n - 1, H2 - 1, False)
                context_hi(2, n - 1)
                leave(act)

            def feed_forward(f, tiles):
                if f == 3:
                    act.wait_ge(rsel_loaded, 32)
                    act.copy(SELW, sel_raw)
                    act.copy(routh[:], router_raw).then_inc(rsel_hi, 1)

                def x_hi(b, k):
                    act.wait_ge(xt_turned[f], KT * b + k + 1)
                    act.copy(XT_f[0][:, k, :], ps[:, 6 + k, :]).then_inc(xt_hi[f], 1)

                def one(i, last):
                    if f == 3:
                        act.wait_ge(lgT_turned, i + 1)
                        act.copy(lgT, ps[0:GATES, 6, :]).then_inc(lgT_ready, 1)
                        act.wait_ge(lg_ready, i + 1)
                        act.activation(ex, lg, ACT.Exp).then_inc(ex_ready, 1)

                    def silu(j):
                        act.wait_ge(gate_ready[f], tiles * i + j + 1)
                        act.activation(sg[:, j % 2, :], ps[:, 2 + 2 * (j % 2), :], ACT.Silu).then_inc(silu_ready[f], 1)

                    def hidden_hi(j):
                        act.wait_ge(prod_ready[f], tiles * i + j + 1)
                        if j >= 3:
                            act.wait_ge(down_done[f], tiles * i + j - 2)
                        act.copy(HT[:, j % 3, 0, :], hf[:, j % 3, :]).then_inc(hid_hi[f], 1)

                    silu(0)
                    if f == 3:
                        act.wait_ge(cwT_turned, i + 1)
                        act.copy(CWT, ps[0:2 * GATES, 6, :]).then_inc(cwT_ready, 1)
                    for j in range(1, tiles):
                        silu(j)
                        hidden_hi(j - 1)
                    hidden_hi(tiles - 1)
                    if not last:
                        x_hi(i + 1, 0)
                        x_hi(i + 1, 1)

                x_hi(0, 0)
                x_hi(0, 1)
                with act.Fori(0, iterations[f] - 1) as i:
                    one(i, False)
                one(iterations[f] - 1, True)
                leave(act)

            phase0()
            feed_forward(1, TILES1)
            phase2()
            feed_forward(3, TILES3)

        @blk.vector
        def _(dve):
            def halves(bank):
                return ps[:, bank, :].rearrange("p (k t) -> p k t", k=2)

            def step(count, value, m, alone=False):
                m.then_inc(count, 1)
                dve.wait_ge(count, value)
                if alone:
                    apart(dve)

            def add(f, b, nt, xr, banks):
                n = OUT_STEPS[f] * b + OUT_STEPS[f] - 1 - len(banks)
                dve.wait_ge(xr_loaded[f], 16 * b + 16)
                for k, bank in enumerate(banks):
                    m = dve.tensor_tensor(xr[:, 2 * k:2 * k + 2, :], halves(bank), xr[:, 2 * k:2 * k + 2, :], ALU.add)
                    step(out_step[f], n + k + 1, m)
                if f in (1, 3):
                    dve.sem_inc(z_done[f], 1)
                for t in range(nt):
                    m = dve.bn_stats(stats[:, t, :], xr[:, t, :])
                step(out_step[f], n + len(banks) + 1, m, alone=True)
                for t in range(nt):
                    m = dve.bn_aggr(mv[:, t, :], stats[:, t, :])
                m.then_inc(var_ready[f], 1)

            def norm(f, b, nt, xr, xo):
                dve.wait_ge(rstd_ready[f], b + 1)
                dve.wait_ge(stored[f], 16 * b + 16)
                for t in range(nt):
                    m = dve.tensor_scalar(xo[:, t, :], xr[:, t, :], mv[:, t, 0:1], rstd[:, t:t + 1], ALU.subtract, ALU.mult)
                m.then_inc(xo_ready[f], 1)

            def x_lo(f, b):
                dve.wait_ge(xt_hi[f], b + 1)
                dve.tensor_tensor(XT_a[1], halves(B_XT), XT_a[0].bitcast(F32), ALU.subtract).then_inc(xt_ready[f], 1)

            def context(f, b, n, d):
                nb = len(C_BANKS[f])
                dve.wait_ge(c_turned[f], nb * b + n + 1)
                v = ps[:, C_BANKS[f][n], :].rearrange("p (h c) -> p h c", c=32)
                r = rden[:, 16 * n:16 * (n + 1)].unsqueeze(2)
                step(out_step[f], OUT_STEPS[f] * b + n + 1, dve.reciprocal(r, v[:, :, d:d + 1]))
                t, part = divmod(n, nb // 2)
                o = ctx_a[:, t, 16 * d * part:16 * d * (part + 1)].rearrange("p (h c) -> p h c", h=16)
                dve.tensor_tensor(o, v[:, :, 0:d], r.to_broadcast([P, 16, d]), ALU.mult).then_inc(ctx_done[f], 1)

            def context_lo(f, b):
                dve.wait_ge(ct_hi[f], b + 1)
                dve.tensor_tensor(CT_a[1], halves(B_CT), CT_a[0].bitcast(F32), ALU.subtract).then_inc(ct_ready[f], 1)

            def phase0():
                dve.wait_ge(aw0_hi, 1)
                raw = WORK[:, 0:2048].rearrange("p (k n) -> p k n", k=KT)
                dve.tensor_tensor(AW[:, 1], raw, AW[:, 0].bitcast(F32), ALU.subtract).then_inc(aw0_ready, 1)
                dve.wait_ge(aw0_ready, 1)
                dve.wait_ge(consts, 32)
                n = iterations[0]
                rh = ROT.rearrange("p (n d) -> p n d", d=D0)
                ch = CEN.rearrange("p (n d) -> p n d", d=D0)
                sh = SQ.rearrange("p (n d) -> p n d", d=D0)
                full = [P, 4 * H0, D0]

                def rope_half(b, t):
                    r4 = ROT.rearrange("p (t h s e) -> p t h s e", t=2, s=2, e=8)
                    r24 = ROT2.rearrange("p (t h s e) -> p t h s e", t=2, s=2, e=8)
                    dve.wait_ge(qk_ready[0], 2 * b + t + 1)
                    src = ps[:, B_QK[t], :].rearrange("p (h s e) -> p h s e", s=2, e=8)
                    cos = ropet[:, 16 * t:16 * t + 8].unsqueeze(1).unsqueeze(1).to_broadcast([P, 2 * H0, 2, 8])
                    sin = ropet[:, 16 * t + 8:16 * t + 16].unsqueeze(1).to_broadcast([P, 2 * H0, 8])
                    dve.tensor_tensor(r4[:, t], src, cos, ALU.mult)
                    dve.scalar_tensor_tensor(out=r24[:, t, :, 0, :], in0=src[:, :, 1, :], scalar=-1.0, in1=sin,
                                             op0=ALU.mult, op1=ALU.mult)
                    dve.tensor_tensor(r24[:, t, :, 1, :], src[:, :, 0, :], sin, ALU.mult).then_inc(in_step, 3)

                def centre(b):
                    dve.wait_ge(rope_added, b + 1)
                    step(in_step, IN_STEPS * b + 7, dve.tensor_reduce(hsum, rh, AX_X, ALU.add))
                    step(in_step, IN_STEPS * b + 8,
                         dve.scalar_tensor_tensor(out=ch, in0=hsum.unsqueeze(2).to_broadcast(full), scalar=-1.0 / D0,
                                                  in1=rh, op0=ALU.mult, op1=ALU.add))

                def variance(b):
                    dve.wait_ge(cen_squared, b + 1)
                    dve.tensor_reduce(hvar, sh, AX_X, ALU.add).then_inc(in_step, 1)

                def scaled(b):
                    dve.wait_ge(head_std, b + 1)
                    step(in_step, IN_STEPS * b + 10, dve.reciprocal(hrs, hrs))
                    step(in_step, IN_STEPS * b + 11, dve.tensor_tensor(ch, ch, hrs.unsqueeze(2).to_broadcast(full), ALU.mult))
                    step(in_step, IN_STEPS * b + 12,
                         dve.tensor_tensor(ch, ch, lnt[:, 0:D0].unsqueeze(1).to_broadcast(full), ALU.mult))
                    step(in_step, IN_STEPS * b + 13,
                         dve.tensor_tensor(sh, ch, lnt[:, D0:2 * D0].unsqueeze(1).to_broadcast(full), ALU.add))

                def lo_parts(b):
                    n5 = SQ.rearrange("p (t w h d) -> p t w h d", t=2, w=2, h=H0)
                    for w, (dst, places) in enumerate(((QS, (1, 3)), (KS, (2, 3)))):
                        d5 = dst.rearrange("p (t h s d) -> p t h s d", t=2, h=H0, s=4)
                        dve.wait_ge(split_hi[0], 4 * b + 2 * w + 2)
                        for s in places:
                            dve.tensor_tensor(d5[:, :, :, s, :], n5[:, :, w], d5[:, :, :, 0, :].bitcast(F32), ALU.subtract
                                              ).then_inc(split_ready[0], 1)

                def quartic(i, p, first):
                    dve.wait_ge(masked, H0 // 2 * i + p + 1)
                    if p >= 2 or not first:
                        dve.wait_ge(mixed0, H0 // 4 * i + p // 2)
                    dve.tensor_tensor(P4(p), U(p), U(p), ALU.mult).then_inc(quartic_even, 1)

                def one(i, first, left):
                    if left:
                        for t in range(2):
                            rope_half(i + 1, t)
                    quartic(i, 0, first)
                    if left:
                        centre(i + 1)
                    quartic(i, 2, first)
                    if not first:
                        for c in range(2):
                            context(0, i - 1, c, D0)
                    if left:
                        variance(i + 1)
                    if not first:
                        context_lo(0, i - 1)
                    if left:
                        scaled(i + 1)
                    quartic(i, 4, first)
                    if not first:
                        dve.wait_ge(y_ready[0], i)
                        add(0, i - 1, 2, xr_a, (B_Y,))
                    if left:
                        lo_parts(i + 1)
                    if left > 1:
                        x_lo(0, i + 2)
                    if not first:
                        norm(0, i - 1, 2, xr_a, xo_a)
                    quartic(i, 6, first)

                x_lo(0, 0)
                for t in range(2):
                    rope_half(0, t)
                x_lo(0, 1)
                centre(0)
                variance(0)
                scaled(0)
                lo_parts(0)
                passes(dve, n, one)
                for c in range(2):
                    context(0, n - 1, c, D0)
                context_lo(0, n - 1)
                dve.wait_ge(y_ready[0], n)
                add(0, n - 1, 2, xr_a, (B_Y,))
                norm(0, n - 1, 2, xr_a, xo_a)
                leave(dve)

            def phase2():
                dve.wait_ge(rel_loaded, 16)
                dve.tensor_reduce(small[0:TABLE, 15:16], small[0:TABLE, 0:D2], AX_X, ALU.add).then_inc(rel_mean, 1)
                dve.wait_ge(rel_mean, 1)
                dve.tensor_scalar(small[0:TABLE, 16:17], small[0:TABLE, 15:16], -1.0 / D2, None, ALU.mult
                                  ).then_inc(rel_neg, 1)
                dve.wait_ge(diag_row, 1)
                lo = S - MAXPOS
                dve.tensor_copy(WORK[0:1, lo:lo + TABLE], ps[0:1, 0, 0:TABLE])
                dve.tensor_copy(WORK[0:1, 0:lo], ps[0:1, 0, 0:1].to_broadcast([1, lo]))
                dve.tensor_copy(WORK[0:1, lo + TABLE:ROWS], ps[0:1, 0, TABLE - 1:TABLE].to_broadcast([1, ROWS - lo - TABLE])
                                ).then_inc(diag_ready, 1)
                dve.wait_ge(bias_turned, 1)
                dve.tensor_copy(nb[:], ps[:, 1, :]).then_inc(bias_ready, 1)
                dve.wait_ge(bias_ready, 1)
                nbv = nb[:].rearrange("p (t k) -> p t k", t=2)
                n = iterations[2]

                def lo_parts(b, t):
                    src = ps[:, B_QK[t], :].rearrange("p (w h d) -> p w h d", w=2, h=H2)
                    dve.wait_ge(split_hi[2], 8 * b + 4 * t + 4)
                    for w, (dst, places) in enumerate(((QS, (1, 3)), (KS, (2, 3)))):
                        d5 = dst.rearrange("p (t h s d) -> p t h s d", t=2, h=H2, s=4)
                        for s in places:
                            m = dve.scalar_tensor_tensor(out=d5[:, t, :, s, :], in0=src[:, w],
                                                         scalar=QSCALE if w == 0 else 1.0,
                                                         in1=d5[:, t, :, 0, :].bitcast(F32), op0=ALU.mult, op1=ALU.subtract)
                    m.then_inc(split_ready[2], 2)

                def k_heads(b, n):
                    dve.wait_ge(heads_turned[2], 8 * b + 2 * n + 2)
                    dve.tensor_copy(KTT[:, 2 * n:2 * n + 2, :], halves(B_KT)).then_inc(heads_k[2], 1)

                def least(i, h, first):
                    dve.wait_ge(score_ready[2], H2 * i + h + 1)
                    if h >= 2 or not first:
                        dve.wait_ge(prob_ready, H2 * i + h - 1)
                    apart(dve)
                    for t in range(2):
                        k = 2 * (h % 2) + t
                        m = dve.tensor_tensor_reduce(biased(h)[:, t, :], ps[:, h % 2, S * t:S * (t + 1)],
                                                     nbv[:, t, :], 1.0, -FMIN, ALU.add, ALU.min, mneg[:, k:k + 1])
                    m.then_inc(biased_ready, 1)

                def take(i, h, first):
                    dve.wait_ge(probT_turned, H2 * i + h + 1)
                    if h >= 8 or not first:
                        dve.wait_ge(mixed2, H2 // 4 * i + (h - 8) // 4 + 1)
                    dve.tensor_copy(probT(h), halves(2 + h % 2)).then_inc(probT_even, 1)

                def outputs(b, n):
                    dve.wait_ge(mixed2, H2 // 4 * b + 2 * n + 2)
                    dve.tensor_copy(OT[:, 512 * n:512 * (n + 1)], ps[:, 4 + n % 2, :]).then_inc(o_copied[2], 1)

                def one(i, first, left):
                    for h in range(H2):
                        least(i, h, first)
                        if h % 2 and (h > 2 or not first):
                            take(i, h - 3, first)
                        if h == 3:
                            k_heads(i, 3)
                        if h == 5 and not first:
                            outputs(i - 1, 3)
                        if h == 7 and left:
                            x_lo(2, i + 1)
                        if h in (13, 21, 29):
                            outputs(i, (h - 13) // 8)
                        if not first:
                            if h in (9, 11, 14, 15):
                                context(2, i - 1, (9, 11, 14, 15).index(h), D2)
                            if h == 18:
                                context_lo(2, i - 1)
                            if h == 22:
                                dve.wait_ge(y_ready[2], i)
                                add(2, i - 1, 2, xr_a, (B_Y,))
                            if h == 24:
                                norm(2, i - 1, 2, xr_a, xo_a)
                        if left:
                            if h in (19, 23):
                                lo_parts(i + 1, (h - 19) // 4)
                            if h in (28, 30, 31):
                                k_heads(i + 1, (h - 27) // 2 if h < 31 else 2)

                x_lo(2, 0)
                for t in range(2):
                    lo_parts(0, t)
                for q in range(3):
                    k_heads(0, q)
                passes(dve, n, one)
                take(n - 1, H2 - 2, False)
                outputs(n - 1, 3)
                for c in range(4):
                    context(2, n - 1, c, D2)
                context_lo(2, n - 1)
                dve.wait_ge(y_ready[2], n)
                add(2, n - 1, 2, xr_a, (B_Y,))
                norm(2, n - 1, 2, xr_a, xo_a)
                leave(dve)

            def feed_forward(f, tiles):
                if f == 3:
                    dve.wait_ge(rsel_hi, 1)
                    dve.tensor_tensor(routl[:], router_raw, routh[:].bitcast(F32), ALU.subtract).then_inc(rsel_ready, 1)
                dve.sem_inc(z_done[f], 1)

                def x_lo(b, k):
                    dve.wait_ge(xt_hi[f], KT * b + k + 1)
                    dve.tensor_tensor(XT_f[1][:, k, :], ps[:, 6 + k, :], XT_f[0][:, k, :].bitcast(F32), ALU.subtract
                                      ).then_inc(xt_ready[f], 1)

                def one(i, first, left):
                    if f == 3:
                        route(i)

                    def product(j):
                        dve.wait_ge(silu_ready[f], tiles * i + j + 1)
                        dve.wait_ge(up_ready[f], tiles * i + j + 1)
                        up, s, h = ps[:, 3 + 2 * (j % 2), :], sg[:, j % 2, :], hf[:, j % 3, :]
                        if f == 1:
                            dve.tensor_tensor(h, up, s, ALU.mult).then_inc(prod_ready[f], 1)
                        else:
                            dve.tensor_tensor(tt[:, j % 3, :], up, s, ALU.mult).then_inc(prod_u, 1)
                            dve.wait_ge(prod_u, tiles * i + j + 1)
                            dve.wait_ge(wcol_ready, tiles * i + j + 1)
                            dve.tensor_tensor(h, ps[:, 7 - j % 2, :], tt[:, j % 3, :], ALU.mult).then_inc(prod_ready[f], 1)

                    def hidden_lo(j):
                        dve.wait_ge(hid_hi[f], tiles * i + j + 1)
                        dve.tensor_tensor(HT[:, j % 3, 1, :], hf[:, j % 3, :], HT[:, j % 3, 0, :].bitcast(F32),
                                          ALU.subtract).then_inc(hid_ready[f], 1)

                    product(0)
                    if not first:
                        norm(f, i - 1, 4, xr_f, xo_f)
                    for j in range(1, tiles):
                        product(j)
                        hidden_lo(j - 1)
                    hidden_lo(tiles - 1)
                    if left:
                        x_lo(i + 1, 0)
                        x_lo(i + 1, 1)
                    dve.wait_ge(down_done[f], tiles * i + tiles)
                    add(f, i, 4, xr_f, (0, 1))

                x_lo(0, 0)
                x_lo(0, 1)
                passes(dve, iterations[f], one)
                norm(f, iterations[f] - 1, 4, xr_f, xo_f)
                leave(dve)

            def route(i):
                dve.wait_ge(lg_turned, i + 1)
                raw = ps[:, 7, 0:4 * GATES].rearrange("p (t g) -> p t g", t=4)
                step(route_step, ROUTE_STEPS * i + 1, dve.tensor_reduce(den, raw[:, :, 0:NEXP], AX_X, ALU.max))
                dve.tensor_tensor(lg[:, :, 0:NEXP], raw[:, :, 0:NEXP], den.unsqueeze(2).to_broadcast([P, 4, NEXP]), ALU.subtract)
                dve.tensor_scalar(lg[:, :, NEXP:GATES], raw[:, :, NEXP:GATES], -1.0, None, ALU.mult).then_inc(lg_ready, 1)
                dve.wait_ge(ex_ready, i + 1)
                apart(dve)
                for t in range(4):
                    m = dve.max(top[:, t, :], ex[:, t, 0:NEXP])
                step(route_step, ROUTE_STEPS * i + 2, m)
                step(route_step, ROUTE_STEPS * i + 3, dve.memset(top[:, :, 2:8], -5.0), alone=True)
                for t in range(4):
                    m = dve.match_replace(pick[:, t, :], top[:, t, :], ex[:, t, 0:NEXP], -1.0)
                step(route_step, ROUTE_STEPS * i + 4, m)
                step(route_step, ROUTE_STEPS * i + 5, dve.tensor_reduce(den, top[:, :, 0:2], AX_X, ALU.add))
                step(route_step, ROUTE_STEPS * i + 6, dve.tensor_scalar(pick, pick, 0.0, None, ALU.is_lt))
                dve.tensor_scalar(cw[:, :, NEXP:GATES], ex[:, :, NEXP:GATES], 1.0, None, ALU.add)
                dve.tensor_tensor(cw[:, :, 0:NEXP], pick, ex[:, :, 0:NEXP], ALU.mult)
                step(route_step, ROUTE_STEPS * i + 7, dve.reciprocal(den, den))
                step(route_step, ROUTE_STEPS * i + 8, dve.reciprocal(cw[:, :, NEXP:GATES], cw[:, :, NEXP:GATES]))
                step(route_step, ROUTE_STEPS * i + 9, dve.tensor_tensor(cw[:, :, 0:NEXP], cw[:, :, 0:NEXP],
                                                den.unsqueeze(2).to_broadcast([P, 4, NEXP]), ALU.mult))
                step(route_step, ROUTE_STEPS * i + 10, dve.tensor_copy(cs2[:, :, 0:GATES].bitcast(F32R), cw))
                dve.tensor_tensor(cs2[:, :, GATES:2 * GATES], cw, cs2[:, :, 0:GATES], ALU.subtract).then_inc(cw_ready, 1)

            phase0()
            feed_forward(1, TILES1)
            phase2()
            feed_forward(3, TILES3)

        @blk.gpsimd
        def _(pool):
            pool.memset(ident[:], 0.0).then_inc(ident_ready, 1)
            pool.memset(minus_half, -0.5).then_inc(half_ready, 1)
            pool.memset(eps_col, EPS).then_inc(half_ready, 1)
            pool.wait_ge(ident_ready, 1)
            pool.affine_select(out=ident[:], in_=ident[:], compare_op=ALU.not_equal, fill=1.0, base=0,
                               pattern=[[-1, P]], channel_multiplier=1).then_inc(ident_ready, 1)

            def ones():
                pool.memset(VP, 1.0).then_inc(vp_ones, 1)

            def split_hi_part(part, hi, raw):
                pool.tensor_copy(hi, raw).then_inc(split_w_hi, 1)

            def split_lo_part(part, lo, hi, raw):
                pool.wait_ge(split_w_hi, part + 1)
                pool.tensor_tensor(lo, raw, hi.bitcast(F32), ALU.subtract).then_inc(split_w, 1)

            def free_raw(parts):
                pool.wait_ge(split_w, parts)
                pool.sem_inc(raw_free, 1)

            def split(load, part, hi, lo, raw):
                pool.wait_ge(raw_ready, 16 * load + 16)
                split_hi_part(part, hi, raw)
                split_lo_part(part, lo, hi, raw)
                free_raw(part + 1)

            def unit(load, part, tile):
                wu = WU[:, bass.ts(tile, 1), :, :]
                split(load, part, wu[:, :, 0, :], wu[:, :, 1, :], wraw[:].unsqueeze(1))

            def layernorm_rstd(f, i, nt):
                pool.wait_ge(var_ready[f], i + 1)
                apart(pool)
                pool.tensor_scalar(rstd[:, 0:nt], mv[:, 0:nt, 1:2].rearrange("p t o -> p (t o)"), EPS, None, ALU.add
                                   ).then_inc(eps_added[f], 1)
                pool.wait_ge(eps_added[f], i + 1)
                pool.tensor_tensor(rstd[:, 0:nt], rstd[:, 0:nt], minus_half[:, 0:nt], ALU.pow).then_inc(rstd_ready[f], 1)

            pool.wait_ge(half_ready, 2)
            ones()
            cols = UNIT // PIECES

            def add_rope(b):
                pool.wait_ge(in_step, IN_STEPS * b + 6)
                pool.tensor_tensor(ROT, ROT, ROT2, ALU.add).then_inc(rope_added, 1)

            def one(i, first, left):
                wu = WU[:, bass.ts(i, 1), :, :]
                for p in range(H0 // 2):
                    pool.wait_ge(squared, H0 // 2 * i + p + 1)
                    apart(pool)
                    for block in (0, 2):
                        u = U(p)[:, :, P * block:P * (block + 1)]
                        m = pool.affine_select(out=u, in_=u, compare_op=ALU.is_ge, fill=0.0, base=0,
                                               pattern=[[0, 2], [1, P]], channel_multiplier=-1)
                    m.then_inc(masked, 1)
                    if p == 0 and left:
                        add_rope(i + 1)
                    if p == 5 and not first:
                        layernorm_rstd(0, i - 1, 2)
                    piece = slice(cols * (p // 2), cols * (p // 2 + 1))
                    raw, hi, lo = wraw[:, piece].unsqueeze(1), wu[:, :, 0, piece], wu[:, :, 1, piece]
                    if p == 0:
                        pool.wait_ge(raw_ready, 16 * i + 16)
                    if p % 2 == 0:
                        split_hi_part(PIECES * i + p // 2, hi, raw)
                    else:
                        split_lo_part(PIECES * i + p // 2, lo, hi, raw)
                free_raw(PIECES * (i + 1))

            add_rope(0)
            passes(pool, iterations[0], one)
            layernorm_rstd(0, iterations[0] - 1, 2)
            leave(pool)
            pool.wait_ge(phase_done, 4)
            aw = AW[:].rearrange("p a b c -> p a (b c)")
            with pool.Fori(0, iterations[1]) as i:
                part = bass.ts(i, 512)
                split(LOADS[1] + i, PARTS[1] + i, aw[:, 0, part], aw[:, 1, part], wraw[:, 0:512])
                layernorm_rstd(1, i, 4)
            leave(pool)
            pool.wait_ge(phase_done, 8)
            ones()
            flip = WORK[:, 1024:1024 + P]
            pool.memset(flip, 0.0).then_inc(flip_zero, 1)
            pool.wait_ge(flip_zero, 1)
            pool.affine_select(out=flip, in_=flip, compare_op=ALU.not_equal, fill=1.0, base=1 - P,
                               pattern=[[1, P]], channel_multiplier=1).then_inc(flip_ready, 1)
            with pool.Fori(0, iterations[2]) as i:
                for k in range(2):
                    unit(LOADS[2] + 2 * i + k, PARTS[2] + 2 * i + k, 2 * i + k)
                layernorm_rstd(2, i, 2)
            leave(pool)
            pool.wait_ge(phase_done, 12)
            unit(LOADS[2] + TILES3 - 1, PARTS[2] + TILES3 - 1, TILES3 - 1)
            with pool.Fori(0, iterations[3]) as i:
                layernorm_rstd(3, i, 4)
            leave(pool)


def kernel(**inputs):
    import numpy as np
    import concourse.bacc as bacc
    from concourse.bass_utils import run_bass_kernel_spmd

    a = {k: np.asarray(v) for k, v in inputs.items()}

    def by_partition(w):
        return np.ascontiguousarray(w.reshape(KT, P, -1).transpose(1, 0, 2))

    def units(gate, up, down, tiles):
        out = np.zeros((tiles, P, UNIT), np.float32)
        for m, w in enumerate((gate, up)):
            full = np.zeros((E, tiles * P), np.float32)
            full[:, :w.shape[1]] = w
            out[:, :, m * KT * P:(m + 1) * KT * P] = (
                full.reshape(KT, P, tiles, P).transpose(2, 1, 0, 3).reshape(tiles, P, KT * P))
        rows = np.zeros((tiles * P, E), np.float32)
        rows[:down.shape[0]] = down
        out[:, :, 2 * KT * P:] = rows.reshape(tiles, P, E)
        return out

    inv = (1.0 / np.float32(10000.0) ** (np.arange(0, D0, 2, dtype=np.float32) / np.float32(D0))).astype(np.float32)
    angle = np.arange(S, dtype=np.float32)[:, None] * inv[None, :]
    rope = np.concatenate([np.cos(angle), np.sin(angle)], axis=1).astype(np.float32)
    sel = np.zeros((2 * GATES, TILES3 * P), np.float32)
    for row in range(NEXP * IE + SI):
        g = min(row // IE, NEXP)
        sel[[g, g + GATES], row] = 1.0

    arrays = {
        "x": a["L0_attn_x"].reshape(T, E),
        "rope": np.ascontiguousarray(rope.reshape(2, P, 16).transpose(1, 0, 2)),
        "ln": np.ascontiguousarray(np.broadcast_to(np.stack([a["L0_attn_ln_scale"], a["L0_attn_ln_bias"]]), (P, 2, D0))),
        "aw0": by_partition(np.concatenate([a["L0_attn_w_qkv"], a["L0_attn_w_out"]], axis=1)),
        "wu1": units(a["L0_ffn_w_gate"].T, a["L0_ffn_w_up"].T, a["L0_ffn_w_down"].T, TILES1),
        "aw2": by_partition(np.concatenate([a["L1_attn_wq"].T, a["L1_attn_wk"].T, a["L1_attn_wv"].T,
                                            a["L1_attn_wo"].T], axis=1)).reshape(P, KT * 1024),
        "rel": a["L1_attn_rel_pos"],
        "wu3": units(np.concatenate([a["L1_ffn_w_gate"].transpose(1, 0, 2).reshape(E, -1), a["L1_ffn_sw_gate"]], axis=1),
                     np.concatenate([a["L1_ffn_w_up"].transpose(1, 0, 2).reshape(E, -1), a["L1_ffn_sw_up"]], axis=1),
                     np.concatenate([a["L1_ffn_w_down"].reshape(-1, E), a["L1_ffn_sw_down"]], axis=0), TILES3),
        "router": by_partition(np.concatenate([a["L1_ffn_router_w"].T, a["L1_ffn_shared_gate_w"][:, None]], axis=1)),
        "sel": sel,
    }
    nc = bacc.Bacc("TRN2", target_bir_lowering=False, num_devices=1)
    in_map, args = {}, []
    for name, v in arrays.items():
        v = np.ascontiguousarray(v)
        in_map[f"in_{name}"] = v
        args.append(nc.dram_tensor(f"in_{name}", v.shape, mybir.dt.from_np(v.dtype), kind="ExternalInput").ap())
    out = nc.dram_tensor("out_x", (T, E), F32, kind="ExternalOutput").ap()
    program(nc, *args, out)
    r = run_bass_kernel_spmd(nc, [in_map], core_ids=[0])
    return r.results[0]["out_x"].reshape(a["L0_attn_x"].shape)
```

```python
from contextlib import ExitStack

import concourse.bass as bass
from concourse import mybir

ALU = mybir.AluOpType
ACT = mybir.ActivationFunctionType
F32 = mybir.dt.float32
F32R = mybir.dt.float32r
AX_X = mybir.AxisListType.X

P = 128
T = 2048
E = 256
S = 256
KT = E // P
EPS = 1e-5
ROWS = 2 * S
NBANK = 8
FMIN = -3.0e38

H0, D0 = 16, 16
H2, D2 = 32, 8
MAXPOS = 64
TABLE = 2 * MAXPOS - 1
F1 = 1024
NEXP, IE, SI = 8, 176, 704
TILES1 = F1 // P
TILES3 = -(-(NEXP * IE + SI) // P)
UNIT = 2 * KT * P + E
GATES = NEXP + 1
QSCALE = -float(D2) ** -0.5


def program(nc, x, rope, ln, aw0, wu1, aw2, rel, wu3, router, sel, out):
    with ExitStack() as ctx:
        def sem(name):
            return ctx.enter_context(nc.semaphore(name))

        def sb(name, width, dt=F32):
            return ctx.enter_context(nc.sbuf_tensor(name, [P, width], dt))

        def cut(buf, at, shape, parts=P):
            n = 1
            for s in shape:
                n *= s
            v = buf[0:parts, at:at + n]
            if len(shape) == 2:
                return v.rearrange("p (a b) -> p a b", a=shape[0])
            if len(shape) == 3:
                return v.rearrange("p (a b c) -> p a b c", a=shape[0], b=shape[1])
            if len(shape) == 4:
                return v.rearrange("p (a b c d) -> p a b c d", a=shape[0], b=shape[1], c=shape[2])
            return v

        x1 = nc.dram_tensor("x1", [T, E], F32, kind="Internal").ap()
        x2 = nc.dram_tensor("x2", [T, E], F32, kind="Internal").ap()
        x3 = nc.dram_tensor("x3", [T, E], F32, kind="Internal").ap()
        ediag = nc.dram_tensor("ediag", [1, ROWS], F32, kind="Internal").ap()

        with nc.sbuf_tensor("before", [P, (TILES3 - 3) * 2 * UNIT], F32), nc.sbuf_tensor(
                "ring", [P, 4 * UNIT], F32) as ring:
            pass
        WU = ctx.enter_context(nc.sbuf_tensor("WU", [P, TILES3, 2, UNIT], F32R))
        AW = ctx.enter_context(nc.sbuf_tensor("AW", [P, 2, KT, 1024], F32R))
        RT = sb("RT", 9216, F32R)
        G = sb("G", 11392)
        wraw = sb("wraw", UNIT)
        small = sb("small", 704)
        ident = sb("ident", P)
        nb = sb("nb", 2 * S)
        lnt = sb("lnt", 2 * D0)
        ropet = sb("ropet", 2 * 16)
        routh = sb("routh", KT * GATES, F32R)
        routl = sb("routl", KT * GATES, F32R)
        ps = ctx.enter_context(nc.psum_tensor("ps", [P, NBANK, 512], F32))

        xt_in_a = cut(G, 0, [2, E])
        xr_a = cut(G, 1024, [2, E])
        xo_a = cut(G, 1536, [2, E])
        ctx_a = cut(G, 2048, [2, E])
        OT = G[:, 2560:4608]
        VP = G[:, 4608:5248]
        WORK = G[:, 5248:11392]
        QT = cut(RT, 0, [8, S])
        KTT = cut(RT, 2048, [8, S])
        QS = RT[:, 4096:6144]
        KS = RT[:, 6144:8192]
        XT_a = [cut(RT, 8192 + 512 * h, [KT, S]) for h in range(2)]
        spare = WU[:, TILES3 - 1].rearrange("p a n -> p (a n)")
        CT_a = [spare[:, 512 * h:512 * (h + 1)].rearrange("p (k t) -> p k t", k=KT) for h in range(2)]
        xt_in_f = cut(G, 0, [4, E])
        xr_f = cut(G, 1024, [4, E])
        xo_f = cut(G, 2048, [4, E])
        sg = cut(G, 3072, [2, 512])
        tt = cut(G, 4096, [3, 512])
        hf = cut(G, 5632, [3, 512])
        lgT = G[0:GATES, 7168:7680]
        sel_raw = G[0:2 * GATES, 7680:7680 + TILES3 * P]
        router_raw = G[:, 9856:9856 + KT * GATES]
        hidden = {1: WU[:, TILES1 + 1:TILES1 + 5].rearrange("p u a n -> p (u a n)"), 3: RT[:]}
        XT_f = {f: [cut(v, 1024 * h, [KT, 512]) for h in range(2)] for f, v in hidden.items()}
        HT = {f: cut(v, 2048, [3, 2, 512]) for f, v in hidden.items()}

        stats = cut(small, 0, [4, 6])
        mv = cut(small, 32, [4, 2])
        rstd = cut(small, 48, [4])
        minus_half = small[:, 56:120]
        hsum = small[:, 120:184]
        hvar = small[:, 184:248]
        hrs = small[:, 248:312]
        mneg = small[:, 312:320]
        eps_col = small[:, 320:321]
        rden = small[:, 640:704]
        lg = cut(small, 352, [4, GATES])
        top = cut(small, 392, [4, 8])
        pick = cut(small, 424, [4, 8])
        ex = cut(small, 460, [4, GATES])
        cw = cut(small, 500, [4, GATES])
        cs2 = cut(small, 540, [4, 2 * GATES])
        den = cut(small, 616, [4])

        iterations = {0: 8, 1: 4, 2: 8, 3: 4}
        x_in = {0: x, 1: x1, 2: x2, 3: x3}
        x_out = {0: x1, 1: x2, 2: x3, 3: out}

        def U(p):
            return WORK[:, 768 * (p % 2):768 * (p % 2 + 1)].rearrange("p (h c) -> p h c", h=2)

        def P4(p):
            return ring[:, 768 * (p % 4):768 * (p % 4 + 1)].rearrange("p (h c) -> p h c", h=2)

        def prob(h):
            return WORK[:, 512 * (h % 4):512 * (h % 4 + 1)].rearrange("p (t k) -> p t k", t=2)

        def probT(h):
            return WORK[:, 2048 + 512 * (h % 8):2048 + 512 * (h % 8 + 1)].rearrange("p (t k) -> p t k", t=2)

        diagonals = WORK[0:1, 2048:2048 + ROWS]
        skewed_bias = WORK[:, 2560:3072]
        flip = G[:, 2048:2048 + P]

        SELW = AW[0:2 * GATES].rearrange("p a b c -> p (a b c)")[:, 0:TILES3 * P]
        CWT = AW[0:2 * GATES].rearrange("p a b c -> p (a b c)")[:, TILES3 * P:TILES3 * P + 512]
        ROT, SQ, CEN = (WORK[:, 3072 + 1024 * n:4096 + 1024 * n] for n in range(3))
        ROT2 = SQ
        VS = G[:, 512:1024]

        def v_and_one(f):
            return VP.rearrange("p (t c) -> p t c", t=2)

        B_XT, B_V, B_QT, B_KT = 6, 7, 7, 6
        B_QK = {0: (4, 7), 2: (6, 7)}
        B_CT = {0: 5, 2: 7}
        B_Y = {0: 5, 2: 6}
        C_BANKS = {0: (5, 6), 2: (7, 6, 7, 6)}
        LAST_CT, LAST_Y, LAST_C = 0, 1, (0, 1, 0, 1)

        per_phase = {}

        def sems(name, phases=range(4)):
            per_phase[name] = {f: sem(f"{name}{f}") for f in phases}
            return per_phase[name]

        xt_loaded = sems("xt_loaded")
        xr_loaded = sems("xr_loaded")
        xt_turned = sems("xt_turned")
        xt_hi = sems("xt_hi")
        xt_ready = sems("xt_ready")
        y_ready = sems("y_ready", (0, 2))
        z_done = sems("z_done", (1, 3))
        var_ready = sems("var_ready")
        eps_added = sems("eps_added")
        rstd_ready = sems("rstd_ready")
        xo_ready = sems("xo_ready")
        stored = sems("stored")
        out_step = sems("out_step")
        qk_ready = sems("qk_ready", (0, 2))
        v_ready = sems("v_ready", (0, 2))
        split_hi = sems("split_hi", (0, 2))
        split_ready = sems("split_ready", (0, 2))
        v_staged = sems("v_staged", (0, 2))
        vp_ready = sems("vp_ready", (0, 2))
        heads_turned = sems("heads_turned", (0, 2))
        heads_q = sems("heads_q", (0, 2))
        heads_k = sems("heads_k", (0, 2))
        score_ready = sems("score_ready", (0, 2))
        o_copied = sems("o_copied", (0, 2))
        c_turned = sems("c_turned", (0, 2))
        ctx_done = sems("ctx_done", (0, 2))
        ct_turned = sems("ct_turned", (0, 2))
        ct_hi = sems("ct_hi", (0, 2))
        ct_ready = sems("ct_ready", (0, 2))
        gate_ready = sems("gate_ready", (1, 3))
        up_ready = sems("up_ready", (1, 3))
        silu_ready = sems("silu_ready", (1, 3))
        prod_ready = sems("prod_ready", (1, 3))
        hid_hi = sems("hid_hi", (1, 3))
        hid_ready = sems("hid_ready", (1, 3))
        down_done = sems("down_done", (1, 3))
        names = ("in_step route_step rope_added cen_squared head_std squared masked quartic_even quartic_odd mixed0 biased_ready prob_ready probT_turned "
                 "probT_odd probT_even mixed2 wcol_ready prod_u lgT_turned lgT_ready lg_turned lg_ready ex_ready cw_ready "
                 "cwT_turned cwT_ready ident_ready half_ready consts aw0_raw aw0_hi aw0_ready vp_ones "
                 "rel_loaded rel_mean rel_neg diag_row diag_ready diag_stored skewed flip_zero flip_ready bias_turned "
                 "bias_ready rsel_loaded rsel_hi rsel_ready sel_ready raw_ready raw_free split_w_hi split_w passed").split()
        (in_step, route_step, rope_added, cen_squared, head_std, squared, masked, quartic_even, quartic_odd, mixed0, biased_ready, prob_ready, probT_turned,
         probT_odd, probT_even, mixed2, wcol_ready, prod_u, lgT_turned, lgT_ready, lg_turned, lg_ready, ex_ready, cw_ready,
         cwT_turned, cwT_ready, ident_ready, half_ready, consts, aw0_raw, aw0_hi, aw0_ready, vp_ones,
         rel_loaded, rel_mean, rel_neg, diag_row, diag_ready, diag_stored, skewed, flip_zero, flip_ready, bias_turned,
         bias_ready, rsel_loaded, rsel_hi, rsel_ready, sel_ready, raw_ready, raw_free, split_w_hi, split_w, passed) = (
            sem(n) for n in names)

        PIECES = 4
        PARTS = {0: 0, 1: PIECES * TILES1, 2: PIECES * TILES1 + iterations[1]}
        LOADS = {0: 0, 1: TILES1, 2: TILES1 + iterations[1]}
        IN_STEPS = 13
        ROUTE_STEPS = 10
        OUT_STEPS = {0: 4, 1: 3, 2: 6, 3: 3}

        def taken(eng, i, h):
            if h % 2:
                eng.wait_ge(probT_odd, H2 // 2 * i + (h + 1) // 2)
            else:
                eng.wait_ge(probT_even, H2 // 2 * i + h // 2 + 1)

        blk = ctx.enter_context(nc.Block())

        def apart(eng):
            eng.sem_inc(passed, 1)

        def passes(eng, n, body):
            body(0, True, 2)
            with eng.Fori(1, n - 2) as i:
                body(i, False, 2)
            body(n - 2, False, 1)
            body(n - 1, False, 0)

        def product3(pe, o, lh, ll, rh, rl, start, stop):
            pe.matmul(o, lh, rh, start=start, stop=False, skip_group_check=True)
            pe.matmul(o, lh, rl, start=False, stop=False, skip_group_check=True)
            return pe.matmul(o, ll, rh, start=False, stop=stop, skip_group_check=True)

        @blk.sync
        def _(sp):
            def rows(ap, i, nt):
                return ap[bass.ts(i, nt * P), :].rearrange("(t p) e -> p t e", p=P)

            sp.dma_start(WORK[:, 0:2048], aw0.rearrange("p k n -> p (k n)")).then_inc(aw0_raw, 16)
            sp.dma_start(ropet[:], rope.rearrange("p a b -> p (a b)")).then_inc(consts, 16)
            sp.dma_start(lnt[:], ln.rearrange("p a b -> p (a b)")).then_inc(consts, 16)
            sp.sem_inc(raw_free, 1)
            for f in range(4):
                nt = 2 if f in (0, 2) else 4
                n = iterations[f]
                x_turned_in = xt_in_a if nt == 2 else xt_in_f
                x_added = xr_a if nt == 2 else xr_f
                normed = xo_a if nt == 2 else xo_f
                turns = 1 if nt == 2 else KT
                if f:
                    sp.wait_ge(stored[f - 1], 16 * iterations[f - 1] + 16)
                if f == 0:
                    sp.dma_start(x_turned_in, rows(x_in[f], 0, nt)).then_inc(xt_loaded[f], 16)
                sp.dma_start(x_added, rows(x_in[f], 0, nt)).then_inc(xr_loaded[f], 16)
                sp.sem_inc(stored[f], 16)
                if f == 0:
                    sp.dma_start(small[0:TABLE, 0:D2], rel).then_inc(rel_loaded, 16)
                    sp.wait_ge(diag_ready, 1)
                    sp.dma_start(ediag, diagonals).then_inc(diag_stored, 16)
                    sp.wait_ge(diag_stored, 16)
                    for t in range(2):
                        skew = bass.AP(ediag.tensor, S - P * (t + 1), [[1, P], [1, S]])
                        sp.dma_start(skewed_bias[:, S * t:S * (t + 1)], skew).then_inc(skewed, 16)
                if nt == 2:
                    sp.wait_ge(xt_turned[f], 1)
                    sp.dma_start(x_turned_in, rows(x_in[f], 1, nt)).then_inc(xt_loaded[f], 16)

                def weights(i):
                    if f == 0:
                        sp.wait_ge(raw_free, i + 1)
                        apart(sp)
                        sp.dma_start(wraw[:], wu1[bass.ts(i, 1), :, :].rearrange("a p n -> p (a n)")).then_inc(raw_ready, 16)
                    if f == 1:
                        sp.wait_ge(raw_free, LOADS[1] + i + 1)
                        apart(sp)
                        sp.dma_start(wraw[:, 0:512], aw2[:, bass.ts(i, 512)]).then_inc(raw_ready, 16)
                    if f == 2:
                        for k in range(2):
                            sp.wait_ge(raw_free, LOADS[2] + 2 * i + k + 1)
                            apart(sp)
                            sp.dma_start(wraw[:], wu3[bass.ts(2 * i + k, 1), :, :].rearrange("a p n -> p (a n)")
                                         ).then_inc(raw_ready, 16)

                def turn_next(i):
                    ahead = i + 2 if nt == 2 else i + 1
                    sp.wait_ge(xt_turned[f], turns * ahead)
                    apart(sp)
                    sp.dma_start(x_turned_in, rows(x_in[f], ahead, nt)).then_inc(xt_loaded[f], 16)

                def store(i):
                    sp.wait_ge(xo_ready[f], i + 1)
                    apart(sp)
                    sp.dma_start(rows(x_out[f], i, nt), normed).then_inc(stored[f], 16)

                def add_next(i):
                    sp.dma_start(x_added, rows(x_in[f], i, nt)).then_inc(xr_loaded[f], 16)

                turn_next(0)
                weights(0)
                with sp.Fori(1, n - 2 if nt == 2 else n - 1) as i:
                    turn_next(i)
                    weights(i)
                    store(i - 1)
                    add_next(i)
                for i in (range(n - 2, n) if nt == 2 else range(n - 1, n)):
                    weights(i)
                    if i == n - 1 and f < 3:
                        sp.wait_ge(xt_turned[f], turns * n)
                        sp.wait_ge(stored[f], 16 * 2 if f == 1 else 16 * 3)
                        if nt == 2:
                            sp.wait_ge(vp_ready[f], n)
                        sp.dma_start(xt_in_a if f == 1 else xt_in_f, rows(x_in[f + 1], 0, 2 if f == 1 else 4)
                                     ).then_inc(xt_loaded[f + 1], 16)
                    store(i - 1)
                    add_next(i)
                if f == 2:
                    sp.wait_ge(mixed2, H2 // 4 * n)
                    sp.dma_start(router_raw, router.rearrange("p k n -> p (k n)")).then_inc(rsel_loaded, 16)
                    sp.dma_start(sel_raw, sel).then_inc(rsel_loaded, 16)
                    sp.wait_ge(raw_free, LOADS[2] + TILES3)
                    sp.dma_start(wraw[:], wu3[TILES3 - 1]).then_inc(raw_ready, 16)
                store(n - 1)
            sp.wait_ge(stored[3], 16 * iterations[3] + 16)

        @blk.tensor
        def _(pe):
            pe.wait_ge(ident_ready, 2)
            pe.wait_ge(rel_neg, 1)
            pe.matmul(ps[0:1, 0, 0:TABLE], small[0:TABLE, 16:17], ident[0:TABLE, 0:TABLE],
                      start=True, stop=True).then_inc(diag_row, 1)

            def x_turn(f, b):
                pe.wait_ge(xt_loaded[f], 16 * b + 16)
                for k in range(KT):
                    for t in range(2):
                        m = pe.transpose(ps[:, B_XT, S * k + P * t:S * k + P * (t + 1)],
                                         xt_in_a[:, t, P * k:P * (k + 1)], ident[:])
                m.then_inc(xt_turned[f], 1)

            def qk(f, b, t):
                tok = slice(P * t, P * (t + 1))
                for k in range(KT):
                    m = product3(pe, ps[:, B_QK[f][t], :], XT_a[0][:, k, tok], XT_a[1][:, k, tok],
                                 AW[:, 0, k, 0:512], AW[:, 1, k, 0:512], k == 0, k == KT - 1)
                m.then_inc(qk_ready[f], 1)

            def v(f, b):
                for t in range(2):
                    tok = slice(P * t, P * (t + 1))
                    for k in range(KT):
                        m = product3(pe, ps[:, B_V, S * t:S * (t + 1)], XT_a[0][:, k, tok], XT_a[1][:, k, tok],
                                     AW[:, 0, k, 512:768], AW[:, 1, k, 512:768], k == 0, k == KT - 1)
                m.then_inc(v_ready[f], 1)

            def heads_out(f, b, n):
                pe.wait_ge(heads_q[f], 4 * b + n)
                pe.wait_ge(heads_k[f], 4 * b + n)

            def heads(f, b, n):
                for src, bank, out in ((QS, B_QT, heads_q[f]), (KS, B_KT, heads_k[f])):
                    w = src.bitcast(F32).rearrange("p (t g c) -> p t g c", t=2, g=8)
                    if n:
                        pe.wait_ge(out, 4 * b + n)
                    for g in range(2):
                        for t in range(2):
                            m = pe.transpose(ps[:, bank, S * g + P * t:S * g + P * (t + 1)],
                                             w[:, t, 2 * n + g, :], ident[:])
                    m.then_inc(heads_turned[f], 1)

            def c_turn(f, b, n, groups, last=False):
                if n == 0:
                    pe.wait_ge(o_copied[f], groups // 2 * (b + 1))
                if n >= 2:
                    pe.wait_ge(ctx_done[f], len(C_BANKS[f]) * b + n - 1)
                ot = OT[:, 0:groups * S].rearrange("p (g q) -> p g q", g=groups)
                t, c = divmod(n, len(C_BANKS[f]) // 2)
                for g in range(4):
                    m = pe.transpose(ps[:, LAST_C[n] if last else C_BANKS[f][n], P * g:P * (g + 1)], ot[:, 4 * c + g, P * t:P * (t + 1)], ident[:])
                m.then_inc(c_turned[f], 1)

            def ct_turn(f, b, last=False):
                pe.wait_ge(ctx_done[f], len(C_BANKS[f]) * (b + 1))
                for k in range(KT):
                    for t in range(2):
                        m = pe.transpose(ps[:, LAST_CT if last else B_CT[f], S * k + P * t:S * k + P * (t + 1)],
                                         ctx_a[:, t, P * k:P * (k + 1)], ident[:])
                m.then_inc(ct_turned[f], 1)

            def project(f, b, last=False):
                pe.wait_ge(ct_ready[f], b + 1)
                for t in range(2):
                    tok = slice(P * t, P * (t + 1))
                    for k in range(KT):
                        m = product3(pe, ps[:, LAST_Y if last else B_Y[f], E * t:E * (t + 1)], CT_a[0][:, k, tok], CT_a[1][:, k, tok],
                                     AW[:, 0, k, 768:1024], AW[:, 1, k, 768:1024], k == 0, k == KT - 1)
                m.then_inc(y_ready[f], 1)

            vp = v_and_one(0)

            def phase0():
                pe.wait_ge(aw0_ready, 1)
                pe.wait_ge(vp_ones, 1)
                n = iterations[0]

                def scores(i, p, first):
                    if p % 2 == 0:
                        heads_out(0, i, p // 2 + 1)
                    if p >= 2 or not first:
                        pe.wait_ge(squared, H0 // 2 * i + p - 1)
                    for h in (2 * p, 2 * p + 1):
                        r = slice(64 * (h % 2), 64 * (h % 2) + 64)
                        b = 2 * (p % 2) + h % 2
                        pe.matmul(ps[:, b, 0:S], KTT[r, h // 2, 0:P], QT[r, h // 2, :], start=True, stop=True)
                        m = pe.matmul(ps[:, b, S:S + P], KTT[r, h // 2, P:S], QT[r, h // 2, P:S], start=True, stop=True)
                    m.then_inc(score_ready[0], 1)

                def mix(i, quad, first, left):
                    if quad == 0:
                        if left:
                            pe.wait_ge(in_step, IN_STEPS * (i + 1) + 3)
                        pe.wait_ge(vp_ready[0], i + 1)
                    if quad == 2 and not first:
                        pe.wait_ge(out_step[0], OUT_STEPS[0] * (i - 1) + 3)
                    pe.wait_ge(quartic_even, H0 // 4 * i + quad + 1)
                    pe.wait_ge(quartic_odd, H0 // 4 * i + quad + 1)
                    for kt in range(2):
                        for j in range(4):
                            pv = P4(2 * quad + j // 2)[:, j % 2, :]
                            cols = slice(S * (quad % 2) + P * kt, S * (quad % 2) + S)
                            at = (D0 + 1) * (4 * quad + j)
                            m = pe.matmul(ps[32 * j:32 * j + 32, 4 + quad // 2, cols], vp[:, kt, at:at + 32],
                                          pv[:, 0:S] if kt == 0 else pv[:, S:S + P],
                                          start=kt == 0, stop=kt == 1, skip_group_check=True,
                                          tile_position=(0, 32 * j))
                    m.then_inc(mixed0, 1)

                def one(i, first, left):
                    for p in range(H0 // 2):
                        scores(i, p, first)
                        if p % 2 and (p > 1 or not first):
                            mix(i if p > 1 else i - 1, (p // 2 - 1) % 4, first, left)
                        if p == 1:
                            if left:
                                pe.wait_ge(in_step, IN_STEPS * (i + 1) + 6)
                            heads(0, i, 2)
                        if p == 2:
                            heads(0, i, 3)
                            if not first:
                                c_turn(0, i - 1, 0, 4)
                        if p == 3:
                            heads_out(0, i, 4)
                            if not first:
                                c_turn(0, i - 1, 1, 4)
                            if left:
                                v(0, i + 1)
                        if p == 4:
                            if not first:
                                ct_turn(0, i - 1)
                            if left > 1:
                                x_turn(0, i + 2)
                        if p == 5 and not first:
                            project(0, i - 1)
                        if p == 6 and left:
                            pe.wait_ge(v_staged[0], i + 2)
                            if left > 1:
                                pe.wait_ge(xt_ready[0], i + 3)
                            pe.wait_ge(split_ready[0], 4 * (i + 1) + 4)
                            heads(0, i + 1, 0)
                            if left > 1:
                                pe.wait_ge(o_copied[0], 2 * i + 1)
                                qk(0, i + 2, 0)
                        if p == 7 and left:
                            heads(0, i + 1, 1)
                            if left > 1:
                                pe.wait_ge(heads_q[0], 4 * (i + 1) + 2)
                                qk(0, i + 2, 1)

                x_turn(0, 0)
                pe.wait_ge(xt_ready[0], 1)
                for t in range(2):
                    qk(0, 0, t)
                pe.wait_ge(in_step, 6)
                v(0, 0)
                x_turn(0, 1)
                pe.wait_ge(skewed, 32)
                pe.wait_ge(flip_ready, 1)
                pe.matmul(ps[:, 1, :], flip, skewed_bias, start=True, stop=True).then_inc(bias_turned, 1)
                pe.wait_ge(bias_ready, 1)
                pe.wait_ge(v_staged[0], 1)
                pe.wait_ge(xt_ready[0], 2)
                pe.wait_ge(split_ready[0], 4)
                heads(0, 0, 0)
                qk(0, 1, 0)
                heads(0, 0, 1)
                pe.wait_ge(heads_q[0], 2)
                qk(0, 1, 1)
                passes(pe, n, one)
                mix(n - 1, H0 // 4 - 1, False, 0)
                for c in range(2):
                    c_turn(0, n - 1, c, 4, True)

            def phase2():
                pe.wait_ge(out_step[1], OUT_STEPS[1] * (iterations[1] - 1) + 2)
                n = iterations[2]

                def scores(i, h, first):
                    j, g = h % 4, h // 4
                    r = slice(32 * j, 32 * j + 32)
                    if h % 8 == 0:
                        heads_out(2, i, h // 8 + 1)
                    if h >= 2 or not first:
                        pe.wait_ge(biased_ready, H2 * i + h - 1)
                    for t in range(2):
                        m = pe.matmul(ps[:, h % 2, S * t:S * (t + 1)], QT[r, g, P * t:P * (t + 1)], KTT[r, g, :],
                                      start=True, stop=True, tile_position=(32 * j, 0))
                    m.then_inc(score_ready[2], 1)

                def turn(i, h, first):
                    pe.wait_ge(prob_ready, H2 * i + h + 1)
                    if h >= 2 or not first:
                        taken(pe, i, h - 2)
                    for kt in range(2):
                        for t in range(2):
                            m = pe.transpose(ps[:, 2 + h % 2, S * kt + P * t:S * kt + P * (t + 1)],
                                             prob(h)[:, t, P * kt:P * (kt + 1)], ident[:])
                    m.then_inc(probT_turned, 1)

                def mix(i, quad, first):
                    if quad == 0:
                        pe.wait_ge(vp_ready[2], i + 1)
                    if quad % 2 == 0 and (quad >= 4 or not first):
                        pe.wait_ge(o_copied[2], 4 * i + quad // 2 - 1)
                    taken(pe, i, 4 * quad + 2)
                    taken(pe, i, 4 * quad + 3)
                    for kt in range(2):
                        for j in range(4):
                            h = 4 * quad + j
                            at = (D2 + 1) * h
                            m = pe.matmul(ps[32 * j:32 * j + 32, 4 + quad // 2 % 2, S * (quad % 2):S * (quad % 2 + 1)],
                                          vp[:, kt, at:at + 32], probT(h)[:, kt, :], start=kt == 0, stop=kt == 1,
                                          skip_group_check=True, tile_position=(0, 32 * j))
                    m.then_inc(mixed2, 1)

                def one(i, first, left):
                    for h in range(H2):
                        scores(i, h, first)
                        if h >= 2 or not first:
                            turn(i, h - 2, first)
                        if h % 4 == 3 and (h > 3 or not first):
                            mix(i if h > 3 else i - 1, (h - 7) // 4 % 8, first)
                        if h == 1:
                            pe.wait_ge(v_staged[2], i + 1)
                            heads_out(2, i, 3)
                            heads(2, i, 3)
                        if h == 5:
                            heads_out(2, i, 4)
                            if left:
                                x_turn(2, i + 1)
                        if not first:
                            if h == 8:
                                c_turn(2, i - 1, 0, 8)
                            if h == 10:
                                if left:
                                    pe.wait_ge(xt_ready[2], i + 2)
                                c_turn(2, i - 1, 1, 8)
                            if h in (12, 13):
                                c_turn(2, i - 1, h - 10, 8)
                            if h == 16:
                                ct_turn(2, i - 1)
                        if h == 17 and left:
                            pe.wait_ge(xt_ready[2], i + 2)
                            qk(2, i + 1, 0)
                        if h == 20 and not first:
                            if left:
                                pe.wait_ge(split_ready[2], 4 * (i + 1) + 2)
                            project(2, i - 1)
                        if left:
                            if h == 21:
                                qk(2, i + 1, 1)
                            if h == 25:
                                pe.wait_ge(split_ready[2], 4 * (i + 1) + 4)
                                v(2, i + 1)
                            if h == 27:
                                pe.wait_ge(v_staged[2], i + 2)
                                if not first:
                                    pe.wait_ge(out_step[2], OUT_STEPS[2] * (i - 1) + 5)
                                heads(2, i + 1, 0)
                            if h in (29, 31):
                                heads_out(2, i + 1, (h - 27) // 2)
                                heads(2, i + 1, (h - 27) // 2)

                passes(pe, n, one)
                for h in (H2 - 2, H2 - 1):
                    turn(n - 1, h, False)
                mix(n - 1, H2 // 4 - 1, False)
                for c in range(4):
                    c_turn(2, n - 1, c, 8, True)

            x_turn_attention = x_turn

            def feed_forward(f, tiles):
                def gate_up(i, j):
                    if j >= 2:
                        pe.wait_ge(prod_ready[f], tiles * i + j - 1)
                    for n, ready in enumerate((gate_ready[f], up_ready[f])):
                        for k in range(KT):
                            c = slice((n * KT + k) * P, (n * KT + k + 1) * P)
                            m = product3(pe, ps[:, 2 + 2 * (j % 2) + n, :], WU[:, j, 0, c], WU[:, j, 1, c],
                                         XT_f[f][0][:, k, :], XT_f[f][1][:, k, :], k == 0, k == KT - 1)
                        m.then_inc(ready, 1)
                    if f == 3:
                        if j == 0:
                            logits_turned(i)
                        if j == 1:
                            router_columns(i)
                            spread(j - 1)
                        if j >= 1:
                            spread(j)

                def spread(j):
                    pe.matmul(ps[:, 7 - j % 2, :], SELW[:, P * j:P * (j + 1)], CWT, start=True, stop=True
                              ).then_inc(wcol_ready, 1)

                def down(i, j, first):
                    pe.wait_ge(hid_ready[f], tiles * i + j + 1)
                    if j == 0:
                        if first:
                            pe.wait_ge(out_step[f - 1], OUT_STEPS[f - 1] * iterations[f - 1] - 1)
                        else:
                            pe.wait_ge(z_done[f], i)
                    hh, hl = HT[f][:, j % 3, 0, :], HT[f][:, j % 3, 1, :]
                    wd = [WU[:, j, h, 2 * KT * P:UNIT] for h in range(2)]
                    for t in range(4):
                        tok = slice(P * t, P * (t + 1))
                        m = product3(pe, ps[:, t // 2, E * (t % 2):E * (t % 2 + 1)], hh[:, tok], hl[:, tok],
                                     wd[0], wd[1], j == 0 and t % 2 == 0, j == tiles - 1)
                    m.then_inc(down_done[f], 1)

                def router_logits(i):
                    n = 0
                    for k in range(KT):
                        for a in (routh, routl):
                            for b in XT_f[f]:
                                m = pe.matmul(ps[0:GATES, 6, :], a[:, GATES * k:GATES * (k + 1)], b[:, k, :],
                                              start=n == 0, stop=n == 4 * KT - 1, skip_group_check=True)
                                n += 1
                    m.then_inc(lgT_turned, 1)

                def logits_turned(i):
                    pe.wait_ge(lgT_ready, i + 1)
                    apart(pe)
                    for t in range(4):
                        m = pe.transpose(ps[:, 7, GATES * t:GATES * (t + 1)], lgT[:, P * t:P * (t + 1)],
                                         ident[0:GATES, 0:GATES])
                    m.then_inc(lg_turned, 1)

                def router_columns(i):
                    pe.wait_ge(cw_ready, i + 1)
                    for t in range(4):
                        m = pe.transpose(ps[0:2 * GATES, 6, P * t:P * (t + 1)], cs2[:, t, :], ident[:])
                    m.then_inc(cwT_turned, 1)
                    pe.wait_ge(cwT_ready, i + 1)

                def x_turn(b, k):
                    if k == 0:
                        pe.wait_ge(xt_loaded[f], 16 * b + 16)
                    for t in range(4):
                        m = pe.transpose(ps[:, 6 + k, P * t:P * (t + 1)], xt_in_f[:, t, P * k:P * (k + 1)], ident[:])
                    m.then_inc(xt_turned[f], 1)

                def start_attention(j):
                    if j == 2:
                        pe.wait_ge(split_w, PARTS[2])
                        x_turn_attention(2, 0)
                    if j == 3:
                        pe.wait_ge(xt_ready[2], 1)
                        qk(2, 0, 0)
                    if j == 4:
                        qk(2, 0, 1)
                    if j == 5:
                        pe.wait_ge(split_ready[2], 4)
                        v(2, 0)
                    if j == 6:
                        pe.wait_ge(v_staged[2], 1)
                        heads(2, 0, 0)
                    if j == 7:
                        heads(2, 0, 1)

                def one(i, first, left):
                    last = not left
                    pe.wait_ge(xt_ready[f], KT * i + KT)
                    if f == 3:
                        router_logits(i)
                    gate_up(i, 0)
                    if first:
                        ct_turn(f - 1, iterations[f - 1] - 1, True)
                    if first and f == 3:
                        project(f - 1, iterations[f - 1] - 1, True)
                        pe.wait_ge(sel_ready, 1)
                    gate_up(i, 1)
                    if first and f == 1:
                        project(f - 1, iterations[f - 1] - 1, True)
                    for j in range(2, tiles):
                        if j == tiles - 1 and f == 3:
                            pe.wait_ge(split_w, PARTS[2] + TILES3)
                        gate_up(i, j)
                        down(i, j - 2, first)
                        if f == 1 and last:
                            start_attention(j)
                    for k in range(KT):
                        if not last:
                            if f == 3:
                                pe.wait_ge(prod_ready[f], tiles * i + tiles - 1 + k)
                            x_turn(i + 1, k)
                        down(i, tiles - 2 + k, first)
                    if f == 1 and last:
                        heads(2, 0, 2)

                x_turn(0, 0)
                x_turn(0, 1)
                if f == 3:
                    pe.wait_ge(rsel_ready, 1)
                passes(pe, iterations[f], one)

            phase0()
            pe.wait_ge(split_w, PARTS[1])
            feed_forward(1, TILES1)
            phase2()
            pe.wait_ge(split_w, PARTS[2] + TILES3 - 1)
            feed_forward(3, TILES3)

        @blk.scalar
        def _(act):
            def halves(bank):
                return ps[:, bank, :].rearrange("p (k t) -> p k t", k=2)

            def x_hi(f, b):
                act.wait_ge(xt_turned[f], b + 1)
                act.copy(XT_a[0], halves(B_XT)).then_inc(xt_hi[f], 1)

            def q_heads(f, b, n):
                act.wait_ge(heads_turned[f], 8 * b + 2 * n + 1)
                act.copy(QT[:, 2 * n:2 * n + 2, :], halves(B_QT)).then_inc(heads_q[f], 1)

            def stage_v(f, b):
                act.wait_ge(v_ready[f], b + 1)
                act.copy(VS, ps[:, B_V, :]).then_inc(v_staged[f], 1)

            def place_v(f, b, first, h, d):
                act.wait_ge(v_staged[f], b + 1)
                act.wait_ge(vp_ones, f // 2 + 1)
                if not first:
                    act.wait_ge(mixed0 if f == 0 else mixed2, h // 4 * b)
                o = v_and_one(f)[:, :, 0:h * (d + 1)].rearrange("p t (h c) -> p t h c", h=h)
                act.copy(o[:, :, :, 0:d], VS.rearrange("p (t h d) -> p t h d", t=2, h=h)).then_inc(vp_ready[f], 1)

            def hi_parts(b, t):
                act.wait_ge(qk_ready[2], 2 * b + t + 1)
                src = ps[:, B_QK[2][t], :].rearrange("p (w h d) -> p w h d", w=2, h=H2)
                for w, (dst, places) in enumerate(((QS, (0, 2)), (KS, (0, 1)))):
                    d5 = dst.rearrange("p (t h s d) -> p t h s d", t=2, h=H2, s=4)
                    for s in places:
                        act.mul(d5[:, t, :, s, :], src[:, w], QSCALE if w == 0 else 1.0).then_inc(split_hi[2], 1)

            def context_hi(f, b, last=False):
                act.wait_ge(ct_turned[f], b + 1)
                act.copy(CT_a[0], halves(LAST_CT if last else B_CT[f])).then_inc(ct_hi[f], 1)

            def phase0():
                act.wait_ge(half_ready, 2)
                act.wait_ge(aw0_raw, 16)
                act.copy(AW[:, 0], WORK[:, 0:2048].rearrange("p (k n) -> p k n", k=KT)).then_inc(aw0_hi, 1)
                n = iterations[0]

                def centred_squares(b):
                    act.wait_ge(in_step, IN_STEPS * b + 8)
                    act.square(SQ, CEN).then_inc(cen_squared, 1)

                def deviation(b):
                    act.wait_ge(in_step, IN_STEPS * b + 9)
                    act.activation(hrs, hvar, ACT.Sqrt, scale=1.0 / D0, bias=eps_col).then_inc(head_std, 1)

                def hi_parts(b):
                    act.wait_ge(in_step, IN_STEPS * b + 13)
                    n5 = SQ.rearrange("p (t w h d) -> p t w h d", t=2, w=2, h=H0)
                    for w, (dst, places) in enumerate(((QS, (0, 2)), (KS, (0, 1)))):
                        d5 = dst.rearrange("p (t h s d) -> p t h s d", t=2, h=H0, s=4)
                        for s in places:
                            act.copy(d5[:, :, :, s, :], n5[:, :, w]).then_inc(split_hi[0], 1)

                def turned_heads(b, n):
                    q_heads(0, b, n)
                    act.wait_ge(heads_turned[0], 8 * b + 2 * n + 2)
                    act.copy(KTT[:, 2 * n:2 * n + 2, :], halves(B_KT)).then_inc(heads_k[0], 1)

                def quartic(i, p, first):
                    act.wait_ge(masked, H0 // 2 * i + p + 1)
                    if p >= 4 or not first:
                        act.wait_ge(mixed0, H0 // 4 * i + p // 2 - 1)
                    act.square(P4(p), U(p)).then_inc(quartic_odd, 1)

                def outputs(b, n):
                    act.wait_ge(mixed0, H0 // 4 * b + 2 * n + 2)
                    act.copy(OT[:, 512 * n:512 * (n + 1)], ps[:, 4 + n, :]).then_inc(o_copied[0], 1)

                def one(i, first, left):
                    for p in range(H0 // 2):
                        act.wait_ge(score_ready[0], H0 // 2 * i + p + 1)
                        if p >= 2 or not first:
                            if p % 2:
                                act.wait_ge(quartic_odd, H0 // 4 * i + p // 2)
                            else:
                                act.wait_ge(quartic_even, H0 // 4 * i + p // 2)
                        b = 2 * (p % 2)
                        act.square(U(p), ps[:, b:b + 2, 0:384]).then_inc(squared, 1)
                        if p % 2 == 0 and (p or not first):
                            quartic(i, p - 1, first)
                        if p == 1:
                            if not first:
                                outputs(i - 1, 1)
                            turned_heads(i, 2)
                        if p == 2:
                            if left:
                                centred_squares(i + 1)
                            turned_heads(i, 3)
                            place_v(0, i, first, H0, D0)
                        if p == 3 and left:
                            deviation(i + 1)
                            stage_v(0, i + 1)
                        if p == 4:
                            if not first:
                                context_hi(0, i - 1)
                            if left > 1:
                                x_hi(0, i + 2)
                        if p == 5 and left:
                            hi_parts(i + 1)
                        if p == 6:
                            outputs(i, 0)
                            if left:
                                turned_heads(i + 1, 0)
                        if p == 7 and left:
                            turned_heads(i + 1, 1)

                x_hi(0, 0)
                stage_v(0, 0)
                x_hi(0, 1)
                centred_squares(0)
                deviation(0)
                hi_parts(0)
                for q in range(2):
                    turned_heads(0, q)
                passes(act, n, one)
                quartic(n - 1, H0 // 2 - 1, False)
                outputs(n - 1, 1)

            def phase2():
                n = iterations[2]

                def exponential(i, h, first):
                    act.wait_ge(biased_ready, H2 * i + h + 1)
                    for t in range(2):
                        k = 2 * (h % 4) + t
                        m = act.activation(prob(h)[:, t, :], prob(h)[:, t, :], ACT.Exp, scale=-1.0,
                                           bias=mneg[:, k:k + 1])
                    m.then_inc(prob_ready, 1)

                def take(i, h, first):
                    act.wait_ge(probT_turned, H2 * i + h + 1)
                    if h >= 8 or not first:
                        act.wait_ge(mixed2, H2 // 4 * i + (h - 8) // 4 + 1)
                    act.copy(probT(h), halves(2 + h % 2)).then_inc(probT_odd, 1)

                def one(i, first, left):
                    for h in range(H2):
                        exponential(i, h, first)
                        if h % 2 and (h > 2 or not first):
                            take(i, h - 2, first)
                        if h == 2:
                            q_heads(2, i, 3)
                        if h == 5:
                            place_v(2, i, first, H2, D2)
                        if h == 6 and left:
                            x_hi(2, i + 1)
                        if h == 17 and not first:
                            context_hi(2, i - 1)
                        if left:
                            if h in (18, 22):
                                hi_parts(i + 1, (h - 18) // 4)
                            if h == 26:
                                stage_v(2, i + 1)
                            if h in (28, 30, 31):
                                q_heads(2, i + 1, (h - 27) // 2 if h < 31 else 2)

                passes(act, n, one)
                take(n - 1, H2 - 1, False)

            x_hi_attention = x_hi

            def feed_forward(f, tiles):
                def x_hi(b, k):
                    act.wait_ge(xt_turned[f], KT * b + k + 1)
                    act.copy(XT_f[f][0][:, k, :], ps[:, 6 + k, :]).then_inc(xt_hi[f], 1)

                def one(i, first, left):
                    last = not left
                    if f == 3:
                        act.wait_ge(lgT_turned, i + 1)
                        act.copy(lgT, ps[0:GATES, 6, :]).then_inc(lgT_ready, 1)
                        if first:
                            context_hi(2, iterations[2] - 1, True)
                        act.wait_ge(lg_ready, i + 1)
                        act.activation(ex, lg, ACT.Exp).then_inc(ex_ready, 1)

                    def silu(j):
                        act.wait_ge(gate_ready[f], tiles * i + j + 1)
                        act.activation(sg[:, j % 2, :], ps[:, 2 + 2 * (j % 2), :], ACT.Silu).then_inc(silu_ready[f], 1)

                    def hidden_hi(j):
                        act.wait_ge(prod_ready[f], tiles * i + j + 1)
                        if j >= 3:
                            act.wait_ge(down_done[f], tiles * i + j - 2)
                        act.copy(HT[f][:, j % 3, 0, :], hf[:, j % 3, :]).then_inc(hid_hi[f], 1)

                    def start_attention(j):
                        if j == 3:
                            x_hi_attention(2, 0)
                        if j in (4, 5):
                            hi_parts(0, j - 4)
                        if j == 6:
                            stage_v(2, 0)
                        if j == 7:
                            q_heads(2, 0, 0)

                    silu(0)
                    if first and f == 1:
                        context_hi(0, iterations[0] - 1, True)
                    if first and f == 3:
                        act.wait_ge(y_ready[2], iterations[2])
                        act.copy(SELW, sel_raw).then_inc(sel_ready, 1)
                    if f == 3:
                        act.wait_ge(cwT_turned, i + 1)
                        act.copy(CWT, ps[0:2 * GATES, 6, :]).then_inc(cwT_ready, 1)
                    for j in range(1, tiles):
                        silu(j)
                        hidden_hi(j - 1)
                        if f == 1 and last:
                            start_attention(j)
                    hidden_hi(tiles - 1)
                    if f == 1 and last:
                        q_heads(2, 0, 1)
                        q_heads(2, 0, 2)
                    if not last:
                        x_hi(i + 1, 0)
                        x_hi(i + 1, 1)

                x_hi(0, 0)
                x_hi(0, 1)
                if f == 3:
                    act.wait_ge(rsel_loaded, 32)
                    act.copy(routh[:], router_raw).then_inc(rsel_hi, 1)
                passes(act, iterations[f], one)

            phase0()
            feed_forward(1, TILES1)
            phase2()
            feed_forward(3, TILES3)

        @blk.vector
        def _(dve):
            def halves(bank):
                return ps[:, bank, :].rearrange("p (k t) -> p k t", k=2)

            def step(count, value, m, alone=False):
                m.then_inc(count, 1)
                dve.wait_ge(count, value)
                if alone:
                    apart(dve)

            def add(f, b, nt, xr, banks):
                n = OUT_STEPS[f] * b + OUT_STEPS[f] - 1 - len(banks)
                dve.wait_ge(xr_loaded[f], 16 * b + 16)
                for k, bank in enumerate(banks):
                    m = dve.tensor_tensor(xr[:, 2 * k:2 * k + 2, :], halves(bank), xr[:, 2 * k:2 * k + 2, :], ALU.add)
                    step(out_step[f], n + k + 1, m)
                if f in (1, 3):
                    dve.sem_inc(z_done[f], 1)
                for t in range(nt):
                    m = dve.bn_stats(stats[:, t, :], xr[:, t, :])
                step(out_step[f], n + len(banks) + 1, m, alone=True)
                for t in range(nt):
                    m = dve.bn_aggr(mv[:, t, :], stats[:, t, :])
                m.then_inc(var_ready[f], 1)

            def norm(f, b, nt, xr, xo):
                dve.wait_ge(rstd_ready[f], b + 1)
                dve.wait_ge(stored[f], 16 * b + 16)
                for t in range(nt):
                    m = dve.tensor_scalar(xo[:, t, :], xr[:, t, :], mv[:, t, 0:1], rstd[:, t:t + 1], ALU.subtract, ALU.mult)
                m.then_inc(xo_ready[f], 1)

            def x_lo(f, b):
                dve.wait_ge(xt_hi[f], b + 1)
                dve.tensor_tensor(XT_a[1], halves(B_XT), XT_a[0].bitcast(F32), ALU.subtract).then_inc(xt_ready[f], 1)

            def context(f, b, n, d, last=False):
                nb = len(C_BANKS[f])
                dve.wait_ge(c_turned[f], nb * b + n + 1)
                v = ps[:, LAST_C[n] if last else C_BANKS[f][n], :].rearrange("p (h c) -> p h c", c=32)
                r = rden[:, 16 * n:16 * (n + 1)].unsqueeze(2)
                step(out_step[f], OUT_STEPS[f] * b + n + 1, dve.reciprocal(r, v[:, :, d:d + 1]))
                t, part = divmod(n, nb // 2)
                o = ctx_a[:, t, 16 * d * part:16 * d * (part + 1)].rearrange("p (h c) -> p h c", h=16)
                dve.tensor_tensor(o, v[:, :, 0:d], r.to_broadcast([P, 16, d]), ALU.mult).then_inc(ctx_done[f], 1)

            def context_lo(f, b, last=False):
                dve.wait_ge(ct_hi[f], b + 1)
                dve.tensor_tensor(CT_a[1], halves(LAST_CT if last else B_CT[f]), CT_a[0].bitcast(F32), ALU.subtract).then_inc(ct_ready[f], 1)

            x_lo_attention = x_lo

            def lo_parts_2(b, t):
                src = ps[:, B_QK[2][t], :].rearrange("p (w h d) -> p w h d", w=2, h=H2)
                dve.wait_ge(split_hi[2], 8 * b + 4 * t + 4)
                for w, (dst, places) in enumerate(((QS, (1, 3)), (KS, (2, 3)))):
                    d5 = dst.rearrange("p (t h s d) -> p t h s d", t=2, h=H2, s=4)
                    for s in places:
                        m = dve.scalar_tensor_tensor(out=d5[:, t, :, s, :], in0=src[:, w],
                                                     scalar=QSCALE if w == 0 else 1.0,
                                                     in1=d5[:, t, :, 0, :].bitcast(F32), op0=ALU.mult, op1=ALU.subtract)
                m.then_inc(split_ready[2], 2)

            def k_heads(b, n):
                dve.wait_ge(heads_turned[2], 8 * b + 2 * n + 2)
                dve.tensor_copy(KTT[:, 2 * n:2 * n + 2, :], halves(B_KT)).then_inc(heads_k[2], 1)

            def phase0():
                dve.wait_ge(rel_loaded, 16)
                dve.tensor_reduce(small[0:TABLE, 15:16], small[0:TABLE, 0:D2], AX_X, ALU.add).then_inc(rel_mean, 1)
                dve.wait_ge(rel_mean, 1)
                dve.tensor_scalar(small[0:TABLE, 16:17], small[0:TABLE, 15:16], -1.0 / D2, None, ALU.mult
                                  ).then_inc(rel_neg, 1)
                dve.wait_ge(diag_row, 1)
                lo = S - MAXPOS
                dve.tensor_copy(diagonals[:, lo:lo + TABLE], ps[0:1, 0, 0:TABLE])
                dve.tensor_copy(diagonals[:, 0:lo], ps[0:1, 0, 0:1].to_broadcast([1, lo]))
                dve.tensor_copy(diagonals[:, lo + TABLE:ROWS], ps[0:1, 0, TABLE - 1:TABLE].to_broadcast([1, ROWS - lo - TABLE])
                                ).then_inc(diag_ready, 1)
                dve.wait_ge(aw0_hi, 1)
                raw = WORK[:, 0:2048].rearrange("p (k n) -> p k n", k=KT)
                dve.tensor_tensor(AW[:, 1], raw, AW[:, 0].bitcast(F32), ALU.subtract).then_inc(aw0_ready, 1)
                dve.wait_ge(aw0_ready, 1)
                dve.wait_ge(consts, 32)
                n = iterations[0]
                rh = ROT.rearrange("p (n d) -> p n d", d=D0)
                ch = CEN.rearrange("p (n d) -> p n d", d=D0)
                sh = SQ.rearrange("p (n d) -> p n d", d=D0)
                full = [P, 4 * H0, D0]

                def rope_half(b, t):
                    r4 = ROT.rearrange("p (t h s e) -> p t h s e", t=2, s=2, e=8)
                    r24 = ROT2.rearrange("p (t h s e) -> p t h s e", t=2, s=2, e=8)
                    dve.wait_ge(qk_ready[0], 2 * b + t + 1)
                    src = ps[:, B_QK[0][t], :].rearrange("p (h s e) -> p h s e", s=2, e=8)
                    cos = ropet[:, 16 * t:16 * t + 8].unsqueeze(1).unsqueeze(1).to_broadcast([P, 2 * H0, 2, 8])
                    sin = ropet[:, 16 * t + 8:16 * t + 16].unsqueeze(1).to_broadcast([P, 2 * H0, 8])
                    dve.tensor_tensor(r4[:, t], src, cos, ALU.mult)
                    dve.scalar_tensor_tensor(out=r24[:, t, :, 0, :], in0=src[:, :, 1, :], scalar=-1.0, in1=sin,
                                             op0=ALU.mult, op1=ALU.mult)
                    dve.tensor_tensor(r24[:, t, :, 1, :], src[:, :, 0, :], sin, ALU.mult).then_inc(in_step, 3)

                def centre(b):
                    dve.wait_ge(in_step, IN_STEPS * b + 6)
                    step(rope_added, b + 1, dve.tensor_tensor(ROT, ROT, ROT2, ALU.add))
                    step(in_step, IN_STEPS * b + 7, dve.tensor_reduce(hsum, rh, AX_X, ALU.add))
                    step(in_step, IN_STEPS * b + 8,
                         dve.scalar_tensor_tensor(out=ch, in0=hsum.unsqueeze(2).to_broadcast(full), scalar=-1.0 / D0,
                                                  in1=rh, op0=ALU.mult, op1=ALU.add))

                def variance(b):
                    dve.wait_ge(cen_squared, b + 1)
                    dve.tensor_reduce(hvar, sh, AX_X, ALU.add).then_inc(in_step, 1)

                def scaled(b):
                    dve.wait_ge(head_std, b + 1)
                    step(in_step, IN_STEPS * b + 10, dve.reciprocal(hrs, hrs))
                    step(in_step, IN_STEPS * b + 11, dve.tensor_tensor(ch, ch, hrs.unsqueeze(2).to_broadcast(full), ALU.mult))
                    step(in_step, IN_STEPS * b + 12,
                         dve.tensor_tensor(ch, ch, lnt[:, 0:D0].unsqueeze(1).to_broadcast(full), ALU.mult))
                    step(in_step, IN_STEPS * b + 13,
                         dve.tensor_tensor(sh, ch, lnt[:, D0:2 * D0].unsqueeze(1).to_broadcast(full), ALU.add))

                def lo_parts(b):
                    n5 = SQ.rearrange("p (t w h d) -> p t w h d", t=2, w=2, h=H0)
                    for w, (dst, places) in enumerate(((QS, (1, 3)), (KS, (2, 3)))):
                        d5 = dst.rearrange("p (t h s d) -> p t h s d", t=2, h=H0, s=4)
                        dve.wait_ge(split_hi[0], 4 * b + 2 * w + 2)
                        for s in places:
                            dve.tensor_tensor(d5[:, :, :, s, :], n5[:, :, w], d5[:, :, :, 0, :].bitcast(F32), ALU.subtract
                                              ).then_inc(split_ready[0], 1)

                def quartic(i, p, first):
                    dve.wait_ge(masked, H0 // 2 * i + p + 1)
                    if p >= 4 or not first:
                        dve.wait_ge(mixed0, H0 // 4 * i + p // 2 - 1)
                    dve.tensor_tensor(P4(p), U(p), U(p), ALU.mult).then_inc(quartic_even, 1)

                def one(i, first, left):
                    if left:
                        rope_half(i + 1, 1)
                    quartic(i, 0, first)
                    if left:
                        centre(i + 1)
                    quartic(i, 2, first)
                    if left:
                        variance(i + 1)
                    if not first:
                        context(0, i - 1, 0, D0)
                    if left:
                        scaled(i + 1)
                    if not first:
                        context(0, i - 1, 1, D0)
                    quartic(i, 4, first)
                    if not first:
                        context_lo(0, i - 1)
                    if left > 1:
                        x_lo(0, i + 2)
                    if left:
                        lo_parts(i + 1)
                    if not first:
                        dve.wait_ge(y_ready[0], i)
                        add(0, i - 1, 2, xr_a, (B_Y[0],))
                    quartic(i, 6, first)
                    if not first:
                        norm(0, i - 1, 2, xr_a, xo_a)
                    if left > 1:
                        rope_half(i + 2, 0)

                x_lo(0, 0)
                for t in range(2):
                    rope_half(0, t)
                centre(0)
                x_lo(0, 1)
                dve.wait_ge(bias_turned, 1)
                dve.tensor_copy(nb[:], ps[:, 1, :]).then_inc(bias_ready, 1)
                variance(0)
                scaled(0)
                lo_parts(0)
                rope_half(1, 0)
                passes(dve, n, one)
                for c in range(2):
                    context(0, n - 1, c, D0, True)

            def phase2():
                nbv = nb[:].rearrange("p (t k) -> p t k", t=2)
                n = iterations[2]

                def least(i, h, first):
                    dve.wait_ge(score_ready[2], H2 * i + h + 1)
                    if h >= 4 or not first:
                        dve.wait_ge(probT_turned, H2 * i + h - 3)
                    apart(dve)
                    for t in range(2):
                        k = 2 * (h % 4) + t
                        m = dve.tensor_tensor_reduce(prob(h)[:, t, :], ps[:, h % 2, S * t:S * (t + 1)],
                                                     nbv[:, t, :], 1.0, -FMIN, ALU.add, ALU.min, mneg[:, k:k + 1])
                    m.then_inc(biased_ready, 1)

                def take(i, h, first):
                    dve.wait_ge(probT_turned, H2 * i + h + 1)
                    if h >= 8 or not first:
                        dve.wait_ge(mixed2, H2 // 4 * i + (h - 8) // 4 + 1)
                    dve.tensor_copy(probT(h), halves(2 + h % 2)).then_inc(probT_even, 1)

                def outputs(b, n):
                    dve.wait_ge(mixed2, H2 // 4 * b + 2 * n + 2)
                    dve.tensor_copy(OT[:, 512 * n:512 * (n + 1)], ps[:, 4 + n % 2, :]).then_inc(o_copied[2], 1)

                def one(i, first, left):
                    for h in range(H2):
                        least(i, h, first)
                        if h % 2 and (h > 2 or not first):
                            take(i, h - 3, first)
                        if h == 3:
                            k_heads(i, 3)
                        if h == 5 and not first:
                            outputs(i - 1, 3)
                        if h == 7 and left:
                            x_lo(2, i + 1)
                        if h in (13, 21, 29):
                            outputs(i, (h - 13) // 8)
                        if not first:
                            if h in (9, 11, 14, 15):
                                context(2, i - 1, (9, 11, 14, 15).index(h), D2)
                            if h == 18:
                                context_lo(2, i - 1)
                            if h == 22:
                                dve.wait_ge(y_ready[2], i)
                                add(2, i - 1, 2, xr_a, (B_Y[2],))
                            if h == 24:
                                norm(2, i - 1, 2, xr_a, xo_a)
                        if left:
                            if h in (19, 23):
                                lo_parts_2(i + 1, (h - 19) // 4)
                            if h in (28, 30, 31):
                                k_heads(i + 1, (h - 27) // 2 if h < 31 else 2)

                passes(dve, n, one)
                take(n - 1, H2 - 2, False)
                outputs(n - 1, 3)
                for c in range(4):
                    context(2, n - 1, c, D2, True)

            def feed_forward(f, tiles):
                def x_lo(b, k):
                    dve.wait_ge(xt_hi[f], KT * b + k + 1)
                    dve.tensor_tensor(XT_f[f][1][:, k, :], ps[:, 6 + k, :], XT_f[f][0][:, k, :].bitcast(F32), ALU.subtract
                                      ).then_inc(xt_ready[f], 1)

                def one(i, first, left):
                    before = iterations[f - 1] - 1
                    if f == 3:
                        if first:
                            context_lo(2, before, True)
                        route(i)

                    def product(j):
                        dve.wait_ge(silu_ready[f], tiles * i + j + 1)
                        dve.wait_ge(up_ready[f], tiles * i + j + 1)
                        up, s, h = ps[:, 3 + 2 * (j % 2), :], sg[:, j % 2, :], hf[:, j % 3, :]
                        if f == 1:
                            dve.tensor_tensor(h, up, s, ALU.mult).then_inc(prod_ready[f], 1)
                        else:
                            dve.tensor_tensor(tt[:, j % 3, :], up, s, ALU.mult).then_inc(prod_u, 1)
                            dve.wait_ge(prod_u, tiles * i + j + 1)
                            dve.wait_ge(wcol_ready, tiles * i + j + 1)
                            dve.tensor_tensor(h, ps[:, 7 - j % 2, :], tt[:, j % 3, :], ALU.mult).then_inc(prod_ready[f], 1)

                    def hidden_lo(j):
                        dve.wait_ge(hid_hi[f], tiles * i + j + 1)
                        dve.tensor_tensor(HT[f][:, j % 3, 1, :], hf[:, j % 3, :], HT[f][:, j % 3, 0, :].bitcast(F32),
                                          ALU.subtract).then_inc(hid_ready[f], 1)

                    product(0)
                    if not first:
                        norm(f, i - 1, 4, xr_f, xo_f)
                    if first and f == 1:
                        context_lo(0, before, True)
                    for j in range(1, tiles):
                        product(j)
                        hidden_lo(j - 1)
                        if first and j == 1:
                            dve.wait_ge(y_ready[f - 1], before + 1)
                            add(f - 1, before, 2, xr_a, (LAST_Y,))
                        if first and j == 2:
                            norm(f - 1, before, 2, xr_a, xo_a)
                        if f == 1 and not left:
                            if j == 3:
                                x_lo_attention(2, 0)
                            if j in (4, 5):
                                lo_parts_2(0, j - 4)
                            if j == 7:
                                k_heads(0, 0)
                    hidden_lo(tiles - 1)
                    if f == 1 and not left:
                        k_heads(0, 1)
                        k_heads(0, 2)
                    if left:
                        x_lo(i + 1, 0)
                        x_lo(i + 1, 1)
                    dve.wait_ge(down_done[f], tiles * i + tiles)
                    add(f, i, 4, xr_f, (0, 1))

                x_lo(0, 0)
                x_lo(0, 1)
                if f == 3:
                    dve.wait_ge(rsel_hi, 1)
                    dve.tensor_tensor(routl[:], router_raw, routh[:].bitcast(F32), ALU.subtract).then_inc(rsel_ready, 1)
                passes(dve, iterations[f], one)
                norm(f, iterations[f] - 1, 4, xr_f, xo_f)

            def route(i):
                dve.wait_ge(lg_turned, i + 1)
                raw = ps[:, 7, 0:4 * GATES].rearrange("p (t g) -> p t g", t=4)
                step(route_step, ROUTE_STEPS * i + 1, dve.tensor_reduce(den, raw[:, :, 0:NEXP], AX_X, ALU.max))
                dve.tensor_tensor(lg[:, :, 0:NEXP], raw[:, :, 0:NEXP], den.unsqueeze(2).to_broadcast([P, 4, NEXP]), ALU.subtract)
                dve.tensor_scalar(lg[:, :, NEXP:GATES], raw[:, :, NEXP:GATES], -1.0, None, ALU.mult).then_inc(lg_ready, 1)
                dve.wait_ge(ex_ready, i + 1)
                apart(dve)
                for t in range(4):
                    m = dve.max(top[:, t, :], ex[:, t, 0:NEXP])
                step(route_step, ROUTE_STEPS * i + 2, m)
                step(route_step, ROUTE_STEPS * i + 3, dve.memset(top[:, :, 2:8], -5.0), alone=True)
                for t in range(4):
                    m = dve.match_replace(pick[:, t, :], top[:, t, :], ex[:, t, 0:NEXP], -1.0)
                step(route_step, ROUTE_STEPS * i + 4, m)
                step(route_step, ROUTE_STEPS * i + 5, dve.tensor_reduce(den, top[:, :, 0:2], AX_X, ALU.add))
                step(route_step, ROUTE_STEPS * i + 6, dve.tensor_scalar(pick, pick, 0.0, None, ALU.is_lt))
                dve.tensor_scalar(cw[:, :, NEXP:GATES], ex[:, :, NEXP:GATES], 1.0, None, ALU.add)
                dve.tensor_tensor(cw[:, :, 0:NEXP], pick, ex[:, :, 0:NEXP], ALU.mult)
                step(route_step, ROUTE_STEPS * i + 7, dve.reciprocal(den, den))
                step(route_step, ROUTE_STEPS * i + 8, dve.reciprocal(cw[:, :, NEXP:GATES], cw[:, :, NEXP:GATES]))
                step(route_step, ROUTE_STEPS * i + 9, dve.tensor_tensor(cw[:, :, 0:NEXP], cw[:, :, 0:NEXP],
                                                den.unsqueeze(2).to_broadcast([P, 4, NEXP]), ALU.mult))
                step(route_step, ROUTE_STEPS * i + 10, dve.tensor_copy(cs2[:, :, 0:GATES].bitcast(F32R), cw))
                dve.tensor_tensor(cs2[:, :, GATES:2 * GATES], cw, cs2[:, :, 0:GATES], ALU.subtract).then_inc(cw_ready, 1)

            phase0()
            feed_forward(1, TILES1)
            phase2()
            feed_forward(3, TILES3)

        @blk.gpsimd
        def _(pool):
            pool.memset(ident[:], 0.0).then_inc(ident_ready, 1)
            pool.memset(minus_half, -0.5).then_inc(half_ready, 1)
            pool.memset(eps_col, EPS).then_inc(half_ready, 1)
            pool.wait_ge(ident_ready, 1)
            pool.affine_select(out=ident[:], in_=ident[:], compare_op=ALU.not_equal, fill=1.0, base=0,
                               pattern=[[-1, P]], channel_multiplier=1).then_inc(ident_ready, 1)

            def ones():
                pool.memset(VP, 1.0).then_inc(vp_ones, 1)

            def split_hi_part(part, hi, raw):
                pool.tensor_copy(hi, raw).then_inc(split_w_hi, 1)

            def split_lo_part(part, lo, hi, raw):
                pool.wait_ge(split_w_hi, part + 1)
                pool.tensor_tensor(lo, raw, hi.bitcast(F32), ALU.subtract).then_inc(split_w, 1)

            def free_raw(parts):
                pool.wait_ge(split_w, parts)
                pool.sem_inc(raw_free, 1)

            def split(load, part, hi, lo, raw):
                pool.wait_ge(raw_ready, 16 * load + 16)
                split_hi_part(part, hi, raw)
                split_lo_part(part, lo, hi, raw)
                free_raw(part + 1)

            def unit(load, part, tile):
                wu = WU[:, bass.ts(tile, 1), :, :]
                split(load, part, wu[:, :, 0, :], wu[:, :, 1, :], wraw[:].unsqueeze(1))

            def layernorm_rstd(f, i, nt):
                pool.wait_ge(var_ready[f], i + 1)
                apart(pool)
                pool.tensor_scalar(rstd[:, 0:nt], mv[:, 0:nt, 1:2].rearrange("p t o -> p (t o)"), EPS, None, ALU.add
                                   ).then_inc(eps_added[f], 1)
                pool.wait_ge(eps_added[f], i + 1)
                pool.tensor_tensor(rstd[:, 0:nt], rstd[:, 0:nt], minus_half[:, 0:nt], ALU.pow).then_inc(rstd_ready[f], 1)

            pool.memset(flip, 0.0).then_inc(flip_zero, 1)
            pool.wait_ge(flip_zero, 1)
            pool.affine_select(out=flip, in_=flip, compare_op=ALU.not_equal, fill=1.0, base=1 - P,
                               pattern=[[1, P]], channel_multiplier=1).then_inc(flip_ready, 1)
            pool.wait_ge(half_ready, 2)
            ones()
            cols = UNIT // PIECES

            def one(i, first, left):
                wu = WU[:, bass.ts(i, 1), :, :]
                for p in range(H0 // 2):
                    pool.wait_ge(squared, H0 // 2 * i + p + 1)
                    apart(pool)
                    for block in (0, 2):
                        u = U(p)[:, :, P * block:P * (block + 1)]
                        m = pool.affine_select(out=u, in_=u, compare_op=ALU.is_ge, fill=0.0, base=0,
                                               pattern=[[0, 2], [1, P]], channel_multiplier=-1)
                    m.then_inc(masked, 1)
                    if p == 6 and not first:
                        layernorm_rstd(0, i - 1, 2)
                    piece = slice(cols * (p // 2), cols * (p // 2 + 1))
                    raw, hi, lo = wraw[:, piece].unsqueeze(1), wu[:, :, 0, piece], wu[:, :, 1, piece]
                    if p == 0:
                        pool.wait_ge(raw_ready, 16 * i + 16)
                    if p % 2 == 0:
                        split_hi_part(PIECES * i + p // 2, hi, raw)
                    else:
                        split_lo_part(PIECES * i + p // 2, lo, hi, raw)
                free_raw(PIECES * (i + 1))

            passes(pool, iterations[0], one)
            layernorm_rstd(0, iterations[0] - 1, 2)
            pool.wait_ge(y_ready[0], iterations[0])
            aw = AW[:].rearrange("p a b c -> p a (b c)")
            with pool.Fori(0, iterations[1]) as i:
                part = bass.ts(i, 512)
                split(LOADS[1] + i, PARTS[1] + i, aw[:, 0, part], aw[:, 1, part], wraw[:, 0:512])
                layernorm_rstd(1, i, 4)
            pool.wait_ge(hid_ready[1], TILES1 * iterations[1])
            pool.wait_ge(down_done[1], TILES1 * iterations[1])
            ones()
            with pool.Fori(0, iterations[2]) as i:
                for k in range(2):
                    unit(LOADS[2] + 2 * i + k, PARTS[2] + 2 * i + k, 2 * i + k)
                layernorm_rstd(2, i, 2)
            pool.wait_ge(y_ready[2], iterations[2])
            unit(LOADS[2] + TILES3 - 1, PARTS[2] + TILES3 - 1, TILES3 - 1)
            with pool.Fori(0, iterations[3]) as i:
                layernorm_rstd(3, i, 4)


def kernel(**inputs):
    import numpy as np
    import concourse.bacc as bacc
    from concourse.bass_utils import run_bass_kernel_spmd

    a = {k: np.asarray(v) for k, v in inputs.items()}

    def by_partition(w):
        return np.ascontiguousarray(w.reshape(KT, P, -1).transpose(1, 0, 2))

    def units(gate, up, down, tiles):
        out = np.zeros((tiles, P, UNIT), np.float32)
        for m, w in enumerate((gate, up)):
            full = np.zeros((E, tiles * P), np.float32)
            full[:, :w.shape[1]] = w
            out[:, :, m * KT * P:(m + 1) * KT * P] = (
                full.reshape(KT, P, tiles, P).transpose(2, 1, 0, 3).reshape(tiles, P, KT * P))
        rows = np.zeros((tiles * P, E), np.float32)
        rows[:down.shape[0]] = down
        out[:, :, 2 * KT * P:] = rows.reshape(tiles, P, E)
        return out

    inv = (1.0 / np.float32(10000.0) ** (np.arange(0, D0, 2, dtype=np.float32) / np.float32(D0))).astype(np.float32)
    angle = np.arange(S, dtype=np.float32)[:, None] * inv[None, :]
    rope = np.concatenate([np.cos(angle), np.sin(angle)], axis=1).astype(np.float32)
    sel = np.zeros((2 * GATES, TILES3 * P), np.float32)
    for row in range(NEXP * IE + SI):
        g = min(row // IE, NEXP)
        sel[[g, g + GATES], row] = 1.0

    arrays = {
        "x": a["L0_attn_x"].reshape(T, E),
        "rope": np.ascontiguousarray(rope.reshape(2, P, 16).transpose(1, 0, 2)),
        "ln": np.ascontiguousarray(np.broadcast_to(np.stack([a["L0_attn_ln_scale"], a["L0_attn_ln_bias"]]), (P, 2, D0))),
        "aw0": by_partition(np.concatenate([a["L0_attn_w_qkv"], a["L0_attn_w_out"]], axis=1)),
        "wu1": units(a["L0_ffn_w_gate"].T, a["L0_ffn_w_up"].T, a["L0_ffn_w_down"].T, TILES1),
        "aw2": by_partition(np.concatenate([a["L1_attn_wq"].T, a["L1_attn_wk"].T, a["L1_attn_wv"].T,
                                            a["L1_attn_wo"].T], axis=1)).reshape(P, KT * 1024),
        "rel": a["L1_attn_rel_pos"],
        "wu3": units(np.concatenate([a["L1_ffn_w_gate"].transpose(1, 0, 2).reshape(E, -1), a["L1_ffn_sw_gate"]], axis=1),
                     np.concatenate([a["L1_ffn_w_up"].transpose(1, 0, 2).reshape(E, -1), a["L1_ffn_sw_up"]], axis=1),
                     np.concatenate([a["L1_ffn_w_down"].reshape(-1, E), a["L1_ffn_sw_down"]], axis=0), TILES3),
        "router": by_partition(np.concatenate([a["L1_ffn_router_w"].T, a["L1_ffn_shared_gate_w"][:, None]], axis=1)),
        "sel": sel,
    }
    nc = bacc.Bacc("TRN2", target_bir_lowering=False, num_devices=1)
    in_map, args = {}, []
    for name, v in arrays.items():
        v = np.ascontiguousarray(v)
        in_map[f"in_{name}"] = v
        args.append(nc.dram_tensor(f"in_{name}", v.shape, mybir.dt.from_np(v.dtype), kind="ExternalInput").ap())
    out = nc.dram_tensor("out_x", (T, E), F32, kind="ExternalOutput").ap()
    program(nc, *args, out)
    r = run_bass_kernel_spmd(nc, [in_map], core_ids=[0])
    return r.results[0]["out_x"].reshape(a["L0_attn_x"].shape)
```
